# Optimizing a Trainium2 kernel written in Bass

```python
import numpy as np
import jax
import jax.numpy as jnp

def _softmax(x, axis=-1):
    return jax.nn.softmax(x, axis=axis)

def _gelu(x):
    return jax.nn.gelu(x, approximate=True)

def _silu(x):
    return jax.nn.silu(x)

def _sigmoid(x):
    return jax.nn.sigmoid(x)

def _layernorm(x, axis=-1, eps=1e-05):
    m = jnp.mean(x, axis=axis, keepdims=True)
    v = jnp.var(x, axis=axis, keepdims=True)
    return (x - m) / jnp.sqrt(v + eps)

def _scatter_add(tgt, idx, src, axis=0):
    return tgt.at[idx].add(src)

def _segment_sum(src, seg, n):
    return jax.ops.segment_sum(src, seg, n)
kernel_name = 'mk_xattn_ffn_d1_seqx_r8_934b3d'

def setup_inputs(seed: int=0):
    np.random.seed(seed)
    _w = jnp.asarray

    def _rec_inputs():
        import jax
        import jax.numpy as jnp
        _rk = jax.random.key(seed)
        x = -0.0002928 + 1 * jax.random.normal(jax.random.fold_in(_rk, 1), (64, 64, 128), jnp.float32)
        _lenS = 64 - jax.random.randint(jax.random.fold_in(_rk, 7), (64,), 0, max(1, 64 // 4) + 1, jnp.int32)
        _lenS2 = 64 - jax.random.randint(jax.random.fold_in(_rk, 8), (64,), 0, max(1, 64 // 4) + 1, jnp.int32)
        _ctx_1024P = jax.random.normal(jax.random.fold_in(_rk, 11), (64, 16, 128), jnp.float32)
        _ctx_1024c = jax.random.dirichlet(jax.random.fold_in(_rk, 511), 0.3 * jnp.ones((16,), jnp.float32), (64, 64))
        _ctx_1024t = jnp.einsum('bsk,bkd->bsd', _ctx_1024c, _ctx_1024P)
        _ctx_1024t = _ctx_1024t * jax.lax.rsqrt(jnp.mean(jnp.square(_ctx_1024t)) + 1e-12) * 0.953939
        ctx_1024 = -1.39393e-06 + 0.999914 * (_ctx_1024t + 0.3 * jax.random.normal(jax.random.fold_in(_rk, 611), (64, 64, 128), jnp.float32))
        return (x, ctx_1024)
    x, ctx_1024 = _rec_inputs()

    def _L0_xattn_setup():
        import jax, jax.numpy as jnp
        import numpy as np
        import math
        D_MODEL = 128
        N_HEADS = 16
        HEAD_DIM = D_MODEL // N_HEADS
        WINDOW = 64
        B, S = (2, 256)

        def _window_mask(seq_len: int, w: int) -> jnp.ndarray:
            idx = jnp.arange(seq_len)
            return jnp.abs(idx[:, None] - idx[None, :]) <= w
        key = jax.random.key(seed)
        ks = jax.random.split(key, 11)
        s = 1.0 / math.sqrt(D_MODEL)
        return {'query': jax.random.normal(ks[0], (B, S, D_MODEL), jnp.float32), 'key': jax.random.normal(ks[1], (B, S, D_MODEL), jnp.float32), 'value': jax.random.normal(ks[2], (B, S, D_MODEL), jnp.float32), 'Wq': jax.random.normal(ks[3], (D_MODEL, D_MODEL), jnp.float32) * s, 'bq': jnp.zeros((D_MODEL,), jnp.float32), 'Wk': jax.random.normal(ks[4], (D_MODEL, D_MODEL), jnp.float32) * s, 'bk': jnp.zeros((D_MODEL,), jnp.float32), 'Wv': jax.random.normal(ks[5], (D_MODEL, D_MODEL), jnp.float32) * s, 'bv': jnp.zeros((D_MODEL,), jnp.float32), 'Wo': jax.random.normal(ks[6], (D_MODEL, D_MODEL), jnp.float32) * s, 'bo': jnp.zeros((D_MODEL,), jnp.float32)}
    _L0_xattn_all = _L0_xattn_setup()
    _L0_xattn_in = {k: v for k, v in _L0_xattn_all.items() if k in ('Wq', 'bq', 'Wk', 'bk', 'Wv', 'bv', 'Wo', 'bo')}
    del _L0_xattn_all

    def _L0_ffn_setup():
        import jax, jax.numpy as jnp
        import numpy as np
        D_MODEL = 128
        EXPERT_DIM = 256
        N_EXPERTS = 8
        LN_EPS = 1e-05

        def _bit_quant(W):
            scale = jnp.clip(jnp.mean(jnp.abs(W), axis=-1, keepdims=True), 1e-05, None)
            w_q = jnp.clip(jnp.round(W / scale), -1.0, 1.0) * scale
            return W + jax.lax.stop_gradient(w_q - W)
        key = jax.random.key(seed)
        ks = jax.random.split(key, 7)
        x = jax.random.normal(ks[0], (4, 256, D_MODEL), dtype=jnp.float32)
        shared_w1 = jax.random.normal(ks[1], (EXPERT_DIM, D_MODEL), dtype=jnp.float32) / np.sqrt(EXPERT_DIM)
        shared_w2 = jax.random.normal(ks[2], (D_MODEL, EXPERT_DIM), dtype=jnp.float32) / np.sqrt(D_MODEL)
        expert_w1 = jax.random.normal(ks[3], (N_EXPERTS, EXPERT_DIM, D_MODEL), dtype=jnp.float32) / np.sqrt(EXPERT_DIM)
        expert_w2 = jax.random.normal(ks[4], (N_EXPERTS, D_MODEL, EXPERT_DIM), dtype=jnp.float32) / np.sqrt(D_MODEL)
        router_w = 0.02 * jax.random.normal(ks[5], (N_EXPERTS, D_MODEL), dtype=jnp.float32)
        ln_gamma = jnp.ones((D_MODEL,), dtype=jnp.float32)
        ln_beta = jnp.zeros((D_MODEL,), dtype=jnp.float32)
        return {'x': x, 'shared_w1': shared_w1, 'shared_w2': shared_w2, 'expert_w1': expert_w1, 'expert_w2': expert_w2, 'router_w': router_w, 'ln_gamma': ln_gamma, 'ln_beta': ln_beta}
    _L0_ffn_all = _L0_ffn_setup()
    _L0_ffn_in = {k: v for k, v in _L0_ffn_all.items() if k in ('shared_w1', 'shared_w2', 'expert_w1', 'expert_w2', 'router_w', 'ln_gamma', 'ln_beta')}
    del _L0_ffn_all
    return {'x': x, 'ctx_1024': ctx_1024, 'L0_xattn_Wq': _L0_xattn_in['Wq'], 'L0_xattn_bq': _L0_xattn_in['bq'], 'L0_xattn_Wk': _L0_xattn_in['Wk'], 'L0_xattn_bk': _L0_xattn_in['bk'], 'L0_xattn_Wv': _L0_xattn_in['Wv'], 'L0_xattn_bv': _L0_xattn_in['bv'], 'L0_xattn_Wo': _L0_xattn_in['Wo'], 'L0_xattn_bo': _L0_xattn_in['bo'], 'L0_ffn_shared_w1': _L0_ffn_in['shared_w1'], 'L0_ffn_shared_w2': _L0_ffn_in['shared_w2'], 'L0_ffn_expert_w1': _L0_ffn_in['expert_w1'], 'L0_ffn_expert_w2': _L0_ffn_in['expert_w2'], 'L0_ffn_router_w': _L0_ffn_in['router_w'], 'L0_ffn_ln_gamma': _L0_ffn_in['ln_gamma'], 'L0_ffn_ln_beta': _L0_ffn_in['ln_beta']}

def reference(x, ctx_1024, L0_xattn_Wq, L0_xattn_bq, L0_xattn_Wk, L0_xattn_bk, L0_xattn_Wv, L0_xattn_bv, L0_xattn_Wo, L0_xattn_bo, L0_ffn_shared_w1, L0_ffn_shared_w2, L0_ffn_expert_w1, L0_ffn_expert_w2, L0_ffn_router_w, L0_ffn_ln_gamma, L0_ffn_ln_beta):
    import jax
    import jax.numpy as jnp

    def _L0_xattn_ref(query, key, value, Wq, bq, Wk, bk, Wv, bv, Wo, bo):
        import jax, jax.numpy as jnp
        import numpy as np
        import math
        D_MODEL = 128
        N_HEADS = 16
        HEAD_DIM = D_MODEL // N_HEADS
        WINDOW = 64
        B, S = (2, 256)

        def _window_mask(seq_len: int, w: int) -> jnp.ndarray:
            idx = jnp.arange(seq_len)
            return jnp.abs(idx[:, None] - idx[None, :]) <= w
        b, s, _ = query.shape
        Q = (query @ Wq.T + bq).reshape(b, s, N_HEADS, HEAD_DIM).transpose(0, 2, 1, 3)
        K = (key @ Wk.T + bk).reshape(b, s, N_HEADS, HEAD_DIM).transpose(0, 2, 1, 3)
        V = (value @ Wv.T + bv).reshape(b, s, N_HEADS, HEAD_DIM).transpose(0, 2, 1, 3)
        scale = 1.0 / math.sqrt(HEAD_DIM)
        scores = jnp.einsum('bhqd,bhkd->bhqk', Q, K) * scale
        mask = _window_mask(s, WINDOW)
        scores = jnp.where(mask[None, None], scores, jnp.float32(-jnp.inf))
        attn = jax.nn.softmax(scores, axis=-1)
        out = jnp.einsum('bhqk,bhkd->bhqd', attn, V)
        out = out.transpose(0, 2, 1, 3).reshape(b, s, D_MODEL)
        return out @ Wo.T + bo

    def _L0_ffn_ref(x, shared_w1, shared_w2, expert_w1, expert_w2, router_w, ln_gamma, ln_beta):
        import jax, jax.numpy as jnp
        import numpy as np
        D_MODEL = 128
        EXPERT_DIM = 256
        N_EXPERTS = 8
        LN_EPS = 1e-05

        def _bit_quant(W):
            scale = jnp.clip(jnp.mean(jnp.abs(W), axis=-1, keepdims=True), 1e-05, None)
            w_q = jnp.clip(jnp.round(W / scale), -1.0, 1.0) * scale
            return W + jax.lax.stop_gradient(w_q - W)
        mu = jnp.mean(x, axis=-1, keepdims=True)
        var = jnp.mean(jnp.square(x - mu), axis=-1, keepdims=True)
        h = (x - mu) / jnp.sqrt(var + LN_EPS) * ln_gamma + ln_beta
        sw1, sw2 = (_bit_quant(shared_w1), _bit_quant(shared_w2))
        shared_out = jax.nn.silu(jnp.einsum('btd,fd->btf', h, sw1)) @ sw2.T
        probs = jax.nn.softmax(h @ router_w.T, axis=-1)
        top_prob = jnp.max(probs, axis=-1)
        top_idx = jnp.argmax(probs, axis=-1)
        ew1, ew2 = (_bit_quant(expert_w1), _bit_quant(expert_w2))
        h1 = jax.nn.silu(jnp.einsum('btd,efd->ebtf', h, ew1))
        eo = jnp.einsum('ebtf,edf->ebtd', h1, ew2)
        gate = jax.nn.one_hot(top_idx, N_EXPERTS, dtype=h.dtype) * top_prob[..., None]
        routed_out = jnp.einsum('ebtd,bte->btd', eo, gate)
        return shared_out + routed_out
    x = x + _L0_xattn_ref(_layernorm(x, axis=-1), ctx_1024, ctx_1024, L0_xattn_Wq, L0_xattn_bq, L0_xattn_Wk, L0_xattn_bk, L0_xattn_Wv, L0_xattn_bv, L0_xattn_Wo, L0_xattn_bo)
    x = x + _L0_ffn_ref(_layernorm(x, axis=-1), L0_ffn_shared_w1, L0_ffn_shared_w2, L0_ffn_expert_w1, L0_ffn_expert_w2, L0_ffn_router_w, L0_ffn_ln_gamma, L0_ffn_ln_beta)
    return x

_drawn_inputs = setup_inputs


def setup_inputs(seed=0):
    import zlib

    import numpy as np

    out = dict(_drawn_inputs(seed))
    spreads = {'L0_xattn_bq': (0.0, 0.341),
     'L0_xattn_bk': (0.0, 0.8),
     'L0_xattn_bv': (0.0, 0.1),
     'L0_xattn_bo': (0.0, 0.1),
     'L0_ffn_ln_gamma': (1.0, 0.2),
     'L0_ffn_ln_beta': (0.0, 0.336)}
    factors = {}
    for name, (base, spread) in spreads.items():
        noise = np.random.default_rng([zlib.crc32(name.encode()), seed]).standard_normal(out[name].shape)
        drawn = base * np.exp(spread * noise) if base else spread * noise
        out[name] = jnp.asarray(drawn.astype(out[name].dtype))
    for name, factor in factors.items():
        out[name] = (out[name] * factor).astype(out[name].dtype)
    return out
```

```python
from contextlib import ExitStack

import concourse.bass as bass
from concourse import mybir

ALU = mybir.AluOpType
ACT = mybir.ActivationFunctionType
X = mybir.AxisListType.X
F32 = mybir.dt.float32
F16 = mybir.dt.float16
BF16 = mybir.dt.bfloat16
I32 = mybir.dt.int32

P = 128
D = 128
S = 64
HEADS, HD = 16, 8
QUADS = HEADS // 4
TILE = 128
CH = 256
NB = CH // S
EXPERTS = 8
FE = 256
BLOCKS = EXPERTS + 1
LN_EPS = 1e-5
VW = HD + 1
LNE = 4.1588830833596715
ROW = 2 * D + 4
GATE, TOKEN = 2 * D, 2 * D + 1


def block_program(nc, x, ctx_in, Wq, bq, Wk, bk, Wv, bv, Wo, bo, sw1, sw2, ew1, ew2, rw, gamma, beta, out):
    TOKENS = x.shape[0]
    NCH = TOKENS // CH
    NT = TOKENS // TILE
    SLOTS = -(-((TOKENS + EXPERTS * (TILE - 1)) // TILE) // 2) * 2
    STEPS = SLOTS // 2
    NOWHERE = float(2 * TOKENS)
    SCALE = float(HD) ** -0.5
    W_LOADS = 21

    qk_dram = nc.dram_tensor("qk_terms", (NCH, 2, 4, 4, 32, CH), F16).ap()
    by_expert = nc.dram_tensor("rows_by_expert", (EXPERTS * TOKENS, ROW), F32).ap()

    with ExitStack() as stack:
        def sb(name, shape, dt=F32):
            return stack.enter_context(nc.sbuf_tensor(name, shape, dt))

        def sem(name):
            return stack.enter_context(nc.semaphore(name))

        ident = sb("ident", [P, P])
        identb = sb("identb", [P, P], BF16)
        identh = sb("identh", [P, P], F16)
        w_in = sb("w_in", [P, 4, P])
        wT = sb("wT", [P, 3, P])
        woT = sb("woT", [64, 2, P])
        b_col = sb("b_col", [P, 2])
        bv_col = sb("bv_col", [64, 2])
        bo_row = sb("bo_row", [P, D])
        b_row = sb("b_row", [P, D])
        ln_col = sb("ln_col", [P, 2])
        rw_in = sb("rw_in", [EXPERTS, D])
        rwT = sb("rwT", [D, EXPERTS])
        w1_in = sb("w1_in", [P, BLOCKS, 2, D])
        w2_in = sb("w2_in", [P, BLOCKS, FE])
        sign1 = sb("sign1", [P, BLOCKS, 2, D], F16)
        sign2 = sb("sign2", [P, BLOCKS, FE], F16)
        low1 = sb("low1", [P, 2, D], F16)
        low2 = sb("low2", [P, FE], F16)
        s1 = sb("s1", [P, BLOCKS * 2])
        s1h = sb("s1h", [P, BLOCKS * 2])
        s1n = sb("s1n", [P, BLOCKS * 2])
        s2 = sb("s2", [P, BLOCKS])
        s2h = sb("s2h", [P, BLOCKS])
        s2n = sb("s2n", [P, BLOCKS])
        s2_row = sb("s2_row", [P, BLOCKS, D])
        t1 = sb("t1", [P, BLOCKS, 2, P], F16)
        t2 = sb("t2", [P, BLOCKS, 2, D], F16)
        zeros = sb("zeros", [P, ROW])
        lne = sb("lne", [P, 1])

        x_in = sb("x_in", [P, 2, 2, D])
        c_in = sb("c_in", [P, 2, 2, D])
        x_res = sb("x_res", [P, 2, 2, D])
        stats = sb("stats", [P, 2, 6])
        mv = sb("mv", [P, 2, 2, 2])
        veps = sb("veps", [P, 2, 2])
        rstd = sb("rstd", [P, 2, 2])
        minus_half = sb("minus_half", [P, 2])
        xn = sb("xn", [P, 2, 2, D])
        xcT = sb("xcT", [P, 2, 4, TILE])
        qk_hl = sb("qk_hl", [P, 2, 2, CH], F16)
        q_t = sb("q_t", [P, 2, QUADS, CH], F16)
        k_t = sb("k_t", [P, 2, QUADS, NB, 4, S], F16)
        v_hi = sb("v_hi", [P, 2, NB, 2 * QUADS, 2, VW], F16)
        v_lo = sb("v_lo", [P, 2, NB, 2 * QUADS, 2, VW], F16)
        negmax = sb("negmax", [P, 2, P], BF16)
        negmaxT = sb("negmaxT", [P, 2, P], BF16)
        sel = sb("sel", [P, HEADS // 2, 2, S], BF16)
        e32 = sb("e32", [P, 2, 2, 4, S])
        e_hi = sb("e_hi", [P, 2, 2, 2, 4, S], F16)
        e_lo = sb("e_lo", [P, 2, 2, 2, 4, S], F16)
        rden = sb("rden", [P, 2, 8])
        attn = sb("attn", [P, 2, NB, 2 * QUADS, HD])
        attnT = sb("attnT", [64, 2, NB, S])
        stats2 = sb("stats2", [P, 2, 6])
        mv2 = sb("mv2", [P, 2, 2])
        w2var = sb("w2var", [P, 2])
        rstd2 = sb("rstd2", [P, 2])
        rows = sb("rows", [P, 2, 2, ROW])
        hT32 = sb("hT32", [P, CH])
        top = sb("top", [P, 2])
        shifted = sb("shifted", [P, 2, EXPERTS])
        is_top = sb("is_top", [P, 2, EXPERTS])
        first = sb("first", [P, 2])
        onehot = sb("onehot", [P, 2, EXPERTS])
        onehot_b = sb("onehot_b", [P, 2, EXPERTS], BF16)
        expo = sb("expo", [P, 2, EXPERTS])
        expsum = sb("expsum", [P, 2])
        seen = sb("seen", [P, EXPERTS], BF16)
        seen2 = sb("seen2", [P, EXPERTS], BF16)
        pos8 = sb("pos8", [P, 2, EXPERTS])
        pos8m = sb("pos8m", [P, 2, EXPERTS])
        dest = sb("dest", [P, 2, 2], I32)
        token_no = sb("token_no", [P, 2])
        before = sb("before", [P, P], BF16)
        ones_b = sb("ones_b", [P, P], BF16)
        rank8 = sb("rank8", [P, EXPERTS])
        region8 = sb("region8", [P, EXPERTS])
        iota8 = sb("iota8", [P, EXPERTS])
        thr = sb("thr", [P, EXPERTS, NT])
        tri8 = sb("tri8", [P, EXPERTS, EXPERTS])
        slot_no = sb("slot_no", [P, SLOTS])
        part_no = sb("part_no", [P, 1])
        cnt = sb("cnt", [P, EXPERTS])
        over = sb("over", [P, EXPERTS, NT])
        tiles8 = sb("tiles8", [P, EXPERTS])
        prod8 = sb("prod8", [P, EXPERTS, EXPERTS])
        upto8 = sb("upto8", [P, EXPERTS])
        start8 = sb("start8", [P, EXPERTS])
        sl_ge = sb("sl_ge", [P, SLOTS, EXPERTS])
        sl_e = sb("sl_e", [P, SLOTS])
        sl_oh = sb("sl_oh", [P, SLOTS, EXPERTS])
        sl_m = sb("sl_m", [P, SLOTS, EXPERTS])
        sl_m2 = sb("sl_m2", [P, SLOTS, EXPERTS])
        sl_start = sb("sl_start", [P, SLOTS])
        sl_n = sb("sl_n", [P, SLOTS])
        sl_j = sb("sl_j", [P, SLOTS])
        sl_last = sb("sl_last", [P, SLOTS])
        sl_off = sb("sl_off", [P, SLOTS])
        sl_row = sb("sl_row", [P, SLOTS])
        sl_v1 = sb("sl_v1", [P, SLOTS])
        sl_v2 = sb("sl_v2", [P, SLOTS])
        valid = sb("valid", [P, SLOTS])
        sl_ec = sb("sl_ec", [P, SLOTS])
        sl_base = sb("sl_base", [P, SLOTS])
        tab = sb("tab", [1, 2, SLOTS], I32)
        n_rows = sb("n_rows", [P, 2, 2, D])
        x_rows = sb("x_rows", [P, 2, 2, ROW - D])
        hf = sb("hf", [P, CH])
        h_hi = sb("h_hi", [P, 2, CH], F16)
        h_lo = sb("h_lo", [P, 2, CH], F16)
        g32 = sb("g32", [P, 2, 2, CH])
        g_hi = sb("g_hi", [P, 2, 2, 2, CH], F16)
        g_lo = sb("g_lo", [P, 2, 2, 2, CH], F16)
        sh_out = sb("sh_out", [P, 2, D])
        ex_out = sb("ex_out", [P, 2, D])
        o_sum = sb("o_sum", [P, 2, D])
        o_rows = sb("o_rows", [P, 2, 2, D])
        o_idx_f = sb("o_idx_f", [P, 2])
        o_idx = sb("o_idx", [P, 2, 2], I32)

        banks = [stack.enter_context(nc.psum_tensor(f"bank{i}", [P, 512], F32)) for i in range(8)]
        A = banks[0:2]
        ST = banks[2:4]
        AV = banks[4]
        M0, M1, M2 = banks[5:8]

        w_loaded = sem("w_loaded")
        ffn_w_loaded = sem("ffn_w_loaded")
        xc_loaded = [sem("xc_loaded0"), sem("xc_loaded1")]
        res_loaded = [sem("res_loaded0"), sem("res_loaded1")]
        terms_stored = sem("terms_stored")
        terms_loaded = [sem("terms_loaded0"), sem("terms_loaded1")]
        region_cleared = sem("region_cleared")
        scattered = [sem("scattered0"), sem("scattered1")]
        n_loaded = [sem("n_loaded0"), sem("n_loaded1")]
        x_loaded = [sem("x_loaded0"), sem("x_loaded1")]
        out_stored = [sem("out_stored0"), sem("out_stored1")]
        consts = sem("consts")
        vconsts = sem("vconsts")
        w_turned = sem("w_turned")
        w_kept = sem("w_kept")
        bv_proj = sem("bv_proj")
        bo_ready = sem("bo_ready")
        signs = sem("signs")
        t_turned = sem("t_turned")
        t_kept = sem("t_kept")
        stats_done = sem("stats_done")
        xn_ready = sem("xn_ready")
        xc_turned = sem("xc_turned")
        xcT_ready = sem("xcT_ready")
        q_proj, k_proj, v_proj = sem("q_proj"), sem("k_proj"), sem("v_proj")
        qk_hi_done = sem("qk_hi_done")
        qk_lo_done = sem("qk_lo_done")
        v_hi_done = sem("v_hi_done")
        v_lo_done = sem("v_lo_done")
        a_done = sem("a_done")
        max_done = sem("max_done")
        negmax_turned = sem("negmax_turned")
        negmaxT_ready = sem("negmaxT_ready")
        st_done = sem("st_done")
        e_hi_done = sem("e_hi_done")
        e32_done = sem("e32_done")
        e_lo_done = sem("e_lo_done")
        av_done = sem("av_done")
        rden_done = sem("rden_done")
        attn_done = sem("attn_done")
        attn_turned = sem("attn_turned")
        attnT_ready = sem("attnT_ready")
        y_done = sem("y_done")
        res_ready = sem("res_ready")
        x2_done = sem("x2_done")
        stats2_done = sem("stats2_done")
        rstd2_done = sem("rstd2_done")
        n2_done = sem("n2_done")
        n2_turned = sem("n2_turned")
        hT_ready = sem("hT_ready")
        logits_done = sem("logits_done")
        shifted_done = sem("shifted_done")
        expo_done = sem("expo_done")
        onehot_done = sem("onehot_done")
        pos_done = sem("pos_done")
        dest_done = sem("dest_done")
        row_done = sem("row_done")
        seen_done = sem("seen_done")
        carried = sem("carried")
        chain = sem("chain")
        st_chain = sem("st_chain")
        st2_chain = sem("st2_chain")
        pick_chain = sem("pick_chain")
        gate_chain = sem("gate_chain")
        place_chain = sem("place_chain")
        h_chain = sem("h_chain")
        g_chain = sem("g_chain")
        o_chain = sem("o_chain")
        pchain = sem("pchain")
        counts_done = sem("counts_done")
        tab_done = sem("tab_done")
        h_turned = sem("h_turned")
        h_done = sem("h_done")
        f1_done = sem("f1_done")
        g32_done = sem("g32_done")
        g_done = sem("g_done")
        f2_done = sem("f2_done")
        o_done = sem("o_done")

        EARLY, LATE = (3, NCH - 5), NCH + 2

        def chunks(eng, body):
            for c in range(EARLY[0]):
                body(c, c % 2, c)
            with eng.Fori(EARLY[0], EARLY[1] - 1, 2) as c:
                body(c, 1, EARLY[0])
                body(c + 1, 0, EARLY[0] + 1)
            for c in range(EARLY[1], LATE):
                body(c, c % 2, c)

        def twos(c, r, shift):
            return (c + (shift + 2 - (r + shift) % 2)) * 8

        def carry_waits(eng):
            eng.sem_inc(carried, 1)

        def v_sums(hp):
            return M0[64 * hp:64 * hp + 64, :].rearrange("p (b q pp hp d) -> p hp (b q) pp d", b=NB, q=QUADS, pp=2, hp=2)[:, hp]

        def v_part(t, r, hp, lo=0, hi=HD):
            return t[64 * hp:64 * hp + 64, r].rearrange("p b (q hp) pp d -> p hp (b q) pp d", hp=2)[:, hp, :, :, lo:hi]

        def has(j):
            return 0 <= j < NCH

        block = stack.enter_context(nc.Block())
        x_v = x.rearrange("(c t p) d -> c p t d", p=P, t=2)
        c_v = ctx_in.rearrange("(c t p) d -> c p t d", p=P, t=2)

        @block.sync
        def _(sp):
            def load_xc(c, r):
                sp.dma_start(x_in[:, r], x_v[c]).then_inc(xc_loaded[r], 16)
                sp.dma_start(c_in[:, r], c_v[c]).then_inc(xc_loaded[r], 16)

            load_xc(0, 0)
            for i, w in enumerate((Wq, Wk, Wv)):
                sp.dma_start(w_in[:, i, :], w).then_inc(w_loaded, 16)
            for p in range(2):
                sp.dma_start(w_in[:, 3, 64 * p:64 * p + 64].rearrange("o (q r) -> o q r", q=QUADS),
                             Wo.rearrange("o (q p r) -> o p q r", q=QUADS, p=2)[:, p]).then_inc(w_loaded, 16)
            sp.dma_start(rw_in[:, :], rw).then_inc(w_loaded, 16)
            with nc.allow_non_contiguous_dma(reason="512 bytes of biases"):
                for i, b in enumerate((bq, bk)):
                    for m in range(4):
                        sp.dma_start(b_col[32 * m:32 * m + 32, i:i + 1],
                                     b.rearrange("(q m d) -> m d q", m=4, d=HD)[m].unsqueeze(2)).then_inc(w_loaded, 16)
                for q in range(QUADS):
                    sp.dma_start(bv_col[16 * q:16 * q + 16, :],
                                 bv.rearrange("(q p r) -> q r p", q=QUADS, p=2)[q]).then_inc(w_loaded, 16)
                sp.dma_start(ln_col[:, 0:1], gamma.unsqueeze(1)).then_inc(w_loaded, 16)
                sp.dma_start(ln_col[:, 1:2], beta.unsqueeze(1)).then_inc(w_loaded, 16)
            sp.dma_start(bo_row[:, :], bo.unsqueeze(0).to_broadcast([P, D])).then_inc(w_loaded, 16)
            load_xc(1, 1)
            sp.dma_start(w1_in[:, 0], sw1.rearrange("(c f) d -> f c d", f=P)).then_inc(ffn_w_loaded, 16)
            sp.dma_start(w1_in[:, 1:].rearrange("p e c d -> p (e c) d"),
                         ew1.rearrange("e (c f) d -> f (e c) d", f=P)).then_inc(ffn_w_loaded, 16)
            sp.dma_start(w2_in[:, 0], sw2).then_inc(ffn_w_loaded, 16)
            sp.dma_start(w2_in[:, 1:], ew2.rearrange("e d f -> d e f")).then_inc(ffn_w_loaded, 16)
            sp.wait_ge(vconsts, 1)
            for e in range(EXPERTS):
                sp.dma_start(by_expert[e * TOKENS:e * TOKENS + TILE], zeros[:, :]).then_inc(region_cleared, 16)

            def store_terms(c):
                sp.wait_ge(qk_lo_done, (c + 1) * 2)
                for qk in range(2):
                    for t in range(4):
                        part = t % 2 if qk == 0 else t // 2
                        sp.dma_start(qk_dram[c, qk, :, t], qk_hl[:, qk, part, :]).then_inc(terms_stored, 16)

            def load_terms(c, r, used):
                sp.wait_ge(terms_stored, (c + 1) * 128)
                carry_waits(sp)
                if used:
                    sp.wait_ge(st_done, (c - 1) * 4)
                sp.dma_start(q_t[:, r], qk_dram[c, 0].rearrange("m t (d q) n -> (m t d) q n", q=QUADS)).then_inc(terms_loaded[r], 16)
                for m in range(4):
                    sp.dma_start(k_t[32 * m:32 * m + 32, r, :, :, m, :].rearrange("p q b s -> p (q b) s"),
                                 qk_dram[c, 1, m].rearrange("t (d q) (b s) -> (t d) (q b) s", q=QUADS, s=S)).then_inc(terms_loaded[r], 16)

            def load_res(c, r, used):
                if used:
                    sp.wait_ge(x2_done, c - 1)
                sp.dma_start(x_res[:, r], x_v[c]).then_inc(res_loaded[r], 16)

            sp.wait_ge(xc_turned, 1)
            load_xc(2, 0)
            sp.wait_ge(consts, 1)
            store_terms(0)
            load_terms(0, 0, False)
            sp.wait_ge(xc_turned, 2)
            load_xc(3, 1)
            store_terms(1)

            def body(c, r, k):
                if has(k + 1):
                    load_terms(c + 1, 1 - r, k + 1 >= 2)
                if has(k):
                    load_res(c, r, k >= 2)
                if has(k + 2):
                    if has(k + 4):
                        sp.wait_ge(xc_turned, c + 3)
                        load_xc(c + 4, r)
                    store_terms(c + 2)

            chunks(sp, body)

            sp.wait_ge(tab_done, 1)
            sp.wait_ge(scattered[0], NCH * 16)
            sp.wait_ge(scattered[1], NCH * 16)

            def load_rows(u, i, to, cols, done):
                row = sp.value_load(tab[0:1, 0, bass.ds(u * 2 + i, 1)], min_val=0, max_val=EXPERTS * TOKENS - TILE)
                sp.dma_start(to[:, i, :], by_expert[bass.ds(row, TILE), cols]).then_inc(done, 16)

            def step(u, r, k):
                if k < STEPS:
                    if k >= 2:
                        sp.wait_ge(h_turned, u - 1)
                        carry_waits(sp)
                    for i in range(2):
                        load_rows(u, i, n_rows[:, r], slice(0, D), n_loaded[r])
                if k >= 1:
                    if k >= 3:
                        sp.wait_ge(o_done, u - 2)
                        carry_waits(sp)
                    for i in range(2):
                        load_rows(u - 1, i, x_rows[:, 1 - r], slice(D, ROW), x_loaded[1 - r])

            for u in range(3):
                step(u, u % 2, u)
            with sp.Fori(3, STEPS - 2, 2) as u:
                step(u, 1, 3)
                step(u + 1, 0, 4)
            step(STEPS - 1, 1, STEPS - 1)
            step(STEPS, 0, STEPS)
            for r in range(2):
                sp.wait_ge(out_stored[r], STEPS * 16)

        @block.gpsimd
        def _(pool):
            n = [0]

            def then(ins):
                n[0] += 1
                ins.then_inc(pchain, 1)
                pool.wait_ge(pchain, n[0])

            nc.gpsimd.memset(minus_half[:, :], -0.5)
            nc.gpsimd.memset(ones_b[:, :], 1.0)
            nc.gpsimd.memset(before[:, :], 1.0)
            then(nc.gpsimd.memset(ident[:, :], 0.0))
            then(nc.gpsimd.affine_select(out=ident[:, :], in_=ident[:, :], compare_op=ALU.not_equal, fill=1.0,
                                         base=0, pattern=[[-1, P]], channel_multiplier=1))
            nc.gpsimd.tensor_copy(identb[:, :], ident[:, :])
            nc.gpsimd.tensor_copy(identh[:, :], ident[:, :])
            nc.gpsimd.affine_select(out=before[:, :], in_=before[:, :], compare_op=ALU.is_gt, fill=0.0,
                                    base=0, pattern=[[1, P]], channel_multiplier=-1)
            then(nc.gpsimd.memset(sel[:], 0.0))
            then(nc.gpsimd.affine_select(out=sel[:], in_=sel[:], compare_op=ALU.not_equal, fill=1.0, base=0,
                                         pattern=[[-2, HEADS // 2], [-1, 2], [0, S]], channel_multiplier=1))
            iotas = ((rank8[:, :], [[-1, EXPERTS]], EXPERTS, 0), (region8[:, :], [[TOKENS, EXPERTS]], 0, 0),
                     (iota8[:, :], [[1, EXPERTS]], 0, 0), (token_no[:, :], [[TILE, 2]], 0, 1),
                     (thr[:], [[0, EXPERTS], [TILE, NT]], 0, 0), (slot_no[:, :], [[1, SLOTS]], 0, 0),
                     (part_no[:, :], [[0, 1]], 0, 1))
            for o, pat, base, cm in iotas:
                nc.gpsimd.iota(o, pattern=pat, base=base, channel_multiplier=cm, allow_small_or_imprecise_dtypes=True)
            then(nc.gpsimd.memset(tri8[:], 1.0))
            then(nc.gpsimd.affine_select(out=tri8[:], in_=tri8[:], compare_op=ALU.is_ge, fill=0.0, base=0,
                                         pattern=[[1, EXPERTS], [-1, EXPERTS]], channel_multiplier=0))
            nc.gpsimd.memset(k_t[:, 0], 0.0)
            nc.gpsimd.memset(k_t[:, 1], 0.0).then_inc(consts, 1)

            def normalise(c, r, k):
                pool.wait_ge(stats_done, c + 1)
                if k >= 2:
                    pool.wait_ge(xc_turned, c - 1)
                ins = nc.gpsimd.tensor_tensor(rstd[:, r], veps[:, r], minus_half[:, :], ALU.pow)
                ins.then_inc(xn_ready, 1)
                pool.wait_ge(xn_ready, c * 3 + 1)
                carry_waits(pool)
                for i in range(2):
                    nc.gpsimd.tensor_scalar(xn[:, r, i, :], x_in[:, r, i, :], mv[:, r, i, 0:1], rstd[:, r, i:i + 1],
                                            ALU.subtract, ALU.mult).then_inc(xn_ready, 1)

            for c in range(3):
                normalise(c, c % 2, c)
            pool.wait_ge(bo_ready, 1)
            pool.wait_ge(region_cleared, EXPERTS * 16)

            def body(c, r, k):
                if has(k + 3):
                    normalise(c + 3, 1 - r, k + 3)
                if has(k - 1):
                    pool.wait_ge(res_loaded[1 - r], twos(c, r, -1))
                    nc.gpsimd.tensor_tensor(x_res[:, 1 - r], x_res[:, 1 - r], b_row[:, :].unsqueeze(1).to_broadcast([P, 2, D]),
                                            ALU.add).then_inc(res_ready, 1)
                    pool.wait_ge(stats2_done, c)
                    nc.gpsimd.tensor_tensor(rstd2[:, :], w2var[:, :], minus_half[:, :], ALU.pow).then_inc(rstd2_done, 1)
                if has(k - 2):
                    pool.wait_ge(dest_done, c - 1)
                    pool.wait_ge(row_done, c - 1)
                    carry_waits(pool)
                    for i in range(2):
                        nc.gpsimd.indirect_dma_start(by_expert, bass.IndirectOffsetOnAxis(ap=dest[:, r, i:i + 1], axis=0),
                                                     rows[:, r, i, :], None).then_inc(scattered[r], 16)

            chunks(pool, body)

            def step(u, r, k):
                pool.wait_ge(o_done, u + 1)
                carry_waits(pool)
                for i in range(2):
                    nc.gpsimd.indirect_dma_start(out, bass.IndirectOffsetOnAxis(ap=o_idx[:, r, i:i + 1], axis=0),
                                                 o_rows[:, r, i, :], None, bounds_check=TOKENS - 1,
                                                 oob_is_err=False).then_inc(out_stored[r], 16)

            with pool.Fori(0, STEPS - 1, 2) as u:
                step(u, 0, 2)
                step(u + 1, 1, 3)

        @block.tensor
        def _(pe):
            mm, tr = nc.tensor.matmul, nc.tensor.transpose

            pe.wait_ge(w_loaded, W_LOADS * 16)
            pe.wait_ge(consts, 1)
            for i in range(3):
                tr(A[0][:, i * P:(i + 1) * P], w_in[:, i, :], ident[:, :])
            tr(A[0][:, 3 * P:3 * P + EXPERTS], rw_in[:, :], ident[0:EXPERTS, 0:EXPERTS])
            for p in range(2):
                last = tr(A[1][0:64, p * P:(p + 1) * P], w_in[:, 3, 64 * p:64 * p + 64], ident[:, :])
            last.then_inc(w_turned, 1)

            def turn_xc(c, r, k):
                pe.wait_ge(xn_ready, (c + 1) * 3)
                pe.wait_ge(xc_loaded[r], twos(c, r, 0) * 2)
                if k >= 4:
                    pe.wait_ge(x2_done, c - 3)
                for i in range(2):
                    tr(M0[:, i * P:(i + 1) * P], xn[:, r, i, :], ident[:, :])
                for i in range(2):
                    last = tr(M0[:, (2 + i) * P:(3 + i) * P], c_in[:, r, i, :], ident[:, :])
                last.then_inc(xc_turned, 1)

            def proj_q(c, r):
                pe.wait_ge(xcT_ready, c + 1)
                mm(M0[:, 0:CH], wT[:, 0, :], xcT[:, r, 0:2, :], start=True, stop=True).then_inc(q_proj, 1)

            def proj_k(c, r, before_it):
                before_it()
                mm(M1[:, 0:CH], wT[:, 1, :], xcT[:, r, 2:4, :], start=True, stop=True).then_inc(k_proj, 1)

            def proj_v(c, r, before_it):
                before_it()
                for b in range(NB):
                    src = xcT[:, r, 2 + b // 2, (b % 2) * S:(b % 2 + 1) * S]
                    for hp in range(2):
                        last = mm(M0[64 * hp:64 * hp + 64, b * P:(b + 1) * P], src, wT[:, 2, :], start=True, stop=True,
                                  skip_group_check=True)
                last.then_inc(v_proj, 1)

            def scores_a(T, r, i, k):
                if i == 0:
                    pe.wait_ge(terms_loaded[r], k)
                for hh in range(2):
                    if T is not None:
                        pe.wait_ge(max_done, T * 2 - 1 + hh)
                    for b in range(2):
                        for q in (2 * hh, 2 * hh + 1):
                            t0 = i * TILE + b * S
                            last = mm(A[hh][b * S:(b + 1) * S, (q % 2) * 256:(q % 2 + 1) * 256],
                                      q_t[:, r, q, t0:t0 + S], k_t[:, r, q, 2 * i + b].rearrange("p m s -> p (m s)"), start=True, stop=True,
                                      skip_group_check=True)
                    last.then_inc(a_done, 1)

            def turn_negmax(T, i, k):
                pe.wait_ge(max_done, T * 2 + 2)
                if k >= 1:
                    pe.wait_ge(negmaxT_ready, T)
                tr(M2[:, :].bitcast(BF16)[:, 0:P], negmax[:, i, :], identb[:, :]).then_inc(negmax_turned, 1)

            def scores_st(T, r, i, k):
                pe.wait_ge(negmaxT_ready, T + 1)
                for hh in range(2):
                    if k >= 1:
                        pe.wait_ge(e32_done, T * 2 - 1 + hh)
                    for pr in range(4):
                        pair = 4 * hh + pr
                        q, m = pair // 2, (pair % 2) * 2
                        mm(ST[hh][:, pr * 128:(pr + 1) * 128], sel[:, pair].rearrange("p a b -> p (a b)"), negmaxT[:, i, :],
                           start=True, stop=False, skip_group_check=True)
                        for b in range(2):
                            t0 = i * TILE + b * S
                            last = mm(ST[hh][:, pr * 128 + b * S:pr * 128 + (b + 1) * S],
                                      k_t[:, r, q, 2 * i + b, m:m + 2, :].rearrange("p m s -> p (m s)"), q_t[:, r, q, t0:t0 + S],
                                      start=False, stop=True, skip_group_check=True)
                    last.then_inc(st_done, 1)

            def attend(T, r, i, k):
                pe.wait_ge(e_lo_done, T * 2 + 2)
                if k >= 1:
                    pe.wait_ge(attn_done, T * 2)
                for b in range(2):
                    for q in range(QUADS):
                        o = AV[:, b * 256 + q * 4 * VW:b * 256 + (q + 1) * 4 * VW]
                        pr = (q % 2) * 2
                        for n, (e, v) in enumerate(((e_hi, v_hi), (e_lo, v_hi), (e_hi, v_lo), (e_lo, v_lo))):
                            last = mm(o, e[:, i, q // 2, b, pr:pr + 2, :].rearrange("p a b -> p (a b)"),
                                      v[:, r, 2 * i + b, 2 * q:2 * q + 2].rearrange("p a b c -> p (a b c)"),
                                      start=(n == 0), stop=(n == 3))
                last.then_inc(av_done, 1)

            def turn_attn(c, r, before_it):
                pe.wait_ge(attn_done, (c + 1) * 4)
                before_it()
                carry_waits(pe)
                for b in range(NB):
                    last = tr(M1[0:64, b * P:(b + 1) * P], attn[:, r, b].rearrange("p a b -> p (a b)"), ident[:, :])
                last.then_inc(attn_turned, 1)

            def proj_o(c, before_it):
                pe.wait_ge(attnT_ready, c + 1)
                before_it()
                for i in range(2):
                    for p in range(2):
                        last = mm(M0[:, i * P:(i + 1) * P], attnT[:, p, 2 * i:2 * i + 2, :].rearrange("p a b -> p (a b)"), woT[:, p, :],
                                  start=(p == 0), stop=(p == 1))
                last.then_inc(y_done, 1)

            def turn_n2(c, r, before_it):
                pe.wait_ge(n2_done, (c + 1) * 2)
                before_it()
                for i in range(2):
                    last = tr(M1[:, i * P:(i + 1) * P], rows[:, r, i, 0:D], ident[:, :])
                last.then_inc(n2_turned, 1)

            def route(c, before_it):
                pe.wait_ge(hT_ready, c + 1)
                before_it()
                for i in range(2):
                    last = mm(M0[:, i * EXPERTS:(i + 1) * EXPERTS], hT32[:, i * TILE:(i + 1) * TILE], rwT[:, :],
                              start=True, stop=True)
                last.then_inc(logits_done, 1)

            def count(c, k, before_it):
                pe.wait_ge(onehot_done, c + 1)
                if k >= 3:
                    pe.wait_ge(seen_done, c)
                before_it()
                mm(M1[:, 0:EXPERTS], before[:, :], onehot_b[:, 0, :], start=True, stop=False)
                mm(M1[:, 0:EXPERTS], ones_b[:, :], seen[:, :], start=False, stop=True)
                mm(M1[:, EXPERTS:2 * EXPERTS], before[:, :], onehot_b[:, 1, :], start=True, stop=False)
                mm(M1[:, EXPERTS:2 * EXPERTS], ones_b[:, :], onehot_b[:, 0, :], start=False, stop=False)
                mm(M1[:, EXPERTS:2 * EXPERTS], ones_b[:, :], seen[:, :], start=False, stop=True).then_inc(pos_done, 1)

            nothing = lambda: None
            pe.wait_ge(w_kept, 1)
            for p in range(2):
                last = mm(M2[:, 0:D], bv_col[:, p:p + 1].to_broadcast([64, P]), woT[:, p, :], start=(p == 0), stop=(p == 1))
            last.then_inc(bv_proj, 1)
            for c in range(2):
                if c == 1:
                    pe.wait_ge(qk_lo_done, 1)
                turn_xc(c, c, c)
                proj_q(c, c)
                proj_k(c, c, (lambda: pe.wait_ge(qk_lo_done, 2)) if c else nothing)
            proj_v(0, 0, lambda: pe.wait_ge(qk_lo_done, 3))
            pe.wait_ge(bo_ready, 1)
            scores_a(None, 0, 0, 80)
            turn_negmax(0, 0, 0)

            def body(c, r, k):
                if has(k):
                    scores_a(c * 2 + 1, r, 1, None)
                if has(k + 2):
                    if not has(k - 2):
                        pe.wait_ge(v_lo_done, (c + 1) * 2)
                    turn_xc(c + 2, r, k + 2)
                if has(k - 2):
                    turn_n2(c - 2, r, lambda: pe.wait_ge(dest_done, c - 2) if has(k - 3)
                            else pe.wait_ge(attnT_ready, c - 1))
                if has(k):
                    scores_st(c * 2, r, 0, k)
                if has(k + 2):
                    proj_q(c + 2, r)
                    proj_k(c + 2, r, lambda: pe.wait_ge(hT_ready, c - 1) if has(k - 2)
                           else pe.wait_ge(qk_lo_done, (c + 2) * 2))
                if has(k - 1):
                    attend(c * 2 - 1, 1 - r, 1, k - 1 + 1)
                if has(k - 2):
                    route(c - 2, lambda: pe.wait_ge(qk_lo_done, (c + 3) * 2 - 1) if has(k + 2)
                          else pe.wait_ge(x2_done, c - 1))
                if has(k):
                    turn_negmax(c * 2 + 1, 1, k + 1)
                if has(k + 1):
                    proj_v(c + 1, 1 - r, lambda: pe.wait_ge(onehot_done, c - 1) if has(k - 2)
                           else pe.wait_ge(qk_lo_done, (c + 3) * 2 - 1))
                if has(k + 1):
                    scores_a(c * 2 + 2, 1 - r, 0, twos(c, r, 1) * 5)
                if has(k - 1):
                    turn_attn(c - 1, 1 - r, lambda: pe.wait_ge(qk_lo_done, (c + 3) * 2) if has(k + 2)
                              else pe.wait_ge(hT_ready, c - 1))
                if has(k):
                    scores_st(c * 2 + 1, r, 1, k + 1)
                if has(k - 1):
                    proj_o(c - 1, lambda: pe.wait_ge(v_lo_done, (c + 2) * 2) if has(k + 1)
                           else pe.wait_ge(onehot_done, c - 1))
                if has(k):
                    attend(c * 2, r, 0, k)
                if has(k - 2):
                    count(c - 2, k, lambda: pe.wait_ge(attnT_ready, c) if has(k - 1)
                          else pe.wait_ge(hT_ready, c - 1))
                if has(k + 1):
                    turn_negmax(c * 2 + 2, 0, k + 1)

            chunks(pe, body)

            pe.wait_ge(seen_done, NCH)
            pe.wait_ge(dest_done, NCH)
            mm(M1[:, 0:EXPERTS], ones_b[:, :], seen[:, :], start=True, stop=True).then_inc(counts_done, 1)

            pe.wait_ge(signs, 1)
            pe.wait_ge(max_done, NT * 2)
            pe.wait_ge(e32_done, NT * 2)
            pe.wait_ge(attn_done, NT * 2)
            places = [A[0], A[1], ST[0], ST[1], AV]
            for n in range(4 * BLOCKS):
                e, c = (n % (2 * BLOCKS)) // 2, n % 2
                src = sign1[:, e, c, :] if n < 2 * BLOCKS else sign2[:, e, c * P:(c + 1) * P]
                last = tr(places[n // 8][:, :].bitcast(F16)[:, (n % 8) * P:(n % 8 + 1) * P], src, identh[:, :])
                if n % 8 == 7 or n == 4 * BLOCKS - 1:
                    last.then_inc(t_turned, 1)
            pe.wait_ge(t_kept, 3)
            for e in range(BLOCKS):
                last = mm(places[e // 4][:, (e % 4) * D:(e % 4 + 1) * D], s2[:, e:e + 1].to_broadcast([P, P]), ident[:, :],
                          start=True, stop=True, skip_group_check=True)
            last.then_inc(t_turned, 1)
            pe.wait_ge(t_kept, 6)

            XT, F1, YY = banks[0], [[banks[1], banks[2]], [banks[3], banks[4]]], [banks[5], banks[6]]

            def turn_h(u, r, k):
                pe.wait_ge(n_loaded[r], twos(u, r, 0) * 2)
                if k >= 1:
                    pe.wait_ge(h_done, u)
                for i in range(2):
                    last = tr(XT[:, i * TILE:(i + 1) * TILE], n_rows[:, r, i, :], ident[:, :])
                last.then_inc(h_turned, 1)

            def layer1(u, r, k):
                pe.wait_ge(h_done, u + 1)
                if k >= 2:
                    pe.wait_ge(g32_done, u - 1)
                for c in range(2):
                    for n, h in enumerate((h_hi, h_lo)):
                        mm(F1[r][0][:, c * CH:(c + 1) * CH], t1[:, 0, c, :], h[:, r, :], start=(n == 0), stop=(n == 1))
                for i in range(2):
                    e = pe.value_load(tab[0:1, 1, bass.ds(u * 2 + i, 1)], min_val=0, max_val=EXPERTS - 1)
                    for c in range(2):
                        for n, h in enumerate((h_hi, h_lo)):
                            last = mm(F1[r][1][:, c * CH + i * TILE:c * CH + (i + 1) * TILE], t1[:, bass.ds(e + 1, 1), c, :].rearrange("p a b -> p (a b)"),
                                      h[:, r, i * TILE:(i + 1) * TILE], start=(n == 0), stop=(n == 1))
                last.then_inc(f1_done, 1)

            def layer2(u, r, k):
                pe.wait_ge(g_done, u + 1)
                if k >= 2:
                    pe.wait_ge(o_done, u - 1)
                carry_waits(pe)
                for i in range(2):
                    e = pe.value_load(tab[0:1, 1, bass.ds(u * 2 + i, 1)], min_val=0, max_val=EXPERTS - 1)
                    for w in range(2):
                        o = YY[r][:, (2 * w + i) * D:(2 * w + i + 1) * D]
                        for n in range(4):
                            c, g = n // 2, (g_hi, g_lo)[n % 2]
                            wt = t2[:, 0, c, :] if w == 0 else t2[:, bass.ds(e + 1, 1), c, :].rearrange("p a b -> p (a b)")
                            last = mm(o, g[:, r, w, c, i * TILE:(i + 1) * TILE], wt, start=(n == 0), stop=(n == 3))
                last.then_inc(f2_done, 1)

            def step(u, r, k):
                if k + 1 < STEPS:
                    turn_h(u + 1, 1 - r, k + 1)
                layer1(u, r, k)
                if k >= 1:
                    layer2(u - 1, 1 - r, k - 1)

            pe.wait_ge(tab_done, 1)
            turn_h(0, 0, 0)
            for u in range(3):
                step(u, u % 2, u)
            with pe.Fori(3, STEPS - 2, 2) as u:
                step(u, 1, 3)
                step(u + 1, 0, 4)
            step(STEPS - 1, 1, STEPS - 1)
            layer2(STEPS - 1, 1, STEPS - 1)

        @block.scalar
        def _(act):
            fn = nc.scalar.activation

            act.wait_ge(w_turned, 1)
            for i in range(2):
                fn(wT[:, i, :].rearrange("p (m d q) -> p m d q", m=4, d=HD),
                   A[0][:, i * P:(i + 1) * P].rearrange("p (q m d) -> p m d q", q=QUADS, m=4), ACT.Copy)
            fn(wT[:, 2, :], A[0][:, 2 * P:3 * P], ACT.Copy)
            fn(rwT[:, :], A[0][:, 3 * P:3 * P + EXPERTS], ACT.Copy)
            fn(woT[:, :, :], A[1][0:64, 0:2 * P].rearrange("p (a b) -> p a b", a=2), ACT.Copy).then_inc(w_kept, 1)

            def keep_xcT(c, r, k):
                act.wait_ge(xc_turned, c + 1)
                if k >= 2:
                    act.wait_ge(v_proj, c - 1)
                fn(xcT[:, r], M0[:, 0:512].rearrange("p (a b) -> p a b", a=4), ACT.Copy).then_inc(xcT_ready, 1)

            def qk_hi(c, k):
                if k >= 1:
                    act.wait_ge(terms_stored, c * 128)
                for i, (s, bank) in enumerate(((q_proj, M0), (k_proj, M1))):
                    act.wait_ge(s, c + 1)
                    fn(qk_hl[:, i, 0, :], bank[:, 0:CH], ACT.Identity, bias=b_col[:, i:i + 1]).then_inc(qk_hi_done, 1)

            def keep_v_hi(c, r, k):
                act.wait_ge(v_proj, c + 1)
                if k >= 2:
                    act.wait_ge(av_done, (c - 1) * 2)
                for hp in range(2):
                    fn(v_part(v_hi, r, hp), v_sums(hp), ACT.Copy).then_inc(v_hi_done, 1)

            def keep_negmaxT(T, i, k):
                act.wait_ge(negmax_turned, T + 1)
                if k >= 1:
                    act.wait_ge(st_done, (T - 1) * 2)
                fn(negmaxT[:, i, :], M2[:, :].bitcast(BF16)[:, 0:P], ACT.Copy).then_inc(negmaxT_ready, 1)

            def exponentials(T, i, k):
                for hh in range(2):
                    act.wait_ge(st_done, T * 2 + 1 + hh)
                    if k >= 2:
                        act.wait_ge(av_done, T - 1)
                    src = ST[hh][:, :].rearrange("p (a b c) -> p a b c", a=4, b=2)
                    fn(e_hi[:, i, hh].rearrange("p b a c -> p a b c"), src, ACT.Exp, bias=lne_col, scale=SCALE).then_inc(e_hi_done, 1)
                    if k >= 1:
                        act.wait_ge(e_lo_done, T * 2 - 1 + hh)
                    fn(e32[:, hh].rearrange("p b a c -> p a b c"), src, ACT.Exp, bias=lne_col, scale=SCALE).then_inc(e32_done, 1)

            def keep_attnT(c):
                act.wait_ge(attn_turned, c + 1)
                fn(attnT[:].rearrange("p a b c -> p b a c"), M1[0:64, :].rearrange("p (b a c) -> p b a c", b=NB, a=2), ACT.Copy).then_inc(attnT_ready, 1)

            def keep_hT(c):
                act.wait_ge(n2_turned, c + 1)
                fn(hT32[:, :], M1[:, 0:CH], ACT.Identity, bias=ln_col[:, 1:2], scale=ln_col[:, 0:1]).then_inc(hT_ready, 1)

            lne_col = lne[:, 0:1]
            act.wait_ge(vconsts, 2)
            for c in range(2):
                keep_xcT(c, c, c)
                qk_hi(c, c)
            keep_v_hi(0, 0, 0)
            keep_negmaxT(0, 0, 0)

            def body(c, r, k):
                if has(k + 2):
                    keep_xcT(c + 2, r, k + 2)
                if has(k - 2):
                    keep_hT(c - 2)
                if has(k):
                    exponentials(c * 2, 0, 2 * k)
                if has(k + 2):
                    qk_hi(c + 2, k + 2)
                if has(k):
                    keep_negmaxT(c * 2 + 1, 1, k)
                if has(k - 2):
                    act.wait_ge(shifted_done, c - 1)
                    fn(expo[:], shifted[:], ACT.Exp).then_inc(expo_done, 1)
                if has(k + 1):
                    keep_v_hi(c + 1, 1 - r, k + 1)
                if has(k - 1):
                    keep_attnT(c - 1)
                if has(k):
                    exponentials(c * 2 + 1, 1, 2 * k + 1)
                if has(k + 1):
                    keep_negmaxT(c * 2 + 2, 0, k + 1)

            chunks(act, body)

            flat = [t1[:].rearrange("p e c f -> p (e c) f"), t2[:].rearrange("p e c f -> p (e c) f")]
            places = [A[0], A[1], ST[0], ST[1], AV]
            for g in range(5):
                act.wait_ge(t_turned, g + 1)
                src = places[g][:, :].bitcast(F16).rearrange("p (a b) -> p a b", a=8)
                lo, hi = 8 * g, min(8 * g + 8, 4 * BLOCKS)
                edge = min(max(2 * BLOCKS, lo), hi)
                last = None
                for t, (a, b) in enumerate(((lo, edge), (edge, hi))):
                    if b > a:
                        last = fn(flat[t][:, a - t * 2 * BLOCKS:b - t * 2 * BLOCKS, :], src[:, a - lo:b - lo, :], ACT.Copy)
                last.then_inc(t_kept, 1)
            act.wait_ge(t_turned, 6)
            for g in range(3):
                a, b = 4 * g, min(4 * g + 4, BLOCKS)
                last = fn(s2_row[:, a:b, :], places[g][:, 0:(b - a) * D].rearrange("p (a b) -> p a b", b=D), ACT.Copy)
            last.then_inc(t_kept, 1)

            F1 = [[banks[1], banks[2]], [banks[3], banks[4]]]

            def step(u, r, k):
                act.wait_ge(f1_done, u + 1)
                if k >= 1:
                    act.wait_ge(g_done, u)
                for c in range(2):
                    fn(g32[:, 0, c, :], F1[r][0][:, c * CH:(c + 1) * CH], ACT.Silu, scale=s1[:, c:c + 1])
                for i in range(2):
                    e = act.value_load(tab[0:1, 1, bass.ds(u * 2 + i, 1)], min_val=0, max_val=EXPERTS - 1)
                    for c in range(2):
                        last = fn(g32[:, 1, c, i * TILE:(i + 1) * TILE], F1[r][1][:, c * CH + i * TILE:c * CH + (i + 1) * TILE],
                                  ACT.Silu, scale=s1[:, bass.ds(e * 2 + (2 + c), 1)])
                last.then_inc(g32_done, 1)

            act.wait_ge(tab_done, 1)
            for u in range(2):
                step(u, u, u)
            with act.Fori(2, STEPS - 1, 2) as u:
                step(u, 0, 2)
                step(u + 1, 1, 3)

        @block.vector
        def _(dve):
            n = [0]
            v = nc.vector

            def then(ins):
                n[0] += 1
                ins.then_inc(chain, 1)
                dve.wait_ge(chain, n[0])

            v.memset(zeros[:, :], 0.0).then_inc(vconsts, 1)
            v.memset(lne[:, :], LNE)
            v.memset(rows[:, :, :, 2 * D:ROW], 0.0)
            v.memset(seen[:, :], 0.0)
            v.memset(negmax[:], 0.0)
            then(v.memset(v_hi[:], 0.0))
            v.memset(v_lo[:], 0.0)
            for hp in range(2):
                for r in range(2):
                    v.memset(v_part(v_hi, r, hp, HD, VW), 1.0)
            then(v.memset(s1h[:, :], 0.0))
            v.engine_nop().then_inc(vconsts, 1)

            def x_stats(c, r, k):
                dve.wait_ge(xc_loaded[r], twos(c, r, 0) * 2)
                if k >= 2:
                    dve.wait_ge(xn_ready, (c - 1) * 3)
                for i in range(2):
                    v.bn_stats(stats[:, i, :], x_in[:, r, i, :]).then_inc(st_chain, 1)
                for i in range(2):
                    dve.wait_ge(st_chain, c * 4 + 1 + i)
                    carry_waits(dve)
                    v.bn_aggr(mv[:, r, i, :], stats[:, i, :]).then_inc(st_chain, 1)
                dve.wait_ge(st_chain, c * 4 + 4)
                v.tensor_scalar(veps[:, r], mv[:, r, :, 1], LN_EPS, None, ALU.add).then_inc(stats_done, 1)

            def qk_lo(c):
                for i, bank in enumerate((M0, M1)):
                    dve.wait_ge(qk_hi_done, c * 2 + 1 + i)
                    v.scalar_tensor_tensor(qk_hl[:, i, 1, :], bank[:, 0:CH], b_col[:, i:i + 1], qk_hl[:, i, 0, :],
                                           ALU.add, ALU.subtract).then_inc(qk_lo_done, 1)

            def v_low(c, r, k):
                for hp in range(2):
                    dve.wait_ge(v_hi_done, c * 2 + 1 + hp)
                    v.tensor_tensor(v_part(v_lo, r, hp), v_sums(hp), v_part(v_hi, r, hp), ALU.subtract).then_inc(v_lo_done, 1)

            def maxima(T, i, k):
                for hh in range(2):
                    dve.wait_ge(a_done, T * 2 + 1 + hh)
                    if k >= 1:
                        dve.wait_ge(negmax_turned, T - 1)
                    v.tensor_reduce(negmax[:, i, 8 * hh:8 * hh + 8], A[hh][:, :].rearrange("p (a b) -> p a b", b=S),
                                    X, ALU.max, negate=True).then_inc(max_done, 1)

            def e_low(T, i, k):
                for hh in range(2):
                    dve.wait_ge(e32_done, T * 2 + 1 + hh)
                    dve.wait_ge(e_hi_done, T * 2 + 1 + hh)
                    if k >= 2:
                        dve.wait_ge(av_done, T - 1)
                    hi, lo = (t[:, i, hh].rearrange("p a b c -> p (a b c)") for t in (e_hi, e_lo))
                    v.tensor_tensor(lo, e32[:, hh].rearrange("p a b c -> p (a b c)"), hi, ALU.subtract).then_inc(e_lo_done, 1)

            def divide(T, r, i):
                dve.wait_ge(av_done, T + 1)
                av = AV[:, :].rearrange("p (b x) -> p b x", b=2)[:, :, 0:16 * VW].rearrange("p b (h pp d) -> p b h pp d", pp=2, d=VW)
                for pp in range(2):
                    ps = slice(64 * pp, 64 * pp + 64)
                    v.reciprocal(rden[ps], av[ps, :, :, pp, HD]).then_inc(rden_done, 1)
                for pp in range(2):
                    ps = slice(64 * pp, 64 * pp + 64)
                    dve.wait_ge(rden_done, T * 2 + 1 + pp)
                    v.tensor_tensor(attn[ps, r, 2 * i:2 * i + 2], av[ps, :, :, pp, 0:HD],
                                    rden[ps].unsqueeze(3).to_broadcast([64, 2, 8, HD]), ALU.mult).then_inc(attn_done, 1)

            def residual(c, r, k):
                dve.wait_ge(y_done, c + 1)
                dve.wait_ge(res_ready, c + 1)
                if k >= 2:
                    dve.wait_ge(scattered[r], twos(c, r, -2) * 2)
                v.tensor_tensor(rows[:, r, :, D:2 * D], M0[:, 0:CH].rearrange("p (a b) -> p a b", a=2), x_res[:, r],
                                ALU.add).then_inc(x2_done, 1)
                dve.wait_ge(x2_done, c + 1)
                for i in range(2):
                    v.bn_stats(stats2[:, i, :], rows[:, r, i, D:2 * D]).then_inc(st2_chain, 1)
                for i in range(2):
                    dve.wait_ge(st2_chain, c * 4 + 1 + i)
                    carry_waits(dve)
                    v.bn_aggr(mv2[:, i, :], stats2[:, i, :]).then_inc(st2_chain, 1)
                dve.wait_ge(st2_chain, c * 4 + 4)
                v.tensor_scalar(w2var[:, :], mv2[:, :, 1], 1.0 + LN_EPS, LN_EPS * LN_EPS, ALU.mult, ALU.add).then_inc(stats2_done, 1)

            def normalise2(c, r):
                dve.wait_ge(rstd2_done, c + 1)
                for i in range(2):
                    v.tensor_scalar(rows[:, r, i, 0:D], rows[:, r, i, D:2 * D], mv2[:, i, 0:1], rstd2[:, i:i + 1],
                                    ALU.subtract, ALU.mult).then_inc(n2_done, 1)

            def pick(c, k):
                lg = M0[:, 0:2 * EXPERTS].rearrange("p (a b) -> p a b", a=2)
                wide = lambda a: a.unsqueeze(2).to_broadcast([P, 2, EXPERTS])
                dve.wait_ge(logits_done, c + 1)
                v.tensor_reduce(top[:, :], lg, X, ALU.max).then_inc(pick_chain, 1)
                dve.wait_ge(pick_chain, c * 4 + 1)
                if k >= 1:
                    dve.wait_ge(expo_done, c)
                v.tensor_tensor(shifted[:], lg, wide(top[:, :]), ALU.subtract).then_inc(shifted_done, 1)
                dve.wait_ge(shifted_done, c + 1)
                v.scalar_tensor_tensor(is_top[:], shifted[:], 0.0, rank8[:, :].unsqueeze(1).to_broadcast([P, 2, EXPERTS]),
                                       ALU.is_equal, ALU.mult).then_inc(pick_chain, 1)
                dve.wait_ge(pick_chain, c * 4 + 2)
                v.tensor_reduce(first[:, :], is_top[:], X, ALU.max).then_inc(pick_chain, 1)
                dve.wait_ge(pick_chain, c * 4 + 3)
                v.tensor_tensor(onehot[:], is_top[:], wide(first[:, :]), ALU.is_equal).then_inc(pick_chain, 1)
                dve.wait_ge(pick_chain, c * 4 + 4)
                v.tensor_copy(onehot_b[:], onehot[:]).then_inc(onehot_done, 1)

            def gates(c, r):
                dve.wait_ge(expo_done, c + 1)
                v.tensor_reduce(expsum[:, :], expo[:], X, ALU.add).then_inc(gate_chain, 1)
                dve.wait_ge(gate_chain, c * 2 + 1)
                v.reciprocal(rows[:, r, :, GATE], expsum[:, :])
                v.tensor_copy(rows[:, r, :, TOKEN], token_no[:, :]).then_inc(row_done, 1)
                dve.wait_ge(row_done, c + 1)
                v.tensor_scalar(token_no[:, :], token_no[:, :], float(CH), None, ALU.add).then_inc(gate_chain, 1)
                dve.wait_ge(gate_chain, c * 2 + 2)

            def place(c, r, k):
                dve.wait_ge(pos_done, c + 1)
                v.tensor_tensor(pos8[:], M1[:, 0:2 * EXPERTS].rearrange("p (a b) -> p a b", a=2),
                                region8[:, :].unsqueeze(1).to_broadcast([P, 2, EXPERTS]), ALU.add).then_inc(place_chain, 1)
                dve.wait_ge(place_chain, c * 3 + 1)
                v.tensor_tensor(pos8m[:], pos8[:], onehot[:], ALU.mult).then_inc(place_chain, 1)
                v.tensor_tensor(seen2[:, :], seen[:, :], onehot_b[:, 0, :], ALU.add).then_inc(place_chain, 1)
                dve.wait_ge(place_chain, c * 3 + 2)
                with nc.allow_low_precision(reason="whole numbers below 2 ** 24"):
                    v.tensor_reduce(dest[:, r, :], pos8m[:], X, ALU.add).then_inc(dest_done, 1)
                dve.wait_ge(place_chain, c * 3 + 3)
                v.tensor_tensor(seen[:, :], seen2[:, :], onehot_b[:, 1, :], ALU.add).then_inc(seen_done, 1)

            for c in range(2):
                x_stats(c, c, c)
            dve.wait_ge(bv_proj, 1)
            dve.wait_ge(w_loaded, W_LOADS * 16)
            v.tensor_tensor(b_row[:, :], M2[:, 0:D], bo_row[:, :], ALU.add).then_inc(bo_ready, 1)
            for c in range(2):
                qk_lo(c)
                if c == 0:
                    x_stats(2, 0, 2)
            v_low(0, 0, 0)
            maxima(0, 0, 0)

            dve.wait_ge(ffn_w_loaded, 4 * 16)
            for w, s, half, neg, wid in ((w1_in[:].rearrange("p e c d -> p (e c) d"), s1, s1h, s1n, D), (w2_in[:], s2, s2h, s2n, FE)):
                then(v.tensor_reduce(s[:, :], w, X, ALU.add, apply_absolute_value=True))
                then(v.tensor_scalar(s[:, :], s[:, :], 1.0 / wid, 1e-5, ALU.mult, ALU.max))
                v.tensor_scalar(half[:, :], s[:, :], 0.5, None, ALU.mult)
                then(v.tensor_scalar(neg[:, :], s[:, :], -0.5, None, ALU.mult))
            for e in range(BLOCKS):
                for c in range(2):
                    j = 2 * e + c
                    v.tensor_scalar(low1[:, c, :], w1_in[:, e, c, :], s1n[:, j:j + 1], None, ALU.is_lt)
                then(v.tensor_scalar(low2[:, :], w2_in[:, e, :], s2n[:, e:e + 1], None, ALU.is_lt))
                for c in range(2):
                    j = 2 * e + c
                    v.scalar_tensor_tensor(sign1[:, e, c, :], w1_in[:, e, c, :], s1h[:, j:j + 1], low1[:, c, :],
                                           ALU.is_gt, ALU.subtract)
                then(v.scalar_tensor_tensor(sign2[:, e, :], w2_in[:, e, :], s2h[:, e:e + 1], low2[:, :],
                                            ALU.is_gt, ALU.subtract))
            v.engine_nop().then_inc(signs, 1)

            def body(c, r, k):
                if has(k):
                    maxima(c * 2 + 1, 1, k)
                if has(k + 3):
                    x_stats(c + 3, 1 - r, k + 3)
                if has(k):
                    e_low(c * 2, 0, 2 * k)
                if has(k + 2):
                    qk_lo(c + 2)
                if has(k - 1):
                    if k - 1 >= 2:
                        dve.wait_ge(attn_turned, c - 2)
                    divide(c * 2 - 1, 1 - r, 1)
                if has(k - 2):
                    pick(c - 2, k - 2)
                if has(k + 1):
                    v_low(c + 1, 1 - r, k + 1)
                    maxima(c * 2 + 2, 0, k + 1)
                if has(k):
                    e_low(c * 2 + 1, 1, 2 * k + 1)
                if has(k - 2):
                    gates(c - 2, r)
                if has(k - 1):
                    residual(c - 1, 1 - r, k - 1)
                if has(k):
                    if k >= 2:
                        dve.wait_ge(attn_turned, c - 1)
                    divide(c * 2, r, 0)
                if has(k - 2):
                    place(c - 2, r, k - 2)
                if has(k - 1):
                    normalise2(c - 1, 1 - r)

            chunks(dve, body)

            row8 = lambda a: a.unsqueeze(1).to_broadcast([P, SLOTS, EXPERTS])
            col8 = lambda a: a.unsqueeze(2).to_broadcast([P, SLOTS, EXPERTS])
            dve.wait_ge(counts_done, 1)
            then(v.tensor_copy(cnt[:, :], M1[:, 0:EXPERTS]))
            then(v.tensor_tensor(over[:], cnt[:, :].unsqueeze(2).to_broadcast([P, EXPERTS, NT]), thr[:], ALU.is_gt))
            then(v.tensor_reduce(tiles8[:, :], over[:], X, ALU.add))
            then(v.tensor_tensor(prod8[:], tiles8[:, :].unsqueeze(1).to_broadcast([P, EXPERTS, EXPERTS]), tri8[:], ALU.mult))
            then(v.tensor_reduce(upto8[:, :], prod8[:], X, ALU.add))
            then(v.tensor_tensor(start8[:, :], upto8[:, :], tiles8[:, :], ALU.subtract))
            then(v.tensor_tensor(sl_ge[:], col8(slot_no[:, :]), row8(upto8[:, :]), ALU.is_ge))
            then(v.tensor_reduce(sl_e[:, :], sl_ge[:], X, ALU.add))
            then(v.tensor_tensor(sl_oh[:], col8(sl_e[:, :]), row8(iota8[:, :]), ALU.is_equal))
            v.tensor_tensor(sl_m[:], sl_oh[:], row8(start8[:, :]), ALU.mult)
            then(v.tensor_tensor(sl_m2[:], sl_oh[:], row8(cnt[:, :]), ALU.mult))
            v.tensor_reduce(sl_start[:, :], sl_m[:], X, ALU.add)
            then(v.tensor_reduce(sl_n[:, :], sl_m2[:], X, ALU.add))
            v.tensor_scalar(sl_last[:, :], sl_n[:, :], -float(TILE), 0.0, ALU.add, ALU.max)
            then(v.tensor_tensor(sl_j[:, :], slot_no[:, :], sl_start[:, :], ALU.subtract))
            then(v.tensor_scalar(sl_j[:, :], sl_j[:, :], float(TILE), None, ALU.mult))
            then(v.tensor_tensor(sl_off[:, :], sl_j[:, :], sl_last[:, :], ALU.min))
            v.tensor_scalar(sl_ec[:, :], sl_e[:, :], float(EXPERTS - 1), None, ALU.min)
            then(v.tensor_scalar(sl_row[:, :], sl_off[:, :], part_no[:, 0:1], None, ALU.add))
            v.tensor_tensor(sl_v1[:, :], sl_row[:, :], sl_j[:, :], ALU.is_ge)
            then(v.tensor_tensor(sl_v2[:, :], sl_row[:, :], sl_n[:, :], ALU.is_lt))
            then(v.tensor_tensor(valid[:, :], sl_v1[:, :], sl_v2[:, :], ALU.mult))
            then(v.scalar_tensor_tensor(sl_base[:, :], sl_ec[:, :], float(TOKENS), sl_off[:, :], ALU.mult, ALU.add))
            then(v.tensor_copy(tab[0:1, 0, :], sl_base[0:1, :]))
            v.tensor_copy(tab[0:1, 1, :], sl_ec[0:1, :]).then_inc(tab_done, 1)

            XT, YY = banks[0], [banks[5], banks[6]]

            def split_h(u, r, k):
                dve.wait_ge(h_turned, u + 1)
                v.tensor_scalar(hf[:, :], XT[:, 0:CH], ln_col[:, 0:1], ln_col[:, 1:2], ALU.mult, ALU.add).then_inc(h_chain, 1)
                dve.wait_ge(h_chain, u * 2 + 1)
                if k >= 2:
                    dve.wait_ge(f1_done, u - 1)
                v.tensor_copy(h_hi[:, r, :], hf[:, :]).then_inc(h_chain, 1)
                dve.wait_ge(h_chain, u * 2 + 2)
                v.tensor_tensor(h_lo[:, r, :], hf[:, :], h_hi[:, r, :], ALU.subtract).then_inc(h_done, 1)

            def split_g(u, r, k):
                dve.wait_ge(g32_done, u + 1)
                if k >= 2:
                    dve.wait_ge(f2_done, u - 1)
                src = g32[:].rearrange("p a b c -> p (a b c)")
                hi, lo = (t[:, r].rearrange("p a b c -> p (a b c)") for t in (g_hi, g_lo))
                v.tensor_copy(hi, src).then_inc(g_chain, 1)
                dve.wait_ge(g_chain, u + 1)
                v.tensor_tensor(lo, src, hi, ALU.subtract).then_inc(g_done, 1)

            def finish(u, r, k):
                dve.wait_ge(f2_done, u + 1)
                dve.wait_ge(x_loaded[r], twos(u, r, 0) * 2)
                if k >= 2:
                    dve.wait_ge(out_stored[r], twos(u, r, -2) * 2)
                if k >= 1:
                    dve.wait_ge(o_done, u)
                v.scalar_tensor_tensor(o_idx_f[:, :], x_rows[:, r, :, TOKEN - D], -NOWHERE, valid[:, bass.ds(u * 2, 2)],
                                       ALU.add, ALU.mult).then_inc(o_chain, 1)
                v.tensor_tensor(sh_out[:], YY[r][:, 0:2 * D].rearrange("p (a b) -> p a b", a=2),
                                s2_row[:, 0, :].unsqueeze(1).to_broadcast([P, 2, D]), ALU.mult).then_inc(o_chain, 1)
                for i in range(2):
                    e = dve.value_load(tab[0:1, 1, bass.ds(u * 2 + i, 1)], min_val=0, max_val=EXPERTS - 1)
                    v.scalar_tensor_tensor(ex_out[:, i, :], YY[r][:, (2 + i) * D:(3 + i) * D], x_rows[:, r, i, GATE - D:GATE - D + 1],
                                           s2_row[:, bass.ds(e + 1, 1), :].rearrange("p a b -> p (a b)"), ALU.mult, ALU.mult).then_inc(o_chain, 1)
                dve.wait_ge(o_chain, u * 5 + 4)
                v.tensor_tensor(o_sum[:], sh_out[:], ex_out[:], ALU.add).then_inc(o_chain, 1)
                dve.wait_ge(o_chain, u * 5 + 5)
                v.tensor_tensor(o_rows[:, r], o_sum[:], x_rows[:, r, :, 0:D], ALU.add)
                v.tensor_scalar(o_idx[:, r, :], o_idx_f[:, :], NOWHERE, None, ALU.add).then_inc(o_done, 1)

            def step(u, r, k):
                if k + 1 < STEPS:
                    split_h(u + 1, 1 - r, k + 1)
                split_g(u, r, k)
                if k >= 1:
                    finish(u - 1, 1 - r, k - 1)

            dve.wait_ge(t_kept, 6)
            split_h(0, 0, 0)
            for u in range(3):
                step(u, u % 2, u)
            with dve.Fori(3, STEPS - 2, 2) as u:
                step(u, 1, 3)
                step(u + 1, 0, 4)
            step(STEPS - 1, 1, STEPS - 1)
            finish(STEPS - 1, 1, STEPS - 1)


_INS = ["x", "ctx_1024", "L0_xattn_Wq", "L0_xattn_bq", "L0_xattn_Wk", "L0_xattn_bk", "L0_xattn_Wv", "L0_xattn_bv",
        "L0_xattn_Wo", "L0_xattn_bo", "L0_ffn_shared_w1", "L0_ffn_shared_w2", "L0_ffn_expert_w1", "L0_ffn_expert_w2",
        "L0_ffn_router_w", "L0_ffn_ln_gamma", "L0_ffn_ln_beta"]


def kernel(**inputs):
    import numpy as np
    import concourse.bacc as bacc
    from concourse.bass_utils import run_bass_kernel_spmd

    nc = bacc.Bacc("TRN2", target_bir_lowering=False, num_devices=1)
    arrays, args = {}, []
    for name in _INS:
        a = np.ascontiguousarray(inputs[name])
        if name in ("x", "ctx_1024"):
            shape = a.shape
            a = a.reshape(-1, shape[-1])
        arrays["in_" + name] = a
        args.append(nc.dram_tensor("in_" + name, a.shape, mybir.dt.from_np(a.dtype), kind="ExternalInput").ap())
    args.append(nc.dram_tensor("out", arrays["in_x"].shape, F32, kind="ExternalOutput").ap())
    block_program(nc, *args)
    r = run_bass_kernel_spmd(nc, [arrays], core_ids=[0])
    return r.results[0]["out"].reshape(shape)
```

```python
from contextlib import ExitStack

import concourse.bass as bass
from concourse import mybir

ALU = mybir.AluOpType
ACT = mybir.ActivationFunctionType
X = mybir.AxisListType.X
F32 = mybir.dt.float32
F16 = mybir.dt.float16
BF16 = mybir.dt.bfloat16
I32 = mybir.dt.int32

P = 128
D = 128
S = 64
HEADS, HD = 16, 8
QUADS = HEADS // 4
TILE = 128
CH = 256
NB = CH // S
EXPERTS = 8
FE = 256
BLOCKS = EXPERTS + 1
LN_EPS = 1e-5
VW = HD + 1
LNE = 4.1588830833596715
ROW = 2 * D + 4
GATE, TOKEN = 2 * D, 2 * D + 1


def block_program(nc, x, ctx_in, Wq, bq, Wk, bk, Wv, bv, Wo, bo, sw1, sw2, ew1, ew2, rw, gamma, beta, out):
    TOKENS = x.shape[0]
    NCH = TOKENS // CH
    NT = TOKENS // TILE
    SLOTS = -(-((TOKENS + EXPERTS * (TILE - 1)) // TILE) // 8) * 8
    STEPS = SLOTS // 2
    ROWBUFS = 6
    assert (STEPS - 8) % ROWBUFS == 0
    NOWHERE = float(2 * TOKENS)
    SCALE = float(HD) ** -0.5
    W_LOADS = 21

    qk_dram = nc.dram_tensor("qk_terms", (NCH, 2, 4, 4, 32, CH), F16).ap()
    by_expert = nc.dram_tensor("rows_by_expert", (EXPERTS * TOKENS, ROW), F32).ap()

    with ExitStack() as stack:
        def sb(name, shape, dt=F32):
            return stack.enter_context(nc.sbuf_tensor(name, shape, dt))

        def sem(name):
            return stack.enter_context(nc.semaphore(name))

        ident = sb("ident", [P, P])
        identb = sb("identb", [P, P], BF16)
        identh = sb("identh", [P, P], F16)
        w_in = sb("w_in", [P, 4, P])
        wT = sb("wT", [P, 3, P])
        woT = sb("woT", [64, 2, P])
        b_col = sb("b_col", [P, 2])
        bv_col = sb("bv_col", [64, 2])
        bo_row = sb("bo_row", [P, D])
        b_row = sb("b_row", [P, D])
        ln_col = sb("ln_col", [P, 2])
        rw_in = sb("rw_in", [EXPERTS, D])
        rwT = sb("rwT", [D, EXPERTS])
        w1_in = sb("w1_in", [P, BLOCKS, 2, D])
        w2_in = sb("w2_in", [P, BLOCKS, FE])
        sign1 = sb("sign1", [P, BLOCKS, 2, D], F16)
        sign2 = sb("sign2", [P, BLOCKS, FE], F16)
        low1 = sb("low1", [P, 2, D], F16)
        low2 = sb("low2", [P, FE], F16)
        s1 = sb("s1", [P, BLOCKS * 2])
        s1h = sb("s1h", [P, BLOCKS * 2])
        s1n = sb("s1n", [P, BLOCKS * 2])
        s2 = sb("s2", [P, BLOCKS])
        s2h = sb("s2h", [P, BLOCKS])
        s2n = sb("s2n", [P, BLOCKS])
        s2_row = sb("s2_row", [P, BLOCKS, D])
        t1 = sb("t1", [P, BLOCKS, 2, P], F16)
        t2 = sb("t2", [P, BLOCKS, 2, D], F16)
        zeros = sb("zeros", [P, ROW])
        lne = sb("lne", [P, 1])

        x_in = sb("x_in", [P, 2, 2, D])
        c_in = sb("c_in", [P, 2, 2, D])
        x_res = sb("x_res", [P, 2, 2, D])
        stats = sb("stats", [P, 2, 6])
        mv = sb("mv", [P, 2, 2, 2])
        veps = sb("veps", [P, 2, 2])
        rstd = sb("rstd", [P, 2, 2])
        minus_half = sb("minus_half", [P, 2])
        xn = sb("xn", [P, 2, 2, D])
        xcT = sb("xcT", [P, 2, 4, TILE])
        qk_hl = sb("qk_hl", [P, 2, 2, CH], F16)
        q_t = sb("q_t", [P, 2, QUADS, CH], F16)
        k_t = sb("k_t", [P, 2, QUADS, NB, 4, S], F16)
        v_hi = sb("v_hi", [P, 2, NB, 2 * QUADS, 2, VW], F16)
        v_lo = sb("v_lo", [P, 2, NB, 2 * QUADS, 2, VW], F16)
        negmax = sb("negmax", [P, 2, P], BF16)
        negmaxT = sb("negmaxT", [P, 2, P], BF16)
        sel = sb("sel", [P, HEADS // 2, 2, S], BF16)
        e32 = sb("e32", [P, 2, 2, 4, S])
        e_hi = sb("e_hi", [P, 2, 2, 2, 4, S], F16)
        e_lo = sb("e_lo", [P, 2, 2, 2, 4, S], F16)
        rden = sb("rden", [P, 2, 8])
        attn = sb("attn", [P, 2, NB, 2 * QUADS, HD])
        attnT = sb("attnT", [64, 2, NB, S])
        stats2 = sb("stats2", [P, 2, 6])
        mv2 = sb("mv2", [P, 2, 2])
        w2var = sb("w2var", [P, 2])
        rstd2 = sb("rstd2", [P, 2])
        negmean2 = sb("negmean2", [P, 2])
        nmr2 = sb("nmr2", [P, 2])
        rows = sb("rows", [P, 2, 2, ROW])
        hT32 = sb("hT32", [P, CH])
        top = sb("top", [P, 2])
        shifted = sb("shifted", [P, 2, EXPERTS])
        is_top = sb("is_top", [P, 2, EXPERTS])
        first = sb("first", [P, 2])
        onehot = sb("onehot", [P, 2, EXPERTS])
        onehot_b = sb("onehot_b", [P, 2, EXPERTS], BF16)
        expo = sb("expo", [P, 2, EXPERTS])
        expsum = sb("expsum", [P, 2])
        seen = sb("seen", [P, EXPERTS], BF16)
        seen2 = sb("seen2", [P, EXPERTS], BF16)
        pos8 = sb("pos8", [P, 2, EXPERTS])
        pos8m = sb("pos8m", [P, 2, EXPERTS])
        dest = sb("dest", [P, 2, 2], I32)
        token_no = sb("token_no", [P, 2])
        before = sb("before", [P, P], BF16)
        ones_b = sb("ones_b", [P, P], BF16)
        rank8 = sb("rank8", [P, EXPERTS])
        region8 = sb("region8", [P, EXPERTS])
        iota8 = sb("iota8", [P, EXPERTS])
        thr = sb("thr", [P, EXPERTS, NT])
        tri8 = sb("tri8", [P, EXPERTS, EXPERTS])
        slot_no = sb("slot_no", [P, SLOTS])
        part_no = sb("part_no", [P, 1])
        cnt = sb("cnt", [P, EXPERTS])
        over = sb("over", [P, EXPERTS, NT])
        tiles8 = sb("tiles8", [P, EXPERTS])
        prod8 = sb("prod8", [P, EXPERTS, EXPERTS])
        upto8 = sb("upto8", [P, EXPERTS])
        start8 = sb("start8", [P, EXPERTS])
        sl_ge = sb("sl_ge", [P, SLOTS, EXPERTS])
        sl_e = sb("sl_e", [P, SLOTS])
        sl_oh = sb("sl_oh", [P, SLOTS, EXPERTS])
        sl_m = sb("sl_m", [P, SLOTS, EXPERTS])
        sl_m2 = sb("sl_m2", [P, SLOTS, EXPERTS])
        sl_start = sb("sl_start", [P, SLOTS])
        sl_n = sb("sl_n", [P, SLOTS])
        sl_j = sb("sl_j", [P, SLOTS])
        sl_last = sb("sl_last", [P, SLOTS])
        sl_off = sb("sl_off", [P, SLOTS])
        sl_row = sb("sl_row", [P, SLOTS])
        sl_v1 = sb("sl_v1", [P, SLOTS])
        sl_v2 = sb("sl_v2", [P, SLOTS])
        valid = sb("valid", [P, SLOTS])
        sl_ec = sb("sl_ec", [P, SLOTS])
        sl_base = sb("sl_base", [P, SLOTS])
        tab = sb("tab", [1, 2, SLOTS], I32)
        in_rows = sb("in_rows", [P, ROWBUFS, 2, ROW])
        h32 = sb("h32", [P, 2, CH])
        h_hi = sb("h_hi", [P, 2, CH], F16)
        h_lo = sb("h_lo", [P, 2, CH], F16)
        g32 = sb("g32", [P, 2, 2, 2, CH])
        g_hi = sb("g_hi", [P, 2, 2, 2, CH], F16)
        g_lo = sb("g_lo", [P, 2, 2, 2, CH], F16)
        sh_out = sb("sh_out", [P, 2, 2, D])
        ex_out = sb("ex_out", [P, 2, 2, D])
        o_sum = sb("o_sum", [P, 2, D])
        o_rows = sb("o_rows", [P, 2, 2, D])
        o_idx_f = sb("o_idx_f", [P, 2])
        o_idx = sb("o_idx", [P, 2, 2], I32)

        banks = [stack.enter_context(nc.psum_tensor(f"bank{i}", [P, 512], F32)) for i in range(8)]
        A = banks[0:2]
        ST = banks[2:4]
        AV = banks[4]
        M0, M1, M2 = banks[5:8]
        XT = (banks[0], banks[7])
        F1 = ((banks[1], banks[2]), (banks[3], banks[4]))
        YY = (banks[5], banks[6])

        w_loaded = sem("w_loaded")
        ffn_w_loaded = sem("ffn_w_loaded")
        xc_loaded = [sem("xc_loaded0"), sem("xc_loaded1")]
        res_loaded = [sem("res_loaded0"), sem("res_loaded1")]
        terms_stored = sem("terms_stored")
        terms_loaded = [sem("terms_loaded0"), sem("terms_loaded1")]
        region_cleared = sem("region_cleared")
        scattered = [sem("scattered0"), sem("scattered1")]
        rows_loaded = [sem("rows_loaded0"), sem("rows_loaded1")]
        rows_free = sem("rows_free")
        out_stored = [sem("out_stored0"), sem("out_stored1")]
        consts = sem("consts")
        vconsts = sem("vconsts")
        w_turned = sem("w_turned")
        w_kept = sem("w_kept")
        bv_proj = sem("bv_proj")
        bo_ready = sem("bo_ready")
        signs = sem("signs")
        t_turned = sem("t_turned")
        t_kept = sem("t_kept")
        stats_done = sem("stats_done")
        xn_ready = sem("xn_ready")
        xc_turned = sem("xc_turned")
        xcT_ready = sem("xcT_ready")
        q_proj, k_proj, v_proj = sem("q_proj"), sem("k_proj"), sem("v_proj")
        qk_hi_done = sem("qk_hi_done")
        qk_lo_done = sem("qk_lo_done")
        v_hi_done = sem("v_hi_done")
        v_lo_done = sem("v_lo_done")
        a_done = sem("a_done")
        max_done = sem("max_done")
        negmax_turned = sem("negmax_turned")
        negmaxT_ready = sem("negmaxT_ready")
        st_done = sem("st_done")
        e_hi_done = sem("e_hi_done")
        e32_done = sem("e32_done")
        e_lo_done = [sem("e_lo_done0"), sem("e_lo_done1")]
        av_done = sem("av_done")
        rden_done = sem("rden_done")
        attn_done = sem("attn_done")
        attn_turned = sem("attn_turned")
        attnT_ready = sem("attnT_ready")
        y_done = sem("y_done")
        res_ready = sem("res_ready")
        x2_done = sem("x2_done")
        stats2_done = sem("stats2_done")
        rstd2_done = sem("rstd2_done")
        n2_done = sem("n2_done")
        n2_turned = sem("n2_turned")
        hT_ready = sem("hT_ready")
        logits_done = sem("logits_done")
        shifted_done = sem("shifted_done")
        expo_done = sem("expo_done")
        onehot_done = sem("onehot_done")
        pos_done = sem("pos_done")
        dest_done = sem("dest_done")
        row_done = sem("row_done")
        seen_done = sem("seen_done")
        carried = sem("carried")
        chain = sem("chain")
        st_chain = sem("st_chain")
        st2_chain = sem("st2_chain")
        pick_chain = sem("pick_chain")
        gate_chain = sem("gate_chain")
        place_chain = sem("place_chain")
        h_chain = sem("h_chain")
        o_chain = sem("o_chain")
        pchain = sem("pchain")
        counts_done = sem("counts_done")
        tab_done = sem("tab_done")
        h_turned = sem("h_turned")
        h32_done = sem("h32_done")
        h_done = sem("h_done")
        f1_done = sem("f1_done")
        g32_done = sem("g32_done")
        g_done = sem("g_done")
        f2_done = sem("f2_done")
        parts_done = sem("parts_done")
        sum_done = sem("sum_done")
        o_done = sem("o_done")

        EARLY, LATE = (3, NCH - 5), NCH + 2

        def chunks(eng, body):
            for c in range(EARLY[0]):
                body(c, c % 2, c)
            with eng.Fori(EARLY[0], EARLY[1] - 1, 2) as c:
                body(c, 1, EARLY[0])
                body(c + 1, 0, EARLY[0] + 1)
            for c in range(EARLY[1], LATE):
                body(c, c % 2, c)

        def twos(c, r, shift):
            return (c + (shift + 2 - (r + shift) % 2)) * 8

        def carry_waits(eng):
            eng.sem_inc(carried, 1)

        def v_sums(hp):
            return M1[64 * hp:64 * hp + 64, 0:CH].rearrange("p (bq pp d) -> p bq pp d", pp=2, d=HD)

        def v_part(t, r, hp, lo=0, hi=HD):
            return t[64 * hp:64 * hp + 64, r].rearrange("p b (q hp) pp d -> p hp (b q) pp d", hp=2)[:, hp, :, :, lo:hi]

        def has(j):
            return 0 <= j < NCH

        def steps(eng, body):
            for u in range(4):
                body(u, u % ROWBUFS, u)
            with eng.Fori(4, STEPS - 4 - (ROWBUFS - 1), ROWBUFS) as u:
                for j in range(ROWBUFS):
                    body(u + j, (4 + j) % ROWBUFS, 4 + j)
            for u in range(STEPS - 4, STEPS):
                body(u, u % ROWBUFS, u)

        block = stack.enter_context(nc.Block())
        x_v = x.rearrange("(c t p) d -> c p t d", p=P, t=2)
        c_v = ctx_in.rearrange("(c t p) d -> c p t d", p=P, t=2)

        @block.sync
        def _(sp):
            def load_xc(c, r):
                sp.dma_start(x_in[:, r], x_v[c]).then_inc(xc_loaded[r], 16)
                sp.dma_start(c_in[:, r], c_v[c]).then_inc(xc_loaded[r], 16)

            load_xc(0, 0)
            for i, w in enumerate((Wq, Wk, Wv)):
                sp.dma_start(w_in[:, i, :], w).then_inc(w_loaded, 16)
            for p in range(2):
                sp.dma_start(w_in[:, 3, 64 * p:64 * p + 64].rearrange("o (q r) -> o q r", q=QUADS),
                             Wo.rearrange("o (q p r) -> o p q r", q=QUADS, p=2)[:, p]).then_inc(w_loaded, 16)
            sp.dma_start(rw_in[:, :], rw).then_inc(w_loaded, 16)
            with nc.allow_non_contiguous_dma(reason="512 bytes of biases"):
                for i, b in enumerate((bq, bk)):
                    for m in range(4):
                        sp.dma_start(b_col[32 * m:32 * m + 32, i:i + 1],
                                     b.rearrange("(q m d) -> m d q", m=4, d=HD)[m].unsqueeze(2)).then_inc(w_loaded, 16)
                for q in range(QUADS):
                    sp.dma_start(bv_col[16 * q:16 * q + 16, :],
                                 bv.rearrange("(q p r) -> q r p", q=QUADS, p=2)[q]).then_inc(w_loaded, 16)
                sp.dma_start(ln_col[:, 0:1], gamma.unsqueeze(1)).then_inc(w_loaded, 16)
                sp.dma_start(ln_col[:, 1:2], beta.unsqueeze(1)).then_inc(w_loaded, 16)
            sp.dma_start(bo_row[:, :], bo.unsqueeze(0).to_broadcast([P, D])).then_inc(w_loaded, 16)
            load_xc(1, 1)
            sp.dma_start(w1_in[:, 0], sw1.rearrange("(c f) d -> f c d", f=P)).then_inc(ffn_w_loaded, 16)
            sp.dma_start(w1_in[:, 1:].rearrange("p e c d -> p (e c) d"),
                         ew1.rearrange("e (c f) d -> f (e c) d", f=P)).then_inc(ffn_w_loaded, 16)
            sp.dma_start(w2_in[:, 0], sw2).then_inc(ffn_w_loaded, 16)
            sp.dma_start(w2_in[:, 1:], ew2.rearrange("e d f -> d e f")).then_inc(ffn_w_loaded, 16)
            sp.wait_ge(vconsts, 1)
            for e in range(EXPERTS):
                sp.dma_start(by_expert[e * TOKENS:e * TOKENS + TILE], zeros[:, :]).then_inc(region_cleared, 16)

            def store_terms(c):
                sp.wait_ge(qk_lo_done, (c + 1) * 2)
                for qk in range(2):
                    for t in range(4):
                        part = t % 2 if qk == 0 else t // 2
                        sp.dma_start(qk_dram[c, qk, :, t], qk_hl[:, qk, part, :]).then_inc(terms_stored, 16)

            def load_terms(c, r, used):
                sp.wait_ge(terms_stored, (c + 1) * 128)
                carry_waits(sp)
                if used:
                    sp.wait_ge(st_done, (c - 1) * 4)
                sp.dma_start(q_t[:, r], qk_dram[c, 0].rearrange("m t (d q) n -> (m t d) q n", q=QUADS)).then_inc(terms_loaded[r], 16)
                for m in range(4):
                    sp.dma_start(k_t[32 * m:32 * m + 32, r, :, :, m, :].rearrange("p q b s -> p (q b) s"),
                                 qk_dram[c, 1, m].rearrange("t (d q) (b s) -> (t d) (q b) s", q=QUADS, s=S)).then_inc(terms_loaded[r], 16)

            def load_res(c, r, used):
                if used:
                    sp.wait_ge(x2_done, c - 1)
                sp.dma_start(x_res[:, r], x_v[c]).then_inc(res_loaded[r], 16)

            sp.wait_ge(xc_turned, 1)
            load_xc(2, 0)
            sp.wait_ge(consts, 1)
            store_terms(0)
            load_terms(0, 0, False)
            sp.wait_ge(xc_turned, 2)
            load_xc(3, 1)
            store_terms(1)

            def body(c, r, k):
                if has(k + 1):
                    load_terms(c + 1, 1 - r, k + 1 >= 2)
                if has(k):
                    load_res(c, r, k >= 2)
                if has(k + 2):
                    if has(k + 4):
                        sp.wait_ge(xc_turned, c + 3)
                        load_xc(c + 4, r)
                    store_terms(c + 2)

            chunks(sp, body)

            sp.wait_ge(tab_done, 1)
            sp.wait_ge(scattered[0], NCH * 16)
            sp.wait_ge(scattered[1], NCH * 16)

            def body(u, m, k):
                if k >= 2:
                    sp.wait_ge(h_turned, u - 1)
                    carry_waits(sp)
                sp.wait_ge(rows_free, u + 1)
                carry_waits(sp)
                for i in range(2):
                    row = sp.value_load(tab[0:1, 0, bass.ds(u * 2 + i, 1)], min_val=0, max_val=EXPERTS * TOKENS - TILE)
                    sp.dma_start(in_rows[:, m, i, :], by_expert[bass.ds(row, TILE), :]).then_inc(rows_loaded[m % 2], 16)

            steps(sp, body)
            for r in range(2):
                sp.wait_ge(out_stored[r], STEPS * 16)

        @block.gpsimd
        def _(pool):
            n = [0]

            def then(ins):
                n[0] += 1
                ins.then_inc(pchain, 1)
                pool.wait_ge(pchain, n[0])

            nc.gpsimd.memset(minus_half[:, :], -0.5)
            nc.gpsimd.memset(ones_b[:, :], 1.0)
            nc.gpsimd.memset(before[:, :], 1.0)
            then(nc.gpsimd.memset(ident[:, :], 0.0))
            then(nc.gpsimd.affine_select(out=ident[:, :], in_=ident[:, :], compare_op=ALU.not_equal, fill=1.0,
                                         base=0, pattern=[[-1, P]], channel_multiplier=1))
            nc.gpsimd.tensor_copy(identb[:, :], ident[:, :])
            nc.gpsimd.tensor_copy(identh[:, :], ident[:, :])
            nc.gpsimd.affine_select(out=before[:, :], in_=before[:, :], compare_op=ALU.is_gt, fill=0.0,
                                    base=0, pattern=[[1, P]], channel_multiplier=-1)
            then(nc.gpsimd.memset(sel[:], 0.0))
            then(nc.gpsimd.affine_select(out=sel[:], in_=sel[:], compare_op=ALU.not_equal, fill=1.0, base=0,
                                         pattern=[[-2, HEADS // 2], [-1, 2], [0, S]], channel_multiplier=1))
            iotas = ((rank8[:, :], [[-1, EXPERTS]], EXPERTS, 0), (region8[:, :], [[TOKENS, EXPERTS]], 0, 0),
                     (iota8[:, :], [[1, EXPERTS]], 0, 0), (token_no[:, :], [[TILE, 2]], 0, 1),
                     (thr[:], [[0, EXPERTS], [TILE, NT]], 0, 0), (slot_no[:, :], [[1, SLOTS]], 0, 0),
                     (part_no[:, :], [[0, 1]], 0, 1))
            for o, pat, base, cm in iotas:
                nc.gpsimd.iota(o, pattern=pat, base=base, channel_multiplier=cm, allow_small_or_imprecise_dtypes=True)
            then(nc.gpsimd.memset(tri8[:], 1.0))
            then(nc.gpsimd.affine_select(out=tri8[:], in_=tri8[:], compare_op=ALU.is_ge, fill=0.0, base=0,
                                         pattern=[[1, EXPERTS], [-1, EXPERTS]], channel_multiplier=0))
            nc.gpsimd.memset(k_t[:, 0], 0.0)
            nc.gpsimd.memset(k_t[:, 1], 0.0).then_inc(consts, 1)

            def normalise(c, r, k):
                pool.wait_ge(stats_done, c + 1)
                if k >= 2:
                    pool.wait_ge(xc_turned, c - 1)
                ins = nc.gpsimd.tensor_tensor(rstd[:, r], veps[:, r], minus_half[:, :], ALU.pow)
                ins.then_inc(xn_ready, 1)
                pool.wait_ge(xn_ready, c * 3 + 1)
                carry_waits(pool)
                for i in range(2):
                    nc.gpsimd.tensor_scalar(xn[:, r, i, :], x_in[:, r, i, :], mv[:, r, i, 0:1], rstd[:, r, i:i + 1],
                                            ALU.subtract, ALU.mult).then_inc(xn_ready, 1)

            for c in range(3):
                normalise(c, c % 2, c)
            pool.wait_ge(bo_ready, 1)
            pool.wait_ge(region_cleared, EXPERTS * 16)

            def e_low(T, i, k):
                pool.wait_ge(e32_done, T * 2 + 2)
                if k >= 2:
                    pool.wait_ge(av_done, T - 1)
                hi, lo = (t[:, i, 1].rearrange("p a b c -> p (a b c)") for t in (e_hi, e_lo))
                nc.gpsimd.tensor_tensor(lo, e32[:, 1].rearrange("p a b c -> p (a b c)"), hi,
                                        ALU.subtract).then_inc(e_lo_done[1], 1)

            def body(c, r, k):
                if has(k):
                    e_low(c * 2, 0, 2 * k)
                if has(k + 3):
                    normalise(c + 3, 1 - r, k + 3)
                if has(k - 1):
                    pool.wait_ge(res_loaded[1 - r], twos(c, r, -1))
                    nc.gpsimd.tensor_tensor(x_res[:, 1 - r], x_res[:, 1 - r], b_row[:, :].unsqueeze(1).to_broadcast([P, 2, D]),
                                            ALU.add).then_inc(res_ready, 1)
                if has(k):
                    e_low(c * 2 + 1, 1, 2 * k + 1)
                if has(k - 1):
                    pool.wait_ge(stats2_done, c)
                    if k >= 2:
                        pool.wait_ge(n2_done, (c - 1) * 2)
                    nc.gpsimd.tensor_tensor(rstd2[:, :], w2var[:, :], minus_half[:, :], ALU.pow).then_inc(rstd2_done, 1)
                    pool.wait_ge(rstd2_done, c * 2 - 1)
                    nc.gpsimd.tensor_tensor(nmr2[:, :], negmean2[:, :], rstd2[:, :], ALU.mult).then_inc(rstd2_done, 1)
                if has(k - 2):
                    pool.wait_ge(dest_done, c - 1)
                    pool.wait_ge(row_done, c - 1)
                    carry_waits(pool)
                    for i in range(2):
                        nc.gpsimd.indirect_dma_start(by_expert, bass.IndirectOffsetOnAxis(ap=dest[:, r, i:i + 1], axis=0),
                                                     rows[:, r, i, :], None).then_inc(scattered[r], 16)

            chunks(pool, body)

            def add_and_store(u, m, k):
                r = m % 2
                pool.wait_ge(parts_done, u + 1)
                if k >= 1:
                    pool.wait_ge(o_done, u)
                nc.gpsimd.tensor_tensor(o_sum[:], sh_out[:, r], ex_out[:, r], ALU.add).then_inc(sum_done, 1)
                pool.wait_ge(sum_done, u + 1)
                if k >= 2:
                    pool.wait_ge(out_stored[r], twos(u, r, -2) * 2)
                nc.gpsimd.tensor_tensor(o_rows[:, r], o_sum[:], in_rows[:, m, :, D:2 * D], ALU.add).then_inc(o_done, 1)
                pool.wait_ge(o_done, u + 1)
                pool.sem_inc(rows_free, 1)
                for i in range(2):
                    nc.gpsimd.indirect_dma_start(out, bass.IndirectOffsetOnAxis(ap=o_idx[:, r, i:i + 1], axis=0),
                                                 o_rows[:, r, i, :], None, bounds_check=TOKENS - 1,
                                                 oob_is_err=False).then_inc(out_stored[r], 16)

            pool.sem_inc(rows_free, ROWBUFS)
            steps(pool, add_and_store)

        @block.tensor
        def _(pe):
            mm, tr = nc.tensor.matmul, nc.tensor.transpose

            pe.wait_ge(w_loaded, W_LOADS * 16)
            pe.wait_ge(consts, 1)
            for i in range(3):
                tr(A[0][:, i * P:(i + 1) * P], w_in[:, i, :], ident[:, :])
            tr(A[0][:, 3 * P:3 * P + EXPERTS], rw_in[:, :], ident[0:EXPERTS, 0:EXPERTS])
            for p in range(2):
                last = tr(A[1][0:64, p * P:(p + 1) * P], w_in[:, 3, 64 * p:64 * p + 64], ident[:, :])
            last.then_inc(w_turned, 1)

            def turn_xc(c, r, k):
                pe.wait_ge(xn_ready, (c + 1) * 3)
                pe.wait_ge(xc_loaded[r], twos(c, r, 0) * 2)
                if k >= 4:
                    pe.wait_ge(x2_done, c - 3)
                for i in range(2):
                    tr(M0[:, i * P:(i + 1) * P], xn[:, r, i, :], ident[:, :])
                for i in range(2):
                    last = tr(M0[:, (2 + i) * P:(3 + i) * P], c_in[:, r, i, :], ident[:, :])
                last.then_inc(xc_turned, 1)

            def proj_q(c, r):
                pe.wait_ge(xcT_ready, c + 1)
                mm(M0[:, 0:CH], wT[:, 0, :], xcT[:, r, 0:2, :], start=True, stop=True).then_inc(q_proj, 1)

            def proj_k(c, r, before_it):
                before_it()
                mm(M1[:, 0:CH], wT[:, 1, :], xcT[:, r, 2:4, :], start=True, stop=True).then_inc(k_proj, 1)

            def proj_v(c, r, before_it):
                before_it()
                for b in range(NB):
                    src = xcT[:, r, 2 + b // 2, (b % 2) * S:(b % 2 + 1) * S]
                    for hp in range(2):
                        last = mm(M1[64 * hp:64 * hp + 64, b * 64:(b + 1) * 64], src, wT[:, 2, 64 * hp:64 * hp + 64], start=True, stop=True,
                                  skip_group_check=True)
                last.then_inc(v_proj, 1)

            def scores_a(T, r, i, k):
                if i == 0:
                    pe.wait_ge(terms_loaded[r], k)
                for hh in range(2):
                    if T is not None:
                        pe.wait_ge(max_done, T * 2 - 1 + hh)
                    for b in range(2):
                        for q in (2 * hh, 2 * hh + 1):
                            t0 = i * TILE + b * S
                            last = mm(A[hh][b * S:(b + 1) * S, (q % 2) * 256:(q % 2 + 1) * 256],
                                      q_t[:, r, q, t0:t0 + S], k_t[:, r, q, 2 * i + b].rearrange("p m s -> p (m s)"), start=True, stop=True,
                                      skip_group_check=True)
                    last.then_inc(a_done, 1)

            def turn_negmax(T, i, before_it):
                pe.wait_ge(max_done, T * 2 + 2)
                before_it()
                tr(M2[:, :].bitcast(BF16)[:, 0:P], negmax[:, i, :], identb[:, :]).then_inc(negmax_turned, 1)

            def scores_st(T, r, i, k):
                pe.wait_ge(negmaxT_ready, T + 1)
                for hh in range(2):
                    if k >= 1:
                        pe.wait_ge(e32_done, T * 2 - 1 + hh)
                    for pr in range(4):
                        pair = 4 * hh + pr
                        q, m = pair // 2, (pair % 2) * 2
                        mm(ST[hh][:, pr * 128:(pr + 1) * 128], sel[:, pair].rearrange("p a b -> p (a b)"), negmaxT[:, i, :],
                           start=True, stop=False, skip_group_check=True)
                        for b in range(2):
                            t0 = i * TILE + b * S
                            last = mm(ST[hh][:, pr * 128 + b * S:pr * 128 + (b + 1) * S],
                                      k_t[:, r, q, 2 * i + b, m:m + 2, :].rearrange("p m s -> p (m s)"), q_t[:, r, q, t0:t0 + S],
                                      start=False, stop=True, skip_group_check=True)
                    last.then_inc(st_done, 1)

            def attend(T, r, i, k):
                for hh in range(2):
                    pe.wait_ge(e_lo_done[hh], T + 1)
                if k >= 1:
                    pe.wait_ge(attn_done, T * 2)
                for b in range(2):
                    for q in range(QUADS):
                        o = AV[:, b * 256 + q * 4 * VW:b * 256 + (q + 1) * 4 * VW]
                        pr = (q % 2) * 2
                        for n, (e, v) in enumerate(((e_hi, v_hi), (e_lo, v_hi), (e_hi, v_lo), (e_lo, v_lo))):
                            last = mm(o, e[:, i, q // 2, b, pr:pr + 2, :].rearrange("p a b -> p (a b)"),
                                      v[:, r, 2 * i + b, 2 * q:2 * q + 2].rearrange("p a b c -> p (a b c)"),
                                      start=(n == 0), stop=(n == 3))
                last.then_inc(av_done, 1)

            def turn_attn(c, r, before_it):
                pe.wait_ge(attn_done, (c + 1) * 4)
                before_it()
                carry_waits(pe)
                for b in range(NB):
                    last = tr(M1[0:64, b * P:(b + 1) * P], attn[:, r, b].rearrange("p a b -> p (a b)"), ident[:, :])
                last.then_inc(attn_turned, 1)

            def proj_o(c, before_it):
                pe.wait_ge(attnT_ready, c + 1)
                before_it()
                for i in range(2):
                    for p in range(2):
                        last = mm(M0[:, i * P:(i + 1) * P], attnT[:, p, 2 * i:2 * i + 2, :].rearrange("p a b -> p (a b)"), woT[:, p, :],
                                  start=(p == 0), stop=(p == 1))
                last.then_inc(y_done, 1)

            def turn_n2(c, r, before_it):
                pe.wait_ge(n2_done, (c + 1) * 2)
                before_it()
                for i in range(2):
                    last = tr(M1[:, i * P:(i + 1) * P], rows[:, r, i, 0:D], ident[:, :])
                last.then_inc(n2_turned, 1)

            def route(c, before_it):
                pe.wait_ge(hT_ready, c + 1)
                before_it()
                for i in range(2):
                    last = mm(M2[:, i * EXPERTS:(i + 1) * EXPERTS], hT32[:, i * TILE:(i + 1) * TILE], rwT[:, :],
                              start=True, stop=True)
                last.then_inc(logits_done, 1)

            def count(c, k, before_it):
                pe.wait_ge(onehot_done, c + 1)
                if k >= 3:
                    pe.wait_ge(seen_done, c)
                before_it()
                mm(M2[:, 0:EXPERTS], before[:, :], onehot_b[:, 0, :], start=True, stop=False)
                mm(M2[:, 0:EXPERTS], ones_b[:, :], seen[:, :], start=False, stop=True)
                mm(M2[:, EXPERTS:2 * EXPERTS], before[:, :], onehot_b[:, 1, :], start=True, stop=False)
                mm(M2[:, EXPERTS:2 * EXPERTS], ones_b[:, :], onehot_b[:, 0, :], start=False, stop=False)
                mm(M2[:, EXPERTS:2 * EXPERTS], ones_b[:, :], seen[:, :], start=False, stop=True).then_inc(pos_done, 1)

            nothing = lambda: None
            pe.wait_ge(w_kept, 1)
            for p in range(2):
                last = mm(M2[:, 0:D], bv_col[:, p:p + 1].to_broadcast([64, P]), woT[:, p, :], start=(p == 0), stop=(p == 1))
            last.then_inc(bv_proj, 1)
            for c in range(2):
                if c == 1:
                    pe.wait_ge(qk_lo_done, 1)
                turn_xc(c, c, c)
                proj_q(c, c)
                proj_k(c, c, (lambda: pe.wait_ge(qk_lo_done, 2)) if c else nothing)
            proj_v(0, 0, lambda: pe.wait_ge(qk_lo_done, 4))
            pe.wait_ge(bo_ready, 1)
            scores_a(None, 0, 0, 80)
            turn_negmax(0, 0, nothing)

            def body(c, r, k):
                if has(k):
                    scores_st(c * 2, r, 0, k)
                    scores_a(c * 2 + 1, r, 1, None)
                if has(k + 2):
                    if k < 2:
                        pe.wait_ge(qk_lo_done, (c + 2) * 2 - 1)
                    turn_xc(c + 2, r, k + 2)
                if has(k):
                    turn_negmax(c * 2 + 1, 1, lambda: pe.wait_ge(dest_done, c - 2) if has(k - 3)
                                else pe.wait_ge(negmaxT_ready, c * 2 + 1))
                if has(k - 2):
                    turn_n2(c - 2, r, lambda: pe.wait_ge(attnT_ready, c - 1))
                if has(k + 2):
                    proj_q(c + 2, r)
                if has(k - 1):
                    attend(c * 2 - 1, 1 - r, 1, k - 1 + 1)
                if has(k + 2):
                    proj_k(c + 2, r, lambda: pe.wait_ge(hT_ready, c - 1) if has(k - 2)
                           else pe.wait_ge(attnT_ready, c - 1) if k == 2
                           else pe.wait_ge(v_lo_done, (c + 1) * 2))
                if has(k):
                    scores_st(c * 2 + 1, r, 1, k + 1)
                if has(k - 2):
                    route(c - 2, lambda: pe.wait_ge(negmaxT_ready, c * 2 + 2) if has(k)
                          else pe.wait_ge(dest_done, c - 2))
                if has(k + 1):
                    proj_v(c + 1, 1 - r, lambda: pe.wait_ge(qk_lo_done, (c + 3) * 2) if has(k + 2)
                           else pe.wait_ge(hT_ready, c - 1))
                if has(k + 1):
                    scores_a(c * 2 + 2, 1 - r, 0, twos(c, r, 1) * 5)
                if has(k):
                    attend(c * 2, r, 0, k)
                if has(k - 1):
                    turn_attn(c - 1, 1 - r, lambda: pe.wait_ge(v_lo_done, (c + 2) * 2) if has(k + 1)
                              else pe.wait_ge(hT_ready, c - 1))
                if has(k + 1):
                    turn_negmax(c * 2 + 2, 0, lambda: pe.wait_ge(shifted_done, c - 1) if has(k - 2)
                                else pe.wait_ge(negmaxT_ready, c * 2 + 2))
                if has(k - 1):
                    proj_o(c - 1, lambda: pe.wait_ge(qk_lo_done, (c + 3) * 2 - 1) if has(k + 2)
                           else pe.wait_ge(x2_done, c - 1))
                if has(k - 2):
                    count(c - 2, k, lambda: pe.wait_ge(negmaxT_ready, c * 2 + 3) if has(k + 1)
                          else pe.wait_ge(shifted_done, c - 1))

            chunks(pe, body)

            pe.wait_ge(seen_done, NCH)
            pe.wait_ge(dest_done, NCH)
            mm(M2[:, 0:EXPERTS], ones_b[:, :], seen[:, :], start=True, stop=True).then_inc(counts_done, 1)

            pe.wait_ge(signs, 1)
            pe.wait_ge(max_done, NT * 2)
            pe.wait_ge(e32_done, NT * 2)
            pe.wait_ge(attn_done, NT * 2)
            places = [A[0], A[1], ST[0], ST[1], AV]
            for n in range(4 * BLOCKS):
                e, c = (n % (2 * BLOCKS)) // 2, n % 2
                src = sign1[:, e, c, :] if n < 2 * BLOCKS else sign2[:, e, c * P:(c + 1) * P]
                last = tr(places[n // 8][:, :].bitcast(F16)[:, (n % 8) * P:(n % 8 + 1) * P], src, identh[:, :])
                if n % 8 == 7 or n == 4 * BLOCKS - 1:
                    last.then_inc(t_turned, 1)
            pe.wait_ge(t_kept, 3)
            for e in range(BLOCKS):
                last = mm(places[e // 4][:, (e % 4) * D:(e % 4 + 1) * D], s2[:, e:e + 1].to_broadcast([P, P]), ident[:, :],
                          start=True, stop=True, skip_group_check=True)
            last.then_inc(t_turned, 1)
            pe.wait_ge(t_kept, 6)

            def experts_of(u):
                return [pe.value_load(tab[0:1, 1, bass.ds(u * 2 + i, 1)], min_val=0, max_val=EXPERTS - 1) for i in range(2)]

            def turn_h(u, m, k):
                r = m % 2
                pe.wait_ge(rows_loaded[m % 2], twos(u, m % 2, 0) * 2)
                if k >= 2:
                    pe.wait_ge(h32_done, u - 1)
                for i in range(2):
                    last = tr(XT[r][:, i * TILE:(i + 1) * TILE], in_rows[:, m, i, 0:D], ident[:, :])
                last.then_inc(h_turned, 1)

            def layer1(u, r, k, experts):
                pe.wait_ge(h_done, u + 1)
                if k >= 2:
                    pe.wait_ge(g32_done, u - 1)
                for c in range(2):
                    for n, h in enumerate((h_hi, h_lo)):
                        mm(F1[r][0][:, c * CH:(c + 1) * CH], t1[:, 0, c, :], h[:, r, :], start=(n == 0), stop=(n == 1))
                for i, e in enumerate(experts):
                    for c in range(2):
                        for n, h in enumerate((h_hi, h_lo)):
                            last = mm(F1[r][1][:, c * CH + i * TILE:c * CH + (i + 1) * TILE],
                                      t1[:, bass.ds(e + 1, 1), c, :].rearrange("p a b -> p (a b)"),
                                      h[:, r, i * TILE:(i + 1) * TILE], start=(n == 0), stop=(n == 1))
                last.then_inc(f1_done, 1)

            def layer2(u, r, k, experts):
                pe.wait_ge(g_done, u + 1)
                if k >= 2:
                    pe.wait_ge(parts_done, u - 1)
                for i, e in enumerate(experts):
                    for w in range(2):
                        o = YY[r][:, (2 * w + i) * D:(2 * w + i + 1) * D]
                        for n in range(4):
                            c, g = n // 2, (g_hi, g_lo)[n % 2]
                            wt = t2[:, 0, c, :] if w == 0 else t2[:, bass.ds(e + 1, 1), c, :].rearrange("p a b -> p (a b)")
                            last = mm(o, g[:, r, w, c, i * TILE:(i + 1) * TILE], wt, start=(n == 0), stop=(n == 3))
                last.then_inc(f2_done, 1)

            def body(u, m, k):
                r = m % 2
                now = experts_of(u)
                last = experts_of(u - 1) if k >= 1 else None
                if k + 1 < STEPS:
                    turn_h(u + 1, (m + 1) % ROWBUFS, k + 1)
                layer1(u, r, k, now)
                if k >= 1:
                    layer2(u - 1, 1 - r, k - 1, last)

            pe.wait_ge(tab_done, 1)
            turn_h(0, 0, 0)
            steps(pe, body)
            layer2(STEPS - 1, 1, STEPS - 1, experts_of(STEPS - 1))

        @block.scalar
        def _(act):
            fn = nc.scalar.activation

            act.wait_ge(w_turned, 1)
            for i in range(2):
                fn(wT[:, i, :].rearrange("p (m d q) -> p m d q", m=4, d=HD),
                   A[0][:, i * P:(i + 1) * P].rearrange("p (q m d) -> p m d q", q=QUADS, m=4), ACT.Copy)
            fn(wT[:, 2, :].rearrange("p (hp q pp d) -> p hp q pp d", hp=2, q=QUADS, pp=2)[:, 0],
               A[0][:, 2 * P:3 * P].rearrange("p (q pp hp d) -> p hp q pp d", q=QUADS, pp=2, hp=2)[:, 0], ACT.Copy)
            fn(wT[:, 2, :].rearrange("p (hp q pp d) -> p hp q pp d", hp=2, q=QUADS, pp=2)[:, 1],
               A[0][:, 2 * P:3 * P].rearrange("p (q pp hp d) -> p hp q pp d", q=QUADS, pp=2, hp=2)[:, 1], ACT.Copy)
            fn(rwT[:, :], A[0][:, 3 * P:3 * P + EXPERTS], ACT.Copy)
            fn(woT[:, :, :], A[1][0:64, 0:2 * P].rearrange("p (a b) -> p a b", a=2), ACT.Copy).then_inc(w_kept, 1)

            def keep_xcT(c, r, k):
                act.wait_ge(xc_turned, c + 1)
                if k >= 2:
                    act.wait_ge(v_proj, c - 1)
                fn(xcT[:, r], M0[:, 0:512].rearrange("p (a b) -> p a b", a=4), ACT.Copy).then_inc(xcT_ready, 1)

            def q_hi(c, k):
                act.wait_ge(q_proj, c + 1)
                if k >= 1:
                    act.wait_ge(terms_stored, c * 128)
                fn(qk_hl[:, 0, 0, :], M0[:, 0:CH], ACT.Identity, bias=b_col[:, 0:1]).then_inc(qk_hi_done, 1)

            def k_hi(c):
                act.wait_ge(k_proj, c + 1)
                fn(qk_hl[:, 1, 0, :], M1[:, 0:CH], ACT.Identity, bias=b_col[:, 1:2]).then_inc(qk_hi_done, 1)

            def keep_v_hi(c, r, k):
                act.wait_ge(v_proj, c + 1)
                if k >= 2:
                    act.wait_ge(av_done, (c - 1) * 2)
                for hp in range(2):
                    fn(v_part(v_hi, r, hp), v_sums(hp), ACT.Copy).then_inc(v_hi_done, 1)

            def keep_negmaxT(T, i, k):
                act.wait_ge(negmax_turned, T + 1)
                if k >= 1:
                    act.wait_ge(st_done, (T - 1) * 2)
                fn(negmaxT[:, i, :], M2[:, :].bitcast(BF16)[:, 0:P], ACT.Copy).then_inc(negmaxT_ready, 1)

            def exponentials(T, i, k, hh):
                act.wait_ge(st_done, T * 2 + 1 + hh)
                if k >= 2:
                    act.wait_ge(av_done, T - 1)
                src = ST[hh][:, :].rearrange("p (a b c) -> p a b c", a=4, b=2)
                fn(e_hi[:, i, hh].rearrange("p b a c -> p a b c"), src, ACT.Exp, bias=lne_col, scale=SCALE).then_inc(e_hi_done, 1)
                if k >= 1:
                    act.wait_ge(e_lo_done[hh], T)
                fn(e32[:, hh].rearrange("p b a c -> p a b c"), src, ACT.Exp, bias=lne_col, scale=SCALE).then_inc(e32_done, 1)

            def keep_attnT(c):
                act.wait_ge(attn_turned, c + 1)
                fn(attnT[:].rearrange("p a b c -> p b a c"), M1[0:64, :].rearrange("p (b a c) -> p b a c", b=NB, a=2), ACT.Copy).then_inc(attnT_ready, 1)

            def keep_hT(c):
                act.wait_ge(n2_turned, c + 1)
                fn(hT32[:, :], M1[:, 0:CH], ACT.Identity, bias=ln_col[:, 1:2], scale=ln_col[:, 0:1]).then_inc(hT_ready, 1)

            def normalise2(c, r):
                act.wait_ge(rstd2_done, (c + 1) * 2)
                for i in range(2):
                    fn(rows[:, r, i, 0:D], rows[:, r, i, D:2 * D], ACT.Identity, bias=nmr2[:, i:i + 1],
                       scale=rstd2[:, i:i + 1]).then_inc(n2_done, 1)

            lne_col = lne[:, 0:1]
            act.wait_ge(vconsts, 2)
            for c in range(2):
                keep_xcT(c, c, c)
                q_hi(c, c)
                k_hi(c)
            keep_v_hi(0, 0, 0)
            keep_negmaxT(0, 0, 0)

            def body(c, r, k):
                if has(k):
                    exponentials(c * 2, 0, 2 * k, 0)
                if has(k - 2):
                    normalise2(c - 2, r)
                if has(k + 2):
                    keep_xcT(c + 2, r, k + 2)
                if has(k):
                    keep_negmaxT(c * 2 + 1, 1, k)
                    exponentials(c * 2, 0, 2 * k, 1)
                if has(k + 2):
                    q_hi(c + 2, k + 2)
                if has(k - 2):
                    keep_hT(c - 2)
                if has(k + 2):
                    k_hi(c + 2)
                if has(k):
                    exponentials(c * 2 + 1, 1, 2 * k + 1, 0)
                if has(k + 1):
                    keep_v_hi(c + 1, 1 - r, k + 1)
                if has(k):
                    exponentials(c * 2 + 1, 1, 2 * k + 1, 1)
                if has(k - 2):
                    act.wait_ge(shifted_done, c - 1)
                    fn(expo[:], shifted[:], ACT.Exp).then_inc(expo_done, 1)
                if has(k - 1):
                    keep_attnT(c - 1)
                if has(k + 1):
                    keep_negmaxT(c * 2 + 2, 0, k + 1)

            chunks(act, body)

            flat = [t1[:].rearrange("p e c f -> p (e c) f"), t2[:].rearrange("p e c f -> p (e c) f")]
            places = [A[0], A[1], ST[0], ST[1], AV]
            for g in range(5):
                act.wait_ge(t_turned, g + 1)
                src = places[g][:, :].bitcast(F16).rearrange("p (a b) -> p a b", a=8)
                lo, hi = 8 * g, min(8 * g + 8, 4 * BLOCKS)
                edge = min(max(2 * BLOCKS, lo), hi)
                last = None
                for t, (a, b) in enumerate(((lo, edge), (edge, hi))):
                    if b > a:
                        last = fn(flat[t][:, a - t * 2 * BLOCKS:b - t * 2 * BLOCKS, :], src[:, a - lo:b - lo, :], ACT.Copy)
                last.then_inc(t_kept, 1)
            act.wait_ge(t_turned, 6)
            for g in range(3):
                a, b = 4 * g, min(4 * g + 4, BLOCKS)
                last = fn(s2_row[:, a:b, :], places[g][:, 0:(b - a) * D].rearrange("p (a b) -> p a b", b=D), ACT.Copy)
            last.then_inc(t_kept, 1)

            def keep_h(u, r, k):
                act.wait_ge(h_turned, u + 1)
                if k >= 2:
                    act.wait_ge(h_done, u - 1)
                fn(h32[:, r, :], XT[r][:, 0:CH], ACT.Identity, bias=ln_col[:, 1:2], scale=ln_col[:, 0:1]).then_inc(h32_done, 1)

            def silus(u, r, k, experts):
                act.wait_ge(f1_done, u + 1)
                if k >= 2:
                    act.wait_ge(g_done, u - 1)
                    act.wait_ge(f2_done, u - 1)
                for to in (g_hi, g32):
                    for c in range(2):
                        fn(to[:, r, 0, c, :], F1[r][0][:, c * CH:(c + 1) * CH], ACT.Silu, scale=s1[:, c:c + 1])
                    for i, e in enumerate(experts):
                        for c in range(2):
                            last = fn(to[:, r, 1, c, i * TILE:(i + 1) * TILE], F1[r][1][:, c * CH + i * TILE:c * CH + (i + 1) * TILE],
                                      ACT.Silu, scale=s1[:, bass.ds(e * 2 + (2 + c), 1)])
                last.then_inc(g32_done, 1)

            def body(u, m, k):
                r = m % 2
                experts = [act.value_load(tab[0:1, 1, bass.ds(u * 2 + i, 1)], min_val=0, max_val=EXPERTS - 1) for i in range(2)]
                if k + 1 < STEPS:
                    keep_h(u + 1, 1 - r, k + 1)
                silus(u, r, k, experts)

            act.wait_ge(tab_done, 1)
            keep_h(0, 0, 0)
            steps(act, body)

        @block.vector
        def _(dve):
            n = [0]
            v = nc.vector

            def then(ins):
                n[0] += 1
                ins.then_inc(chain, 1)
                dve.wait_ge(chain, n[0])

            v.memset(zeros[:, :], 0.0).then_inc(vconsts, 1)
            v.memset(lne[:, :], LNE)
            v.memset(rows[:, :, :, 2 * D:ROW], 0.0)
            v.memset(seen[:, :], 0.0)
            v.memset(negmax[:], 0.0)
            then(v.memset(v_hi[:], 0.0))
            v.memset(v_lo[:], 0.0)
            for hp in range(2):
                for r in range(2):
                    v.memset(v_part(v_hi, r, hp, HD, VW), 1.0)
            then(v.memset(s1h[:, :], 0.0))
            v.engine_nop().then_inc(vconsts, 1)

            def x_moments(c, r, k):
                dve.wait_ge(xc_loaded[r], twos(c, r, 0) * 2)
                for i in range(2):
                    v.bn_stats(stats[:, i, :], x_in[:, r, i, :]).then_inc(st_chain, 1)

            def x_aggregate(c, r, k):
                if k >= 2:
                    dve.wait_ge(xn_ready, (c - 1) * 3)
                for i in range(2):
                    dve.wait_ge(st_chain, c * 4 + 1 + i)
                    carry_waits(dve)
                    v.bn_aggr(mv[:, r, i, :], stats[:, i, :]).then_inc(st_chain, 1)

            def x_eps(c, r):
                dve.wait_ge(st_chain, c * 4 + 4)
                v.tensor_scalar(veps[:, r], mv[:, r, :, 1], LN_EPS, None, ALU.add).then_inc(stats_done, 1)

            def x_stats(c, r, k):
                x_moments(c, r, k)
                x_aggregate(c, r, k)
                x_eps(c, r)

            def qk_lo(c):
                for i, bank in enumerate((M0, M1)):
                    dve.wait_ge(qk_hi_done, c * 2 + 1 + i)
                    v.scalar_tensor_tensor(qk_hl[:, i, 1, :], bank[:, 0:CH], b_col[:, i:i + 1], qk_hl[:, i, 0, :],
                                           ALU.add, ALU.subtract).then_inc(qk_lo_done, 1)

            def v_low(c, r, hp):
                dve.wait_ge(v_hi_done, c * 2 + 1 + hp)
                v.tensor_tensor(v_part(v_lo, r, hp), v_sums(hp), v_part(v_hi, r, hp), ALU.subtract).then_inc(v_lo_done, 1)

            def maxima(T, i, k, hh):
                dve.wait_ge(a_done, T * 2 + 1 + hh)
                if k >= 1:
                    dve.wait_ge(negmax_turned, T - 1)
                v.tensor_reduce(negmax[:, i, 8 * hh:8 * hh + 8], A[hh][:, :].rearrange("p (a b) -> p a b", b=S),
                                X, ALU.max, negate=True).then_inc(max_done, 1)

            def e_low(T, i, k):
                dve.wait_ge(e32_done, T * 2 + 1)
                if k >= 2:
                    dve.wait_ge(av_done, T - 1)
                hi, lo = (t[:, i, 0].rearrange("p a b c -> p (a b c)") for t in (e_hi, e_lo))
                v.tensor_tensor(lo, e32[:, 0].rearrange("p a b c -> p (a b c)"), hi, ALU.subtract).then_inc(e_lo_done[0], 1)

            av = AV[:, :].rearrange("p (b x) -> p b x", b=2)[:, :, 0:16 * VW].rearrange("p b (h pp d) -> p b h pp d", pp=2, d=VW)

            def denominators(T):
                dve.wait_ge(av_done, T + 1)
                for pp in range(2):
                    ps = slice(64 * pp, 64 * pp + 64)
                    v.reciprocal(rden[ps], av[ps, :, :, pp, HD]).then_inc(rden_done, 1)

            def divide(T, r, i):
                for pp in range(2):
                    ps = slice(64 * pp, 64 * pp + 64)
                    dve.wait_ge(rden_done, T * 2 + 1 + pp)
                    v.tensor_tensor(attn[ps, r, 2 * i:2 * i + 2], av[ps, :, :, pp, 0:HD],
                                    rden[ps].unsqueeze(3).to_broadcast([64, 2, 8, HD]), ALU.mult).then_inc(attn_done, 1)

            def residual(c, r, k):
                dve.wait_ge(y_done, c + 1)
                dve.wait_ge(res_ready, c + 1)
                if k >= 2:
                    dve.wait_ge(scattered[r], twos(c, r, -2) * 2)
                v.tensor_tensor(rows[:, r, :, D:2 * D], M0[:, 0:CH].rearrange("p (a b) -> p a b", a=2), x_res[:, r],
                                ALU.add).then_inc(x2_done, 1)

            def moments2(c, r):
                dve.wait_ge(x2_done, c + 1)
                for i in range(2):
                    v.bn_stats(stats2[:, i, :], rows[:, r, i, D:2 * D]).then_inc(st2_chain, 1)

            def aggregate2(c, k):
                if k >= 1:
                    dve.wait_ge(rstd2_done, c * 2)
                for i in range(2):
                    dve.wait_ge(st2_chain, c * 4 + 1 + i)
                    carry_waits(dve)
                    v.bn_aggr(mv2[:, i, :], stats2[:, i, :]).then_inc(st2_chain, 1)

            def variance2(c):
                dve.wait_ge(st2_chain, c * 4 + 4)
                v.tensor_scalar(negmean2[:, :], mv2[:, :, 0], -1.0, None, ALU.mult)
                v.tensor_scalar(w2var[:, :], mv2[:, :, 1], 1.0 + LN_EPS, LN_EPS * LN_EPS, ALU.mult, ALU.add).then_inc(stats2_done, 1)

            lg = M2[:, 0:2 * EXPERTS].rearrange("p (a b) -> p a b", a=2)
            wide = lambda a: a.unsqueeze(2).to_broadcast([P, 2, EXPERTS])

            def pick_top(c):
                dve.wait_ge(logits_done, c + 1)
                v.tensor_reduce(top[:, :], lg, X, ALU.max).then_inc(pick_chain, 1)

            def pick_shift(c, k):
                dve.wait_ge(pick_chain, c * 4 + 1)
                if k >= 1:
                    dve.wait_ge(expo_done, c)
                v.tensor_tensor(shifted[:], lg, wide(top[:, :]), ALU.subtract).then_inc(shifted_done, 1)

            def pick_rank(c):
                dve.wait_ge(shifted_done, c + 1)
                v.scalar_tensor_tensor(is_top[:], shifted[:], 0.0, rank8[:, :].unsqueeze(1).to_broadcast([P, 2, EXPERTS]),
                                       ALU.is_equal, ALU.mult).then_inc(pick_chain, 1)

            def pick_first(c):
                dve.wait_ge(pick_chain, c * 4 + 2)
                v.tensor_reduce(first[:, :], is_top[:], X, ALU.max).then_inc(pick_chain, 1)

            def pick_onehot(c):
                dve.wait_ge(pick_chain, c * 4 + 3)
                v.tensor_tensor(onehot[:], is_top[:], wide(first[:, :]), ALU.is_equal).then_inc(pick_chain, 1)

            def keep_onehot(c):
                dve.wait_ge(pick_chain, c * 4 + 4)
                v.tensor_copy(onehot_b[:], onehot[:]).then_inc(onehot_done, 1)


            def gate_sum(c):
                dve.wait_ge(expo_done, c + 1)
                if not isinstance(c, int) or c > 0:
                    dve.wait_ge(gate_chain, c * 2)
                v.tensor_reduce(expsum[:, :], expo[:], X, ALU.add).then_inc(gate_chain, 1)

            def gate_and_token(c, r):
                dve.wait_ge(gate_chain, c * 2 + 1)
                v.reciprocal(rows[:, r, :, GATE], expsum[:, :])
                v.tensor_copy(rows[:, r, :, TOKEN], token_no[:, :]).then_inc(row_done, 1)

            def next_tokens(c):
                dve.wait_ge(row_done, c + 1)
                v.tensor_scalar(token_no[:, :], token_no[:, :], float(CH), None, ALU.add).then_inc(gate_chain, 1)


            def place_base(c):
                dve.wait_ge(pos_done, c + 1)
                v.tensor_tensor(pos8[:], M2[:, 0:2 * EXPERTS].rearrange("p (a b) -> p a b", a=2),
                                region8[:, :].unsqueeze(1).to_broadcast([P, 2, EXPERTS]), ALU.add).then_inc(place_chain, 1)

            def place_pick(c):
                dve.wait_ge(place_chain, c * 3 + 1)
                v.tensor_tensor(pos8m[:], pos8[:], onehot[:], ALU.mult).then_inc(place_chain, 1)
                v.tensor_tensor(seen2[:, :], seen[:, :], onehot_b[:, 0, :], ALU.add).then_inc(place_chain, 1)

            def place_rows(c, r):
                dve.wait_ge(place_chain, c * 3 + 2)
                with nc.allow_low_precision(reason="whole numbers below 2 ** 24"):
                    v.tensor_reduce(dest[:, r, :], pos8m[:], X, ALU.add).then_inc(dest_done, 1)
                dve.wait_ge(place_chain, c * 3 + 3)
                v.tensor_tensor(seen[:, :], seen2[:, :], onehot_b[:, 1, :], ALU.add).then_inc(seen_done, 1)

            for c in range(2):
                x_stats(c, c, c)
            dve.wait_ge(bv_proj, 1)
            dve.wait_ge(w_loaded, W_LOADS * 16)
            v.tensor_tensor(b_row[:, :], M2[:, 0:D], bo_row[:, :], ALU.add).then_inc(bo_ready, 1)
            for c in range(2):
                qk_lo(c)
                if c == 0:
                    x_stats(2, 0, 2)
            for half in range(2):
                v_low(0, 0, half)
            for half in range(2):
                maxima(0, 0, 0, half)

            dve.wait_ge(ffn_w_loaded, 4 * 16)
            for w, s, half, neg, wid in ((w1_in[:].rearrange("p e c d -> p (e c) d"), s1, s1h, s1n, D), (w2_in[:], s2, s2h, s2n, FE)):
                then(v.tensor_reduce(s[:, :], w, X, ALU.add, apply_absolute_value=True))
                then(v.tensor_scalar(s[:, :], s[:, :], 1.0 / wid, 1e-5, ALU.mult, ALU.max))
                v.tensor_scalar(half[:, :], s[:, :], 0.5, None, ALU.mult)
                then(v.tensor_scalar(neg[:, :], s[:, :], -0.5, None, ALU.mult))
            for e in range(BLOCKS):
                for c in range(2):
                    j = 2 * e + c
                    v.tensor_scalar(low1[:, c, :], w1_in[:, e, c, :], s1n[:, j:j + 1], None, ALU.is_lt)
                then(v.tensor_scalar(low2[:, :], w2_in[:, e, :], s2n[:, e:e + 1], None, ALU.is_lt))
                for c in range(2):
                    j = 2 * e + c
                    v.scalar_tensor_tensor(sign1[:, e, c, :], w1_in[:, e, c, :], s1h[:, j:j + 1], low1[:, c, :],
                                           ALU.is_gt, ALU.subtract)
                then(v.scalar_tensor_tensor(sign2[:, e, :], w2_in[:, e, :], s2h[:, e:e + 1], low2[:, :],
                                            ALU.is_gt, ALU.subtract))
            v.engine_nop().then_inc(signs, 1)

            def body(c, r, k):
                now, last, routed, ahead, ahead3 = has(k), has(k - 1), has(k - 2), has(k + 1), has(k + 3)
                if ahead3:
                    x_moments(c + 3, 1 - r, k + 3)
                if now:
                    maxima(c * 2 + 1, 1, k, 0)
                    maxima(c * 2 + 1, 1, k, 1)
                if now:
                    e_low(c * 2, 0, 2 * k)
                if ahead3:
                    x_aggregate(c + 3, 1 - r, k + 3)
                if last:
                    denominators(c * 2 - 1)
                if ahead3:
                    x_eps(c + 3, 1 - r)
                if last:
                    if k - 1 >= 2:
                        dve.wait_ge(attn_turned, c - 2)
                    divide(c * 2 - 1, 1 - r, 1)
                if has(k + 2):
                    qk_lo(c + 2)
                if routed:
                    pick_top(c - 2)
                if routed:
                    pick_shift(c - 2, k - 2)
                if ahead:
                    v_low(c + 1, 1 - r, 0)
                if routed:
                    pick_rank(c - 2)
                if ahead:
                    v_low(c + 1, 1 - r, 1)
                if routed:
                    pick_first(c - 2)
                if ahead:
                    maxima(c * 2 + 2, 0, k + 1, 0)
                if routed:
                    pick_onehot(c - 2)
                if ahead:
                    maxima(c * 2 + 2, 0, k + 1, 1)
                if routed:
                    keep_onehot(c - 2)
                if now:
                    denominators(c * 2)
                    e_low(c * 2 + 1, 1, 2 * k + 1)
                    if k >= 2:
                        dve.wait_ge(attn_turned, c - 1)
                    divide(c * 2, r, 0)
                if last:
                    residual(c - 1, 1 - r, k - 1)
                if routed:
                    gate_sum(c - 2)
                if last:
                    moments2(c - 1, 1 - r)
                if routed:
                    place_base(c - 2)
                if last:
                    aggregate2(c - 1, k - 1)
                if routed:
                    place_pick(c - 2)
                if last:
                    variance2(c - 1)
                if routed:
                    gate_and_token(c - 2, r)
                    place_rows(c - 2, r)
                    next_tokens(c - 2)

            chunks(dve, body)

            row8 = lambda a: a.unsqueeze(1).to_broadcast([P, SLOTS, EXPERTS])
            col8 = lambda a: a.unsqueeze(2).to_broadcast([P, SLOTS, EXPERTS])
            dve.wait_ge(counts_done, 1)
            then(v.tensor_copy(cnt[:, :], M2[:, 0:EXPERTS]))
            then(v.tensor_tensor(over[:], cnt[:, :].unsqueeze(2).to_broadcast([P, EXPERTS, NT]), thr[:], ALU.is_gt))
            then(v.tensor_reduce(tiles8[:, :], over[:], X, ALU.add))
            then(v.tensor_tensor(prod8[:], tiles8[:, :].unsqueeze(1).to_broadcast([P, EXPERTS, EXPERTS]), tri8[:], ALU.mult))
            then(v.tensor_reduce(upto8[:, :], prod8[:], X, ALU.add))
            then(v.tensor_tensor(start8[:, :], upto8[:, :], tiles8[:, :], ALU.subtract))
            then(v.tensor_tensor(sl_ge[:], col8(slot_no[:, :]), row8(upto8[:, :]), ALU.is_ge))
            then(v.tensor_reduce(sl_e[:, :], sl_ge[:], X, ALU.add))
            then(v.tensor_tensor(sl_oh[:], col8(sl_e[:, :]), row8(iota8[:, :]), ALU.is_equal))
            v.tensor_tensor(sl_m[:], sl_oh[:], row8(start8[:, :]), ALU.mult)
            then(v.tensor_tensor(sl_m2[:], sl_oh[:], row8(cnt[:, :]), ALU.mult))
            v.tensor_reduce(sl_start[:, :], sl_m[:], X, ALU.add)
            then(v.tensor_reduce(sl_n[:, :], sl_m2[:], X, ALU.add))
            v.tensor_scalar(sl_last[:, :], sl_n[:, :], -float(TILE), 0.0, ALU.add, ALU.max)
            then(v.tensor_tensor(sl_j[:, :], slot_no[:, :], sl_start[:, :], ALU.subtract))
            then(v.tensor_scalar(sl_j[:, :], sl_j[:, :], float(TILE), None, ALU.mult))
            then(v.tensor_tensor(sl_off[:, :], sl_j[:, :], sl_last[:, :], ALU.min))
            v.tensor_scalar(sl_ec[:, :], sl_e[:, :], float(EXPERTS - 1), None, ALU.min)
            then(v.tensor_scalar(sl_row[:, :], sl_off[:, :], part_no[:, 0:1], None, ALU.add))
            v.tensor_tensor(sl_v1[:, :], sl_row[:, :], sl_j[:, :], ALU.is_ge)
            then(v.tensor_tensor(sl_v2[:, :], sl_row[:, :], sl_n[:, :], ALU.is_lt))
            then(v.tensor_tensor(valid[:, :], sl_v1[:, :], sl_v2[:, :], ALU.mult))
            then(v.scalar_tensor_tensor(sl_base[:, :], sl_ec[:, :], float(TOKENS), sl_off[:, :], ALU.mult, ALU.add))
            then(v.tensor_copy(tab[0:1, 0, :], sl_base[0:1, :]))
            v.tensor_copy(tab[0:1, 1, :], sl_ec[0:1, :]).then_inc(tab_done, 1)

            def split_h(u, r, k):
                dve.wait_ge(h32_done, u + 1)
                if k >= 2:
                    dve.wait_ge(f1_done, u - 1)
                v.tensor_copy(h_hi[:, r, :], h32[:, r, :]).then_inc(h_chain, 1)
                dve.wait_ge(h_chain, u + 1)
                v.tensor_tensor(h_lo[:, r, :], h32[:, r, :], h_hi[:, r, :], ALU.subtract).then_inc(h_done, 1)

            def low_g(u, r, k):
                dve.wait_ge(g32_done, u + 1)
                if k >= 2:
                    dve.wait_ge(f2_done, u - 1)
                src, hi, lo = (t[:, r].rearrange("p a b c -> p (a b c)") for t in (g32, g_hi, g_lo))
                v.tensor_tensor(lo, src, hi, ALU.subtract).then_inc(g_done, 1)

            def scale_sums(u, m, k, experts):
                r = m % 2
                dve.wait_ge(f2_done, u + 1)
                dve.wait_ge(rows_loaded[m % 2], twos(u, m % 2, 0) * 2)
                if k >= 1:
                    dve.wait_ge(parts_done, u)
                if k >= 2:
                    dve.wait_ge(sum_done, u - 1)
                    dve.wait_ge(out_stored[r], twos(u, r, -2) * 2)
                v.scalar_tensor_tensor(o_idx_f[:, :], in_rows[:, m, :, TOKEN], -NOWHERE, valid[:, bass.ds(u * 2, 2)],
                                       ALU.add, ALU.mult).then_inc(o_chain, 1)
                v.tensor_tensor(sh_out[:, r], YY[r][:, 0:2 * D].rearrange("p (a b) -> p a b", a=2),
                                s2_row[:, 0, :].unsqueeze(1).to_broadcast([P, 2, D]), ALU.mult)
                for i, e in enumerate(experts):
                    v.scalar_tensor_tensor(ex_out[:, r, i, :], YY[r][:, (2 + i) * D:(3 + i) * D], in_rows[:, m, i, GATE:GATE + 1],
                                           s2_row[:, bass.ds(e + 1, 1), :].rearrange("p a b -> p (a b)"), ALU.mult, ALU.mult)
                dve.wait_ge(o_chain, u + 1)
                v.tensor_scalar(o_idx[:, r, :], o_idx_f[:, :], NOWHERE, None, ALU.add).then_inc(parts_done, 1)

            def experts_of(u):
                return [dve.value_load(tab[0:1, 1, bass.ds(u * 2 + i, 1)], min_val=0, max_val=EXPERTS - 1) for i in range(2)]

            def body(u, m, k):
                r = m % 2
                experts = experts_of(u - 1) if k >= 1 else None
                if k + 1 < STEPS:
                    split_h(u + 1, 1 - r, k + 1)
                low_g(u, r, k)
                if k >= 1:
                    scale_sums(u - 1, (m + ROWBUFS - 1) % ROWBUFS, k - 1, experts)

            dve.wait_ge(t_kept, 6)
            dve.wait_ge(tab_done, 1)
            split_h(0, 0, 0)
            steps(dve, body)
            scale_sums(STEPS - 1, (STEPS - 1) % ROWBUFS, STEPS - 1, experts_of(STEPS - 1))


_INS = ["x", "ctx_1024", "L0_xattn_Wq", "L0_xattn_bq", "L0_xattn_Wk", "L0_xattn_bk", "L0_xattn_Wv", "L0_xattn_bv",
        "L0_xattn_Wo", "L0_xattn_bo", "L0_ffn_shared_w1", "L0_ffn_shared_w2", "L0_ffn_expert_w1", "L0_ffn_expert_w2",
        "L0_ffn_router_w", "L0_ffn_ln_gamma", "L0_ffn_ln_beta"]


def kernel(**inputs):
    import numpy as np
    import concourse.bacc as bacc
    from concourse.bass_utils import run_bass_kernel_spmd

    nc = bacc.Bacc("TRN2", target_bir_lowering=False, num_devices=1)
    arrays, args = {}, []
    for name in _INS:
        a = np.ascontiguousarray(inputs[name])
        if name in ("x", "ctx_1024"):
            shape = a.shape
            a = a.reshape(-1, shape[-1])
        arrays["in_" + name] = a
        args.append(nc.dram_tensor("in_" + name, a.shape, mybir.dt.from_np(a.dtype), kind="ExternalInput").ap())
    args.append(nc.dram_tensor("out", arrays["in_x"].shape, F32, kind="ExternalOutput").ap())
    block_program(nc, *args)
    r = run_bass_kernel_spmd(nc, [arrays], core_ids=[0])
    return r.results[0]["out"].reshape(shape)
```

```python
from contextlib import ExitStack

import concourse.bass as bass
from concourse import mybir

ALU = mybir.AluOpType
ACT = mybir.ActivationFunctionType
X = mybir.AxisListType.X
F32 = mybir.dt.float32
F16 = mybir.dt.float16
BF16 = mybir.dt.bfloat16
I32 = mybir.dt.int32

P = 128
D = 128
S = 64
HEADS, HD = 16, 8
QUADS = HEADS // 4
TILE = 128
CH = 256
NB = CH // S
EXPERTS = 8
FE = 256
BLOCKS = EXPERTS + 1
LN_EPS = 1e-5
VW = HD + 1
LNE = 4.1588830833596715
ROW = 2 * D + 4
GATE, TOKEN = 2 * D, 2 * D + 1


def block_program(nc, x, ctx_in, Wq, bq, Wk, bk, Wv, bv, Wo, bo, sw1, sw2, ew1, ew2, rw, gamma, beta, out):
    TOKENS = x.shape[0]
    NCH = TOKENS // CH
    NT = TOKENS // TILE
    SLOTS = -(-((TOKENS + EXPERTS * (TILE - 1)) // TILE) // 8) * 8
    STEPS = SLOTS // 2
    ROWBUFS = 6
    assert (STEPS - 8) % ROWBUFS == 0
    NOWHERE = float(2 * TOKENS)
    SCALE = float(HD) ** -0.5
    W_LOADS = 7

    qk_dram = nc.dram_tensor("qk_terms", (NCH, 2, 4, 4, 32, CH), F16).ap()
    by_expert = nc.dram_tensor("rows_by_expert", (EXPERTS * TOKENS, ROW), F32).ap()

    with ExitStack() as stack:
        def sb(name, shape, dt=F32):
            return stack.enter_context(nc.sbuf_tensor(name, shape, dt))

        def sem(name):
            return stack.enter_context(nc.semaphore(name))

        ident = sb("ident", [P, P])
        identb = sb("identb", [P, P], BF16)
        identh = sb("identh", [P, P], F16)
        w_in = sb("w_in", [P, 4, P])
        wT = sb("wT", [P, 3, P])
        woT = sb("woT", [64, 2, P])
        b_col = sb("b_col", [P, 2])
        bv_col = sb("bv_col", [64, 2])
        bo_row = sb("bo_row", [P, D])
        b_row = sb("b_row", [P, D])
        ln_col = sb("ln_col", [P, 2])
        rw_in = sb("rw_in", [EXPERTS, D])
        rwT = sb("rwT", [D, EXPERTS])
        w1_in = sb("w1_in", [P, BLOCKS, 2, D])
        w2_in = sb("w2_in", [P, BLOCKS, FE])
        sign1 = sb("sign1", [P, BLOCKS, 2, D], F16)
        sign2 = sb("sign2", [P, BLOCKS, FE], F16)
        low1 = sb("low1", [P, 2, D], F16)
        low2 = sb("low2", [P, FE], F16)
        s1 = sb("s1", [P, BLOCKS * 2])
        s1h = sb("s1h", [P, BLOCKS * 2])
        s1n = sb("s1n", [P, BLOCKS * 2])
        s2 = sb("s2", [P, BLOCKS])
        s2h = sb("s2h", [P, BLOCKS])
        s2n = sb("s2n", [P, BLOCKS])
        s2_row = sb("s2_row", [P, BLOCKS, D])
        t1 = sb("t1", [P, BLOCKS, 2, P], F16)
        t2 = sb("t2", [P, BLOCKS, 2, D], F16)
        zeros = sb("zeros", [P, ROW])
        lne = sb("lne", [P, 1])

        x_in = sb("x_in", [P, 2, 2, D])
        c_in = sb("c_in", [P, 2, 2, D])
        x_res = sb("x_res", [P, 2, 2, D])
        stats = sb("stats", [P, 2, 6])
        mv = sb("mv", [P, 2, 2, 2])
        veps = sb("veps", [P, 2, 2])
        rstd = sb("rstd", [P, 2, 2])
        negmean = sb("negmean", [P, 2, 2])
        nmr = sb("nmr", [P, 2, 2])
        minus_half = sb("minus_half", [P, 2])
        xn = sb("xn", [P, 2, 2, D])
        xcT = sb("xcT", [P, 2, 4, TILE])
        qk_hl = sb("qk_hl", [P, 2, 2, 2, CH], F16)
        q_t = sb("q_t", [P, 2, QUADS, CH], F16)
        k_t = sb("k_t", [P, 2, QUADS, NB, 4, S], F16)
        v_hi = sb("v_hi", [P, 2, NB, 2 * QUADS, 2, VW], F16)
        v_lo = sb("v_lo", [P, 2, NB, 2 * QUADS, 2, VW], F16)
        negmax = sb("negmax", [P, 2, P], BF16)
        negmaxT = sb("negmaxT", [P, 2, P], BF16)
        sel = sb("sel", [P, HEADS // 2, 2, S], BF16)
        e32 = sb("e32", [P, 2, 2, 4, S])
        e_hi = sb("e_hi", [P, 2, 2, 2, 4, S], F16)
        e_lo = sb("e_lo", [P, 2, 2, 2, 4, S], F16)
        rden = sb("rden", [P, 2, 8])
        attn = sb("attn", [P, 2, NB, 2 * QUADS, HD])
        attnT = sb("attnT", [64, 2, NB, S])
        stats2 = sb("stats2", [P, 2, 6])
        mv2 = sb("mv2", [P, 2, 2])
        w2var = sb("w2var", [P, 2])
        rstd2 = sb("rstd2", [P, 2])
        negmean2 = sb("negmean2", [P, 2])
        nmr2 = sb("nmr2", [P, 2])
        rows = sb("rows", [P, 2, 2, ROW])
        hT32 = sb("hT32", [P, CH])
        top = sb("top", [P, 2])
        shifted = sb("shifted", [P, 2, EXPERTS])
        is_top = sb("is_top", [P, 2, EXPERTS])
        first = sb("first", [P, 2])
        onehot = sb("onehot", [P, 2, EXPERTS])
        onehot_b = sb("onehot_b", [P, 2, EXPERTS], BF16)
        expo = sb("expo", [P, 2, EXPERTS])
        expsum = sb("expsum", [P, 2])
        seen = sb("seen", [P, EXPERTS], BF16)
        seen2 = sb("seen2", [P, EXPERTS], BF16)
        pos8 = sb("pos8", [P, 2, EXPERTS])
        pos8m = sb("pos8m", [P, 2, EXPERTS])
        dest = sb("dest", [P, 2, 2], I32)
        token_no = sb("token_no", [P, 2])
        before = sb("before", [P, P], BF16)
        ones_b = sb("ones_b", [P, P], BF16)
        rank8 = sb("rank8", [P, EXPERTS])
        region8 = sb("region8", [P, EXPERTS])
        thr = sb("thr", [P, EXPERTS, NT])
        tri8 = sb("tri8", [P, EXPERTS, EXPERTS])
        slot_no = sb("slot_no", [P, SLOTS])
        part_no = sb("part_no", [P, 1])
        cnt = sb("cnt", [P, EXPERTS])
        over = sb("over", [P, EXPERTS, NT])
        tiles8 = sb("tiles8", [P, EXPERTS])
        prod8 = sb("prod8", [P, EXPERTS, EXPERTS])
        upto8 = sb("upto8", [P, EXPERTS])
        next8 = sb("next8", [P, EXPERTS])
        sl_ge = sb("sl_ge", [P, SLOTS, EXPERTS])
        sl_e = sb("sl_e", [P, SLOTS])
        sl_n0 = sb("sl_n0", [P, SLOTS])
        sl_m = sb("sl_m", [P, SLOTS, EXPERTS])
        sl_m2 = sb("sl_m2", [P, SLOTS, EXPERTS])
        sl_start = sb("sl_start", [P, SLOTS])
        sl_n = sb("sl_n", [P, SLOTS])
        sl_j = sb("sl_j", [P, SLOTS])
        sl_last = sb("sl_last", [P, SLOTS])
        sl_off = sb("sl_off", [P, SLOTS])
        sl_row = sb("sl_row", [P, SLOTS])
        sl_v1 = sb("sl_v1", [P, SLOTS])
        sl_v2 = sb("sl_v2", [P, SLOTS])
        valid = sb("valid", [P, SLOTS])
        sl_ec = sb("sl_ec", [P, SLOTS])
        sl_base = sb("sl_base", [P, SLOTS])
        tab = sb("tab", [1, 2, SLOTS], I32)
        in_rows = sb("in_rows", [P, ROWBUFS, 2, ROW])
        h32 = sb("h32", [P, 2, CH])
        h_hi = sb("h_hi", [P, 2, CH], F16)
        h_lo = sb("h_lo", [P, 2, CH], F16)
        g32 = sb("g32", [P, 2, 2, 2, CH])
        g_hi = sb("g_hi", [P, 2, 2, 2, CH], F16)
        g_lo = sb("g_lo", [P, 2, 2, 2, CH], F16)
        sh_out = sb("sh_out", [P, 2, 2, D])
        ex_out = sb("ex_out", [P, 2, 2, D])
        o_sum = sb("o_sum", [P, 2, D])
        o_rows = sb("o_rows", [P, 2, 2, D])
        o_idx_f = sb("o_idx_f", [P, 2])
        o_idx = sb("o_idx", [P, 2, 2], I32)

        banks = [stack.enter_context(nc.psum_tensor(f"bank{i}", [P, 512], F32)) for i in range(8)]
        A = banks[0:2]
        ST = banks[2:4]
        AV = banks[4]
        M0, M1, M2 = banks[5:8]
        XT = (banks[0], banks[7])
        F1 = ((banks[1], banks[2]), (banks[3], banks[4]))
        YY = (banks[5], banks[6])

        mats_loaded = sem("mats_loaded")
        b_qk_loaded = sem("b_qk_loaded")
        w_loaded = sem("w_loaded")
        ffn_w_loaded = [sem(f"ffn_w_loaded{i}") for i in range(3)]
        xc_loaded = [sem("xc_loaded0"), sem("xc_loaded1")]
        res_loaded = [sem("res_loaded0"), sem("res_loaded1")]
        terms_stored = [sem("terms_stored0"), sem("terms_stored1")]
        terms_loaded = [sem("terms_loaded0"), sem("terms_loaded1")]
        region_cleared = sem("region_cleared")
        scattered = [sem("scattered0"), sem("scattered1")]
        rows_loaded = [sem("rows_loaded0"), sem("rows_loaded1")]
        rows_free = sem("rows_free")
        out_stored = [sem("out_stored0"), sem("out_stored1")]
        consts = sem("consts")
        k_zeroed = sem("k_zeroed")
        vconsts = sem("vconsts")
        w_turned = sem("w_turned")
        w_kept = sem("w_kept")
        bv_proj = sem("bv_proj")
        bo_ready = sem("bo_ready")
        signs = sem("signs")
        t_turned = sem("t_turned")
        t_kept = sem("t_kept")
        stats_done = sem("stats_done")
        rstd_done = sem("rstd_done")
        xn_ready = sem("xn_ready")
        xc_turned = sem("xc_turned")
        xcT_ready = sem("xcT_ready")
        q_proj, k_proj, v_proj = sem("q_proj"), sem("k_proj"), sem("v_proj")
        qk_hi_done = sem("qk_hi_done")
        qk_lo_done = sem("qk_lo_done")
        v_hi_done = sem("v_hi_done")
        v_lo_done = sem("v_lo_done")
        a_done = sem("a_done")
        max_done = sem("max_done")
        negmax_turned = sem("negmax_turned")
        negmaxT_ready = sem("negmaxT_ready")
        st_done = sem("st_done")
        e_hi_done = sem("e_hi_done")
        e32_done = sem("e32_done")
        e_lo_done = [sem("e_lo_done0"), sem("e_lo_done1")]
        av_done = sem("av_done")
        rden_done = sem("rden_done")
        attn_done = sem("attn_done")
        attn_turned = sem("attn_turned")
        attnT_ready = sem("attnT_ready")
        y_done = sem("y_done")
        res_ready = sem("res_ready")
        x2_done = sem("x2_done")
        stats2_done = sem("stats2_done")
        rstd2_done = sem("rstd2_done")
        n2_done = sem("n2_done")
        n2_turned = sem("n2_turned")
        hT_ready = sem("hT_ready")
        logits_done = sem("logits_done")
        shifted_done = sem("shifted_done")
        expo_done = sem("expo_done")
        onehot_done = sem("onehot_done")
        pos_done = sem("pos_done")
        dest_done = sem("dest_done")
        row_done = sem("row_done")
        seen_done = sem("seen_done")
        carried = sem("carried")
        chain = sem("chain")
        st_chain = sem("st_chain")
        st2_chain = sem("st2_chain")
        pick_chain = sem("pick_chain")
        gate_chain = sem("gate_chain")
        place_chain = sem("place_chain")
        h_chain = sem("h_chain")
        g_chain = sem("g_chain")
        o_chain = sem("o_chain")
        pchain = sem("pchain")
        counts_done = sem("counts_done")
        tab_done = sem("tab_done")
        h_turned = sem("h_turned")
        h32_done = sem("h32_done")
        h_done = sem("h_done")
        f1_done = sem("f1_done")
        g32_done = sem("g32_done")
        g_done = sem("g_done")
        f2_done = sem("f2_done")
        parts_done = sem("parts_done")
        sum_done = sem("sum_done")
        o_done = sem("o_done")

        EARLY, LATE = (3, NCH - 5), NCH + 2

        def chunks(eng, body):
            for c in range(EARLY[0]):
                body(c, c % 2, c)
            with eng.Fori(EARLY[0], EARLY[1] - 1, 2) as c:
                body(c, 1, EARLY[0])
                body(c + 1, 0, EARLY[0] + 1)
            for c in range(EARLY[1], LATE):
                body(c, c % 2, c)

        def twos(c, r, shift):
            return (c + (shift + 2 - (r + shift) % 2)) * 8

        def carry_waits(eng):
            eng.sem_inc(carried, 1)

        def v_sums(hp):
            return M1[64 * hp:64 * hp + 64, 0:CH].rearrange("p (bq pp d) -> p bq pp d", pp=2, d=HD)

        def v_part(t, r, hp, lo=0, hi=HD):
            return t[64 * hp:64 * hp + 64, r].rearrange("p b (q hp) pp d -> p hp (b q) pp d", hp=2)[:, hp, :, :, lo:hi]

        def has(j):
            return 0 <= j < NCH

        def steps(eng, body):
            for u in range(4):
                body(u, u % ROWBUFS, u)
            with eng.Fori(4, STEPS - 4 - (ROWBUFS - 1), ROWBUFS) as u:
                for j in range(ROWBUFS):
                    body(u + j, (4 + j) % ROWBUFS, 4 + j)
            for u in range(STEPS - 4, STEPS):
                body(u, u % ROWBUFS, u)

        block = stack.enter_context(nc.Block())
        x_v = x.rearrange("(c t p) d -> c p t d", p=P, t=2)
        c_v = ctx_in.rearrange("(c t p) d -> c p t d", p=P, t=2)

        @block.sync
        def _(sp):
            def load_xc(c, r):
                sp.dma_start(x_in[:, r], x_v[c]).then_inc(xc_loaded[r], 16)
                sp.dma_start(c_in[:, r], c_v[c]).then_inc(xc_loaded[r], 16)

            def load_ffn_weights():
                sp.dma_start(w1_in[:, 0], sw1.rearrange("(c f) d -> f c d", f=P)).then_inc(ffn_w_loaded[0], 16)
                sp.dma_start(w2_in[:, 0], sw2).then_inc(ffn_w_loaded[0], 16)
                for half in range(2):
                    e = 4 * half
                    sp.dma_start(w1_in[:, 1 + e:5 + e].rearrange("p e c d -> p (e c) d"),
                                 ew1[e:e + 4].rearrange("e (c f) d -> f (e c) d", f=P)).then_inc(ffn_w_loaded[1 + half], 16)
                    sp.dma_start(w2_in[:, 1 + e:5 + e], ew2[e:e + 4].rearrange("e d f -> d e f")).then_inc(ffn_w_loaded[1 + half], 16)

            load_xc(0, 0)
            for i, w in enumerate((Wq, Wk, Wv)):
                sp.dma_start(w_in[:, i, :], w).then_inc(mats_loaded, 16)
            for p in range(2):
                sp.dma_start(w_in[:, 3, 64 * p:64 * p + 64].rearrange("o (q r) -> o q r", q=QUADS),
                             Wo.rearrange("o (q p r) -> o p q r", q=QUADS, p=2)[:, p]).then_inc(mats_loaded, 16)
            sp.dma_start(rw_in[:, :], rw).then_inc(mats_loaded, 16)
            with nc.allow_non_contiguous_dma(reason="512 bytes of biases"):
                for i, b in enumerate((bq, bk)):
                    for m in range(4):
                        sp.dma_start(b_col[32 * m:32 * m + 32, i:i + 1],
                                     b.rearrange("(q m d) -> m d q", m=4, d=HD)[m].unsqueeze(2)).then_inc(b_qk_loaded, 16)
                load_xc(1, 1)
                load_ffn_weights()
                for q in range(QUADS):
                    sp.dma_start(bv_col[16 * q:16 * q + 16, :],
                                 bv.rearrange("(q p r) -> q r p", q=QUADS, p=2)[q]).then_inc(w_loaded, 16)
                sp.dma_start(ln_col[:, 0:1], gamma.unsqueeze(1)).then_inc(w_loaded, 16)
                sp.dma_start(ln_col[:, 1:2], beta.unsqueeze(1)).then_inc(w_loaded, 16)
            sp.dma_start(bo_row[:, :], bo.unsqueeze(0).to_broadcast([P, D])).then_inc(w_loaded, 16)

            def store_terms(c, r):
                sp.wait_ge(qk_lo_done, (c + 1) * 2)
                for qk in range(2):
                    for t in range(4):
                        part = t % 2 if qk == 0 else t // 2
                        sp.dma_start(qk_dram[c, qk, :, t], qk_hl[:, r, qk, part, :]).then_inc(terms_stored[r], 16)

            def load_terms(c, r, used):
                sp.wait_ge(terms_stored[r], twos(c, r, 0) * 8)
                carry_waits(sp)
                if used:
                    sp.wait_ge(st_done, (c - 1) * 4)
                sp.dma_start(q_t[:, r], qk_dram[c, 0].rearrange("m t (d q) n -> (m t d) q n", q=QUADS)).then_inc(terms_loaded[r], 16)
                for m in range(4):
                    sp.dma_start(k_t[32 * m:32 * m + 32, r, :, :, m, :].rearrange("p q b s -> p (q b) s"),
                                 qk_dram[c, 1, m].rearrange("t (d q) (b s) -> (t d) (q b) s", q=QUADS, s=S)).then_inc(terms_loaded[r], 16)

            def load_res(c, r, used):
                if used:
                    sp.wait_ge(x2_done, c - 1)
                sp.dma_start(x_res[:, r], x_v[c]).then_inc(res_loaded[r], 16)

            sp.wait_ge(vconsts, 1)
            sp.wait_ge(xc_turned, 1)
            load_xc(2, 0)
            sp.wait_ge(k_zeroed, 1)
            store_terms(0, 0)
            load_terms(0, 0, False)
            sp.wait_ge(xc_turned, 2)
            load_xc(3, 1)
            store_terms(1, 1)
            load_terms(1, 1, False)
            sp.wait_ge(xc_turned, 3)
            load_xc(4, 0)
            store_terms(2, 0)

            def clear_regions():
                for e in range(EXPERTS):
                    sp.dma_start(by_expert[e * TOKENS:e * TOKENS + TILE], zeros[:, :]).then_inc(region_cleared, 16)

            def body(c, r, k):
                if k == 0:
                    clear_regions()
                if has(k):
                    load_res(c, r, k >= 2)
                if has(k + 3):
                    if has(k + 5):
                        sp.wait_ge(xc_turned, c + 4)
                        load_xc(c + 5, 1 - r)
                if has(k + 2):
                    load_terms(c + 2, r, True)
                if has(k + 3):
                    store_terms(c + 3, 1 - r)

            chunks(sp, body)

            sp.wait_ge(tab_done, 1)
            sp.wait_ge(scattered[0], NCH * 16)
            sp.wait_ge(scattered[1], NCH * 16)

            def body(u, m, k):
                if k >= 2:
                    sp.wait_ge(h_turned, u - 1)
                    carry_waits(sp)
                sp.wait_ge(rows_free, u + 1)
                carry_waits(sp)
                for i in range(2):
                    row = sp.value_load(tab[0:1, 0, bass.ds(u * 2 + i, 1)], min_val=0, max_val=EXPERTS * TOKENS - TILE)
                    sp.dma_start(in_rows[:, m, i, :], by_expert[bass.ds(row, TILE), :]).then_inc(rows_loaded[m % 2], 16)

            steps(sp, body)
            for r in range(2):
                sp.wait_ge(out_stored[r], STEPS * 16)

        @block.gpsimd
        def _(pool):
            n = [0]

            def then(ins):
                n[0] += 1
                ins.then_inc(pchain, 1)
                pool.wait_ge(pchain, n[0])

            nc.gpsimd.memset(minus_half[:, :], -0.5)
            nc.gpsimd.memset(ones_b[:, :], 1.0)
            nc.gpsimd.memset(before[:, :], 1.0)
            then(nc.gpsimd.memset(ident[:, :], 0.0))
            then(nc.gpsimd.affine_select(out=ident[:, :], in_=ident[:, :], compare_op=ALU.not_equal, fill=1.0,
                                         base=0, pattern=[[-1, P]], channel_multiplier=1))
            nc.gpsimd.tensor_copy(identb[:, :], ident[:, :])
            nc.gpsimd.tensor_copy(identh[:, :], ident[:, :])
            nc.gpsimd.affine_select(out=before[:, :], in_=before[:, :], compare_op=ALU.is_gt, fill=0.0,
                                    base=0, pattern=[[1, P]], channel_multiplier=-1)
            then(nc.gpsimd.memset(sel[:], 0.0))
            then(nc.gpsimd.affine_select(out=sel[:], in_=sel[:], compare_op=ALU.not_equal, fill=1.0, base=0,
                                         pattern=[[-2, HEADS // 2], [-1, 2], [0, S]], channel_multiplier=1))
            then(nc.gpsimd.memset(tri8[:], 1.0))
            then(nc.gpsimd.affine_select(out=tri8[:], in_=tri8[:], compare_op=ALU.is_ge, fill=0.0, base=0,
                                         pattern=[[1, EXPERTS], [-1, EXPERTS]], channel_multiplier=0))
            iotas = ((rank8[:, :], [[-1, EXPERTS]], EXPERTS, 0), (region8[:, :], [[TOKENS, EXPERTS]], 0, 0),
                     (token_no[:, :], [[TILE, 2]], 0, 1),
                     (thr[:], [[0, EXPERTS], [TILE, NT]], 0, 0), (slot_no[:, :], [[1, SLOTS]], 0, 0),
                     (part_no[:, :], [[0, 1]], 0, 1))
            for o, pat, base, cm in iotas:
                last = nc.gpsimd.iota(o, pattern=pat, base=base, channel_multiplier=cm, allow_small_or_imprecise_dtypes=True)
            last.then_inc(consts, 1)

            def x_scale(c, r, k):
                pool.wait_ge(stats_done, c + 1)
                if k >= 2:
                    pool.wait_ge(xn_ready, c - 1)
                nc.gpsimd.tensor_tensor(rstd[:, r], veps[:, r], minus_half[:, :], ALU.pow).then_inc(rstd_done, 1)
                pool.wait_ge(rstd_done, c * 2 + 1)
                nc.gpsimd.tensor_tensor(nmr[:, r], negmean[:, r], rstd[:, r], ALU.mult).then_inc(rstd_done, 1)

            for c in range(2):
                x_scale(c, c, c)
            nc.gpsimd.memset(k_t[:, 0], 0.0)
            nc.gpsimd.memset(k_t[:, 1], 0.0).then_inc(k_zeroed, 1)
            for c in range(2, 4):
                x_scale(c, c % 2, c)
            pool.wait_ge(bo_ready, 1)

            def e_low(T, i, k):
                pool.wait_ge(e32_done, T * 2 + 2)
                if k >= 2:
                    pool.wait_ge(av_done, T - 1)
                hi, lo = (t[:, i, 1].rearrange("p a b c -> p (a b c)") for t in (e_hi, e_lo))
                nc.gpsimd.tensor_tensor(lo, e32[:, 1].rearrange("p a b c -> p (a b c)"), hi,
                                        ALU.subtract).then_inc(e_lo_done[1], 1)

            def scale2(c, k):
                pool.wait_ge(stats2_done, c + 1)
                if k >= 1:
                    pool.wait_ge(n2_done, c * 2)
                nc.gpsimd.tensor_tensor(rstd2[:, :], w2var[:, :], minus_half[:, :], ALU.pow).then_inc(rstd2_done, 1)
                pool.wait_ge(rstd2_done, c * 2 + 1)
                nc.gpsimd.tensor_tensor(nmr2[:, :], negmean2[:, :], rstd2[:, :], ALU.mult).then_inc(rstd2_done, 1)

            def scatter(c, r, k):
                pool.wait_ge(dest_done, c + 1)
                if k == 0:
                    pool.wait_ge(region_cleared, EXPERTS * 16)
                pool.wait_ge(row_done, c + 1)
                carry_waits(pool)
                for i in range(2):
                    nc.gpsimd.indirect_dma_start(by_expert, bass.IndirectOffsetOnAxis(ap=dest[:, r, i:i + 1], axis=0),
                                                 rows[:, r, i, :], None).then_inc(scattered[r], 16)

            def body(c, r, k):
                if has(k - 1):
                    pool.wait_ge(res_loaded[1 - r], twos(c, r, -1))
                    nc.gpsimd.tensor_tensor(x_res[:, 1 - r], x_res[:, 1 - r], b_row[:, :].unsqueeze(1).to_broadcast([P, 2, D]),
                                            ALU.add).then_inc(res_ready, 1)
                if has(k):
                    e_low(c * 2, 0, 2 * k)
                if has(k + 4):
                    x_scale(c + 4, r, k + 4)
                if has(k):
                    e_low(c * 2 + 1, 1, 2 * k + 1)
                if has(k - 1):
                    scale2(c - 1, k - 1)
                if has(k - 2):
                    scatter(c - 2, r, k - 2)

            chunks(pool, body)

            def add_and_store(u, m, k):
                r = m % 2
                pool.wait_ge(parts_done, u + 1)
                if k >= 1:
                    pool.wait_ge(o_done, u)
                nc.gpsimd.tensor_tensor(o_sum[:], sh_out[:, r], ex_out[:, r], ALU.add).then_inc(sum_done, 1)
                pool.wait_ge(sum_done, u + 1)
                if k >= 2:
                    pool.wait_ge(out_stored[r], twos(u, r, -2) * 2)
                nc.gpsimd.tensor_tensor(o_rows[:, r], o_sum[:], in_rows[:, m, :, D:2 * D], ALU.add).then_inc(o_done, 1)
                pool.wait_ge(o_done, u + 1)
                pool.sem_inc(rows_free, 1)
                for i in range(2):
                    nc.gpsimd.indirect_dma_start(out, bass.IndirectOffsetOnAxis(ap=o_idx[:, r, i:i + 1], axis=0),
                                                 o_rows[:, r, i, :], None, bounds_check=TOKENS - 1,
                                                 oob_is_err=False).then_inc(out_stored[r], 16)

            pool.sem_inc(rows_free, ROWBUFS)
            steps(pool, add_and_store)

        @block.tensor
        def _(pe):
            mm, tr = nc.tensor.matmul, nc.tensor.transpose

            pe.wait_ge(mats_loaded, 6 * 16)
            pe.wait_ge(consts, 1)
            for i in range(3):
                tr(A[0][:, i * P:(i + 1) * P], w_in[:, i, :], ident[:, :])
            tr(A[0][:, 3 * P:3 * P + EXPERTS], rw_in[:, :], ident[0:EXPERTS, 0:EXPERTS])
            for p in range(2):
                last = tr(A[1][0:64, p * P:(p + 1) * P], w_in[:, 3, 64 * p:64 * p + 64], ident[:, :])
            last.then_inc(w_turned, 1)

            def turn_xc(c, r, k):
                pe.wait_ge(xn_ready, c + 1)
                pe.wait_ge(xc_loaded[r], twos(c, r, 0) * 2)
                if k >= 5:
                    pe.wait_ge(x2_done, c - 4)
                for i in range(2):
                    tr(M0[:, i * P:(i + 1) * P], xn[:, r, i, :], ident[:, :])
                for i in range(2):
                    last = tr(M0[:, (2 + i) * P:(3 + i) * P], c_in[:, r, i, :], ident[:, :])
                last.then_inc(xc_turned, 1)

            def proj_q(c, r):
                pe.wait_ge(xcT_ready, c + 1)
                mm(M0[:, 0:CH], wT[:, 0, :], xcT[:, r, 0:2, :], start=True, stop=True).then_inc(q_proj, 1)

            def proj_k(c, r, before_it):
                before_it()
                mm(M1[:, 0:CH], wT[:, 1, :], xcT[:, r, 2:4, :], start=True, stop=True).then_inc(k_proj, 1)

            def proj_v(c, r, before_it):
                before_it()
                for b in range(NB):
                    src = xcT[:, r, 2 + b // 2, (b % 2) * S:(b % 2 + 1) * S]
                    for hp in range(2):
                        last = mm(M1[64 * hp:64 * hp + 64, b * 64:(b + 1) * 64], src, wT[:, 2, 64 * hp:64 * hp + 64], start=True, stop=True,
                                  skip_group_check=True)
                last.then_inc(v_proj, 1)

            def scores_a(T, r, i, k):
                if i == 0:
                    pe.wait_ge(terms_loaded[r], k)
                for hh in range(2):
                    if T is not None:
                        pe.wait_ge(max_done, T * 2 - 1 + hh)
                    for b in range(2):
                        for q in (2 * hh, 2 * hh + 1):
                            t0 = i * TILE + b * S
                            last = mm(A[hh][b * S:(b + 1) * S, (q % 2) * 256:(q % 2 + 1) * 256],
                                      q_t[:, r, q, t0:t0 + S], k_t[:, r, q, 2 * i + b].rearrange("p m s -> p (m s)"), start=True, stop=True,
                                      skip_group_check=True)
                    last.then_inc(a_done, 1)

            def turn_negmax(T, i, before_it):
                pe.wait_ge(max_done, T * 2 + 2)
                before_it()
                tr(M2[:, :].bitcast(BF16)[:, 0:P], negmax[:, i, :], identb[:, :]).then_inc(negmax_turned, 1)

            def scores_st(T, r, i, k):
                pe.wait_ge(negmaxT_ready, T + 1)
                for hh in range(2):
                    if k >= 1:
                        pe.wait_ge(e32_done, T * 2 - 1 + hh)
                    for pr in range(4):
                        pair = 4 * hh + pr
                        q, m = pair // 2, (pair % 2) * 2
                        mm(ST[hh][:, pr * 128:(pr + 1) * 128], sel[:, pair].rearrange("p a b -> p (a b)"), negmaxT[:, i, :],
                           start=True, stop=False, skip_group_check=True)
                        for b in range(2):
                            t0 = i * TILE + b * S
                            last = mm(ST[hh][:, pr * 128 + b * S:pr * 128 + (b + 1) * S],
                                      k_t[:, r, q, 2 * i + b, m:m + 2, :].rearrange("p m s -> p (m s)"), q_t[:, r, q, t0:t0 + S],
                                      start=False, stop=True, skip_group_check=True)
                    last.then_inc(st_done, 1)

            def attend(T, r, i, k):
                for hh in range(2):
                    pe.wait_ge(e_lo_done[hh], T + 1)
                if k >= 1:
                    pe.wait_ge(attn_done, T * 2)
                for b in range(2):
                    for q in range(QUADS):
                        o = AV[:, b * 256 + q * 4 * VW:b * 256 + (q + 1) * 4 * VW]
                        pr = (q % 2) * 2
                        for n, (e, v) in enumerate(((e_hi, v_hi), (e_lo, v_hi), (e_hi, v_lo), (e_lo, v_lo))):
                            last = mm(o, e[:, i, q // 2, b, pr:pr + 2, :].rearrange("p a b -> p (a b)"),
                                      v[:, r, 2 * i + b, 2 * q:2 * q + 2].rearrange("p a b c -> p (a b c)"),
                                      start=(n == 0), stop=(n == 3))
                last.then_inc(av_done, 1)

            def turn_attn(c, r, before_it):
                pe.wait_ge(attn_done, (c + 1) * 4)
                before_it()
                carry_waits(pe)
                for b in range(NB):
                    last = tr(M1[0:64, b * P:(b + 1) * P], attn[:, r, b].rearrange("p a b -> p (a b)"), ident[:, :])
                last.then_inc(attn_turned, 1)

            def proj_o(c, before_it):
                pe.wait_ge(attnT_ready, c + 1)
                before_it()
                for i in range(2):
                    for p in range(2):
                        last = mm(M0[:, i * P:(i + 1) * P], attnT[:, p, 2 * i:2 * i + 2, :].rearrange("p a b -> p (a b)"), woT[:, p, :],
                                  start=(p == 0), stop=(p == 1))
                last.then_inc(y_done, 1)

            def turn_n2(c, r, before_it):
                pe.wait_ge(n2_done, (c + 1) * 2)
                before_it()
                for i in range(2):
                    last = tr(M1[:, i * P:(i + 1) * P], rows[:, r, i, 0:D], ident[:, :])
                last.then_inc(n2_turned, 1)

            def route(c, before_it):
                pe.wait_ge(hT_ready, c + 1)
                before_it()
                for i in range(2):
                    last = mm(M2[:, i * EXPERTS:(i + 1) * EXPERTS], hT32[:, i * TILE:(i + 1) * TILE], rwT[:, :],
                              start=True, stop=True)
                last.then_inc(logits_done, 1)

            def count(c, k, before_it):
                pe.wait_ge(onehot_done, c + 1)
                if k >= 3:
                    pe.wait_ge(seen_done, c)
                before_it()
                mm(M2[:, 0:EXPERTS], before[:, :], onehot_b[:, 0, :], start=True, stop=False)
                mm(M2[:, 0:EXPERTS], ones_b[:, :], seen[:, :], start=False, stop=True)
                mm(M2[:, EXPERTS:2 * EXPERTS], before[:, :], onehot_b[:, 1, :], start=True, stop=False)
                mm(M2[:, EXPERTS:2 * EXPERTS], ones_b[:, :], onehot_b[:, 0, :], start=False, stop=False)
                mm(M2[:, EXPERTS:2 * EXPERTS], ones_b[:, :], seen[:, :], start=False, stop=True).then_inc(pos_done, 1)

            nothing = lambda: None
            pe.wait_ge(w_kept, 1)
            for c in range(2):
                if c == 1:
                    pe.wait_ge(qk_lo_done, 1)
                turn_xc(c, c, c)
                proj_q(c, c)
                proj_k(c, c, (lambda: pe.wait_ge(qk_lo_done, 2)) if c else nothing)
            pe.wait_ge(w_loaded, W_LOADS * 16)
            for p in range(2):
                last = mm(M2[:, 0:D], bv_col[:, p:p + 1].to_broadcast([64, P]), woT[:, p, :], start=(p == 0), stop=(p == 1))
            last.then_inc(bv_proj, 1)
            proj_v(0, 0, lambda: pe.wait_ge(qk_lo_done, 4))
            turn_xc(2, 0, 2)
            proj_q(2, 0)
            proj_k(2, 0, lambda: pe.wait_ge(v_lo_done, 2))
            pe.wait_ge(bo_ready, 1)
            scores_a(None, 0, 0, 80)
            turn_negmax(0, 0, nothing)

            def body(c, r, k):
                if has(k):
                    scores_st(c * 2, r, 0, k)
                    scores_a(c * 2 + 1, r, 1, None)
                if has(k - 1):
                    attend(c * 2 - 1, 1 - r, 1, k - 1 + 1)
                if has(k + 1):
                    proj_v(c + 1, 1 - r, lambda: pe.wait_ge(attnT_ready, c - 1) if has(k - 2)
                           else pe.wait_ge(qk_lo_done, (c + 3) * 2))
                if has(k + 3):
                    if k < 2:
                        pe.wait_ge(qk_lo_done, (c + 3) * 2 - 1)
                    turn_xc(c + 3, 1 - r, k + 3)
                if has(k):
                    turn_negmax(c * 2 + 1, 1, lambda: pe.wait_ge(dest_done, c - 2) if has(k - 3)
                                else pe.wait_ge(negmaxT_ready, c * 2 + 1))
                if has(k + 3):
                    proj_q(c + 3, 1 - r)
                if has(k - 2):
                    turn_n2(c - 2, r, lambda: pe.wait_ge(v_lo_done, (c + 2) * 2) if has(k + 1)
                            else pe.wait_ge(attnT_ready, c - 1))
                if has(k):
                    scores_st(c * 2 + 1, r, 1, k + 1)
                if has(k + 3):
                    proj_k(c + 3, 1 - r, lambda: pe.wait_ge(hT_ready, c - 1) if has(k - 2)
                           else pe.wait_ge(v_lo_done, (c + 2) * 2))
                if has(k - 2):
                    route(c - 2, lambda: pe.wait_ge(negmaxT_ready, c * 2 + 2) if has(k)
                          else pe.wait_ge(dest_done, c - 2))
                if has(k):
                    attend(c * 2, r, 0, k)
                if has(k + 1):
                    scores_a(c * 2 + 2, 1 - r, 0, twos(c, r, 1) * 5)
                if has(k - 1):
                    turn_attn(c - 1, 1 - r, lambda: pe.wait_ge(qk_lo_done, (c + 4) * 2) if has(k + 3)
                              else pe.wait_ge(hT_ready, c - 1) if has(k - 2)
                              else pe.wait_ge(v_lo_done, (c + 2) * 2))
                if has(k + 1):
                    turn_negmax(c * 2 + 2, 0, lambda: pe.wait_ge(shifted_done, c - 1) if has(k - 2)
                                else pe.wait_ge(negmaxT_ready, c * 2 + 2))
                if has(k - 1):
                    proj_o(c - 1, lambda: pe.wait_ge(qk_lo_done, (c + 4) * 2 - 1) if has(k + 3)
                           else pe.wait_ge(x2_done, c - 1))
                if has(k - 2):
                    count(c - 2, k, lambda: pe.wait_ge(negmaxT_ready, c * 2 + 3) if has(k + 1)
                          else pe.wait_ge(shifted_done, c - 1))

            chunks(pe, body)

            pe.wait_ge(seen_done, NCH)
            pe.wait_ge(dest_done, NCH)
            mm(M2[:, 0:EXPERTS], ones_b[:, :], seen[:, :], start=True, stop=True).then_inc(counts_done, 1)

            pe.wait_ge(signs, 1)
            pe.wait_ge(max_done, NT * 2)
            pe.wait_ge(e32_done, NT * 2)
            pe.wait_ge(attn_done, NT * 2)
            places = [A[0], A[1], ST[0], ST[1], AV]
            for n in range(4 * BLOCKS):
                e, c = (n % (2 * BLOCKS)) // 2, n % 2
                src = sign1[:, e, c, :] if n < 2 * BLOCKS else sign2[:, e, c * P:(c + 1) * P]
                last = tr(places[n // 8][:, :].bitcast(F16)[:, (n % 8) * P:(n % 8 + 1) * P], src, identh[:, :])
                if n % 8 == 7 or n == 4 * BLOCKS - 1:
                    last.then_inc(t_turned, 1)
            pe.wait_ge(t_kept, 3)
            for e in range(BLOCKS):
                last = mm(places[e // 4][:, (e % 4) * D:(e % 4 + 1) * D], s2[:, e:e + 1].to_broadcast([P, P]), ident[:, :],
                          start=True, stop=True, skip_group_check=True)
            last.then_inc(t_turned, 1)
            pe.wait_ge(t_kept, 6)

            def experts_of(u):
                return [pe.value_load(tab[0:1, 1, bass.ds(u * 2 + i, 1)], min_val=0, max_val=EXPERTS - 1) for i in range(2)]

            def turn_h(u, m, k):
                r = m % 2
                pe.wait_ge(rows_loaded[m % 2], twos(u, m % 2, 0) * 2)
                if k >= 2:
                    pe.wait_ge(h32_done, u - 1)
                for i in range(2):
                    last = tr(XT[r][:, i * TILE:(i + 1) * TILE], in_rows[:, m, i, 0:D], ident[:, :])
                last.then_inc(h_turned, 1)

            def layer1(u, r, k, experts):
                pe.wait_ge(h_done, u + 1)
                if k >= 2:
                    pe.wait_ge(g32_done, u * 2 - 2)
                for c in range(2):
                    for n, h in enumerate((h_hi, h_lo)):
                        last = mm(F1[r][0][:, c * CH:(c + 1) * CH], t1[:, 0, c, :], h[:, r, :], start=(n == 0), stop=(n == 1))
                last.then_inc(f1_done, 1)
                for i, e in enumerate(experts):
                    for c in range(2):
                        for n, h in enumerate((h_hi, h_lo)):
                            last = mm(F1[r][1][:, c * CH + i * TILE:c * CH + (i + 1) * TILE],
                                      t1[:, bass.ds(e + 1, 1), c, :].rearrange("p a b -> p (a b)"),
                                      h[:, r, i * TILE:(i + 1) * TILE], start=(n == 0), stop=(n == 1))
                last.then_inc(f1_done, 1)

            def layer2(u, r, k, experts):
                if k >= 2:
                    pe.wait_ge(parts_done, u - 1)
                for w in range(2):
                    pe.wait_ge(g_done, u * 2 + 1 + w)
                    for i, e in enumerate(experts):
                        o = YY[r][:, (2 * w + i) * D:(2 * w + i + 1) * D]
                        for n in range(4):
                            c, g = n // 2, (g_hi, g_lo)[n % 2]
                            wt = t2[:, 0, c, :] if w == 0 else t2[:, bass.ds(e + 1, 1), c, :].rearrange("p a b -> p (a b)")
                            last = mm(o, g[:, r, w, c, i * TILE:(i + 1) * TILE], wt, start=(n == 0), stop=(n == 3))
                last.then_inc(f2_done, 1)

            def body(u, m, k):
                r = m % 2
                if k + 1 < STEPS:
                    turn_h(u + 1, (m + 1) % ROWBUFS, k + 1)
                if k in (4, STEPS - 4):
                    loaded[1 - r] = experts_of(u - 1)
                loaded[r] = experts_of(u)
                layer1(u, r, k, loaded[r])
                if k >= 1:
                    layer2(u - 1, 1 - r, k - 1, loaded[1 - r])

            loaded = [None, None]
            pe.wait_ge(tab_done, 1)
            turn_h(0, 0, 0)
            steps(pe, body)
            layer2(STEPS - 1, 1, STEPS - 1, loaded[1])

        @block.scalar
        def _(act):
            fn = nc.scalar.activation

            act.wait_ge(w_turned, 1)
            for i in range(2):
                fn(wT[:, i, :].rearrange("p (m d q) -> p m d q", m=4, d=HD),
                   A[0][:, i * P:(i + 1) * P].rearrange("p (q m d) -> p m d q", q=QUADS, m=4), ACT.Copy)
            fn(wT[:, 2, :].rearrange("p (hp q pp d) -> p hp q pp d", hp=2, q=QUADS, pp=2)[:, 0],
               A[0][:, 2 * P:3 * P].rearrange("p (q pp hp d) -> p hp q pp d", q=QUADS, pp=2, hp=2)[:, 0], ACT.Copy)
            fn(wT[:, 2, :].rearrange("p (hp q pp d) -> p hp q pp d", hp=2, q=QUADS, pp=2)[:, 1],
               A[0][:, 2 * P:3 * P].rearrange("p (q pp hp d) -> p hp q pp d", q=QUADS, pp=2, hp=2)[:, 1], ACT.Copy)
            fn(rwT[:, :], A[0][:, 3 * P:3 * P + EXPERTS], ACT.Copy)
            fn(woT[:, :, :], A[1][0:64, 0:2 * P].rearrange("p (a b) -> p a b", a=2), ACT.Copy).then_inc(w_kept, 1)

            def normalise(c, r, k):
                act.wait_ge(rstd_done, (c + 1) * 2)
                if k >= 2:
                    act.wait_ge(xc_turned, c - 1)
                for i in range(2):
                    last = fn(xn[:, r, i, :], x_in[:, r, i, :], ACT.Identity, bias=nmr[:, r, i:i + 1], scale=rstd[:, r, i:i + 1])
                last.then_inc(xn_ready, 1)

            def keep_xcT(c, r, k):
                act.wait_ge(xc_turned, c + 1)
                if k >= 2:
                    act.wait_ge(v_proj, c - 1)
                fn(xcT[:, r], M0[:, 0:512].rearrange("p (a b) -> p a b", a=4), ACT.Copy).then_inc(xcT_ready, 1)

            def q_hi(c, r, k):
                act.wait_ge(q_proj, c + 1)
                if k == 0:
                    act.wait_ge(b_qk_loaded, 8 * 16)
                if k >= 2:
                    act.wait_ge(terms_stored[r], twos(c, r, -2) * 8)
                fn(qk_hl[:, r, 0, 0, :], M0[:, 0:CH], ACT.Identity, bias=b_col[:, 0:1]).then_inc(qk_hi_done, 1)

            def k_hi(c, r):
                act.wait_ge(k_proj, c + 1)
                fn(qk_hl[:, r, 1, 0, :], M1[:, 0:CH], ACT.Identity, bias=b_col[:, 1:2]).then_inc(qk_hi_done, 1)

            def keep_v_hi(c, r, k):
                act.wait_ge(v_proj, c + 1)
                if k >= 2:
                    act.wait_ge(av_done, (c - 1) * 2)
                for hp in range(2):
                    fn(v_part(v_hi, r, hp), v_sums(hp), ACT.Copy).then_inc(v_hi_done, 1)

            def keep_negmaxT(T, i, k):
                act.wait_ge(negmax_turned, T + 1)
                if k >= 1:
                    act.wait_ge(st_done, (T - 1) * 2)
                fn(negmaxT[:, i, :], M2[:, :].bitcast(BF16)[:, 0:P], ACT.Copy).then_inc(negmaxT_ready, 1)

            def exponentials(T, i, k, hh):
                act.wait_ge(st_done, T * 2 + 1 + hh)
                if k >= 2:
                    act.wait_ge(av_done, T - 1)
                src = ST[hh][:, :].rearrange("p (a b c) -> p a b c", a=4, b=2)
                fn(e_hi[:, i, hh].rearrange("p b a c -> p a b c"), src, ACT.Exp, bias=lne_col, scale=SCALE).then_inc(e_hi_done, 1)
                if k >= 1:
                    act.wait_ge(e_lo_done[hh], T)
                fn(e32[:, hh].rearrange("p b a c -> p a b c"), src, ACT.Exp, bias=lne_col, scale=SCALE).then_inc(e32_done, 1)

            def keep_attnT(c):
                act.wait_ge(attn_turned, c + 1)
                fn(attnT[:].rearrange("p a b c -> p b a c"), M1[0:64, :].rearrange("p (b a c) -> p b a c", b=NB, a=2), ACT.Copy).then_inc(attnT_ready, 1)

            def keep_hT(c):
                act.wait_ge(n2_turned, c + 1)
                fn(hT32[:, :], M1[:, 0:CH], ACT.Identity, bias=ln_col[:, 1:2], scale=ln_col[:, 0:1]).then_inc(hT_ready, 1)

            def normalise2(c, r):
                act.wait_ge(rstd2_done, (c + 1) * 2)
                for i in range(2):
                    fn(rows[:, r, i, 0:D], rows[:, r, i, D:2 * D], ACT.Identity, bias=nmr2[:, i:i + 1],
                       scale=rstd2[:, i:i + 1]).then_inc(n2_done, 1)

            lne_col = lne[:, 0:1]
            act.wait_ge(vconsts, 2)
            for c in range(2):
                normalise(c, c, c)
            for c in range(2):
                keep_xcT(c, c, c)
                q_hi(c, c, c)
                k_hi(c, c)
            keep_v_hi(0, 0, 0)
            normalise(2, 0, 2)
            keep_xcT(2, 0, 2)
            q_hi(2, 0, 2)
            k_hi(2, 0)
            keep_negmaxT(0, 0, 0)
            act.wait_ge(w_loaded, W_LOADS * 16)
            normalise(3, 1, 3)

            def body(c, r, k):
                if has(k):
                    exponentials(c * 2, 0, 2 * k, 0)
                    exponentials(c * 2, 0, 2 * k, 1)
                if has(k - 2):
                    normalise2(c - 2, r)
                if has(k + 1):
                    keep_v_hi(c + 1, 1 - r, k + 1)
                if has(k + 3):
                    keep_xcT(c + 3, 1 - r, k + 3)
                if has(k):
                    keep_negmaxT(c * 2 + 1, 1, k)
                if has(k + 3):
                    q_hi(c + 3, 1 - r, k + 3)
                if has(k - 2):
                    keep_hT(c - 2)
                if has(k):
                    exponentials(c * 2 + 1, 1, 2 * k + 1, 0)
                if has(k + 3):
                    k_hi(c + 3, 1 - r)
                if has(k):
                    exponentials(c * 2 + 1, 1, 2 * k + 1, 1)
                if has(k - 1):
                    keep_attnT(c - 1)
                if has(k - 2):
                    act.wait_ge(shifted_done, c - 1)
                    fn(expo[:], shifted[:], ACT.Exp).then_inc(expo_done, 1)
                if has(k + 1):
                    keep_negmaxT(c * 2 + 2, 0, k + 1)
                if has(k + 4):
                    normalise(c + 4, r, k + 4)

            chunks(act, body)

            flat = [t1[:].rearrange("p e c f -> p (e c) f"), t2[:].rearrange("p e c f -> p (e c) f")]
            places = [A[0], A[1], ST[0], ST[1], AV]
            for g in range(5):
                act.wait_ge(t_turned, g + 1)
                src = places[g][:, :].bitcast(F16).rearrange("p (a b) -> p a b", a=8)
                lo, hi = 8 * g, min(8 * g + 8, 4 * BLOCKS)
                edge = min(max(2 * BLOCKS, lo), hi)
                last = None
                for t, (a, b) in enumerate(((lo, edge), (edge, hi))):
                    if b > a:
                        last = fn(flat[t][:, a - t * 2 * BLOCKS:b - t * 2 * BLOCKS, :], src[:, a - lo:b - lo, :], ACT.Copy)
                last.then_inc(t_kept, 1)
            act.wait_ge(t_turned, 6)
            for g in range(3):
                a, b = 4 * g, min(4 * g + 4, BLOCKS)
                last = fn(s2_row[:, a:b, :], places[g][:, 0:(b - a) * D].rearrange("p (a b) -> p a b", b=D), ACT.Copy)
            last.then_inc(t_kept, 1)

            def keep_h(u, r, k):
                act.wait_ge(h_turned, u + 1)
                if k >= 2:
                    act.wait_ge(h_done, u - 1)
                fn(h32[:, r, :], XT[r][:, 0:CH], ACT.Identity, bias=ln_col[:, 1:2], scale=ln_col[:, 0:1]).then_inc(h32_done, 1)

            def silus(u, r, k, experts):
                act.wait_ge(f1_done, u * 2 + 1)
                if k >= 2:
                    act.wait_ge(g_done, u * 2 - 2)
                for c in range(2):
                    last = fn(g32[:, r, 0, c, :], F1[r][0][:, c * CH:(c + 1) * CH], ACT.Silu, scale=s1[:, c:c + 1])
                last.then_inc(g32_done, 1)
                act.wait_ge(f1_done, u * 2 + 2)
                if k >= 2:
                    act.wait_ge(f2_done, u - 1)
                for to in (g_hi, g32):
                    for i, e in enumerate(experts):
                        for c in range(2):
                            last = fn(to[:, r, 1, c, i * TILE:(i + 1) * TILE], F1[r][1][:, c * CH + i * TILE:c * CH + (i + 1) * TILE],
                                      ACT.Silu, scale=s1[:, bass.ds(e * 2 + (2 + c), 1)])
                last.then_inc(g32_done, 1)

            def body(u, m, k):
                r = m % 2
                experts = [act.value_load(tab[0:1, 1, bass.ds(u * 2 + i, 1)], min_val=0, max_val=EXPERTS - 1) for i in range(2)]
                if k + 1 < STEPS:
                    keep_h(u + 1, 1 - r, k + 1)
                silus(u, r, k, experts)

            act.wait_ge(tab_done, 1)
            keep_h(0, 0, 0)
            steps(act, body)

        @block.vector
        def _(dve):
            n = [0]
            v = nc.vector

            def then(ins):
                n[0] += 1
                ins.then_inc(chain, 1)
                dve.wait_ge(chain, n[0])

            v.memset(zeros[:, :], 0.0).then_inc(vconsts, 1)
            v.memset(lne[:, :], LNE)
            v.memset(rows[:, :, :, 2 * D:ROW], 0.0)
            v.memset(seen[:, :], 0.0)
            v.memset(negmax[:], 0.0)
            then(v.memset(v_hi[:], 0.0))
            v.memset(v_lo[:], 0.0)
            for hp in range(2):
                for r in range(2):
                    v.memset(v_part(v_hi, r, hp, HD, VW), 1.0)
            then(v.memset(s1h[:, :], 0.0))
            v.engine_nop().then_inc(vconsts, 1)

            def x_moments(c, r, k):
                dve.wait_ge(xc_loaded[r], twos(c, r, 0) * 2)
                for i in range(2):
                    v.bn_stats(stats[:, i, :], x_in[:, r, i, :]).then_inc(st_chain, 1)

            def x_aggregate(c, r, k):
                if k >= 2:
                    dve.wait_ge(rstd_done, (c - 1) * 2)
                for i in range(2):
                    dve.wait_ge(st_chain, c * 4 + 1 + i)
                    carry_waits(dve)
                    v.bn_aggr(mv[:, r, i, :], stats[:, i, :]).then_inc(st_chain, 1)

            def x_eps(c, r):
                dve.wait_ge(st_chain, c * 4 + 4)
                v.tensor_scalar(negmean[:, r], mv[:, r, :, 0], -1.0, None, ALU.mult)
                v.tensor_scalar(veps[:, r], mv[:, r, :, 1], LN_EPS, None, ALU.add).then_inc(stats_done, 1)

            def x_stats(c, r, k):
                x_moments(c, r, k)
                x_aggregate(c, r, k)
                x_eps(c, r)

            def q_lo(c, r):
                dve.wait_ge(qk_hi_done, c * 2 + 1)
                v.scalar_tensor_tensor(qk_hl[:, r, 0, 1, :], M0[:, 0:CH], b_col[:, 0:1], qk_hl[:, r, 0, 0, :],
                                       ALU.add, ALU.subtract).then_inc(qk_lo_done, 1)

            def k_lo(c, r):
                dve.wait_ge(qk_hi_done, c * 2 + 2)
                v.scalar_tensor_tensor(qk_hl[:, r, 1, 1, :], M1[:, 0:CH], b_col[:, 1:2], qk_hl[:, r, 1, 0, :],
                                       ALU.add, ALU.subtract).then_inc(qk_lo_done, 1)

            def v_low(c, r, hp):
                dve.wait_ge(v_hi_done, c * 2 + 1 + hp)
                v.tensor_tensor(v_part(v_lo, r, hp), v_sums(hp), v_part(v_hi, r, hp), ALU.subtract).then_inc(v_lo_done, 1)

            def maxima(T, i, k, hh):
                dve.wait_ge(a_done, T * 2 + 1 + hh)
                if k >= 1:
                    dve.wait_ge(negmax_turned, T - 1)
                v.tensor_reduce(negmax[:, i, 8 * hh:8 * hh + 8], A[hh][:, :].rearrange("p (a b) -> p a b", b=S),
                                X, ALU.max, negate=True).then_inc(max_done, 1)

            def e_low(T, i, k):
                dve.wait_ge(e32_done, T * 2 + 1)
                if k >= 2:
                    dve.wait_ge(av_done, T - 1)
                hi, lo = (t[:, i, 0].rearrange("p a b c -> p (a b c)") for t in (e_hi, e_lo))
                v.tensor_tensor(lo, e32[:, 0].rearrange("p a b c -> p (a b c)"), hi, ALU.subtract).then_inc(e_lo_done[0], 1)

            av = AV[:, :].rearrange("p (b x) -> p b x", b=2)[:, :, 0:16 * VW].rearrange("p b (h pp d) -> p b h pp d", pp=2, d=VW)

            def denominators(T):
                dve.wait_ge(av_done, T + 1)
                for pp in range(2):
                    ps = slice(64 * pp, 64 * pp + 64)
                    v.reciprocal(rden[ps], av[ps, :, :, pp, HD]).then_inc(rden_done, 1)

            def divide(T, r, i):
                for pp in range(2):
                    ps = slice(64 * pp, 64 * pp + 64)
                    dve.wait_ge(rden_done, T * 2 + 1 + pp)
                    v.tensor_tensor(attn[ps, r, 2 * i:2 * i + 2], av[ps, :, :, pp, 0:HD],
                                    rden[ps].unsqueeze(3).to_broadcast([64, 2, 8, HD]), ALU.mult).then_inc(attn_done, 1)

            def residual(c, r, k):
                dve.wait_ge(y_done, c + 1)
                dve.wait_ge(res_ready, c + 1)
                if k >= 2:
                    dve.wait_ge(scattered[r], twos(c, r, -2) * 2)
                v.tensor_tensor(rows[:, r, :, D:2 * D], M0[:, 0:CH].rearrange("p (a b) -> p a b", a=2), x_res[:, r],
                                ALU.add).then_inc(x2_done, 1)

            def moments2(c, r):
                dve.wait_ge(x2_done, c + 1)
                for i in range(2):
                    v.bn_stats(stats2[:, i, :], rows[:, r, i, D:2 * D]).then_inc(st2_chain, 1)

            def aggregate2(c, k):
                if k >= 1:
                    dve.wait_ge(rstd2_done, c * 2)
                for i in range(2):
                    dve.wait_ge(st2_chain, c * 4 + 1 + i)
                    carry_waits(dve)
                    v.bn_aggr(mv2[:, i, :], stats2[:, i, :]).then_inc(st2_chain, 1)

            def variance2(c):
                dve.wait_ge(st2_chain, c * 4 + 4)
                v.tensor_scalar(negmean2[:, :], mv2[:, :, 0], -1.0, None, ALU.mult)
                v.tensor_scalar(w2var[:, :], mv2[:, :, 1], 1.0 + LN_EPS, LN_EPS * LN_EPS, ALU.mult, ALU.add).then_inc(stats2_done, 1)

            lg = M2[:, 0:2 * EXPERTS].rearrange("p (a b) -> p a b", a=2)
            wide = lambda a: a.unsqueeze(2).to_broadcast([P, 2, EXPERTS])

            def pick_top(c):
                dve.wait_ge(logits_done, c + 1)
                v.tensor_reduce(top[:, :], lg, X, ALU.max).then_inc(pick_chain, 1)

            def pick_shift(c, k):
                dve.wait_ge(pick_chain, c * 4 + 1)
                if k >= 1:
                    dve.wait_ge(expo_done, c)
                v.tensor_tensor(shifted[:], lg, wide(top[:, :]), ALU.subtract).then_inc(shifted_done, 1)

            def pick_rank(c):
                dve.wait_ge(shifted_done, c + 1)
                v.scalar_tensor_tensor(is_top[:], shifted[:], 0.0, rank8[:, :].unsqueeze(1).to_broadcast([P, 2, EXPERTS]),
                                       ALU.is_equal, ALU.mult).then_inc(pick_chain, 1)

            def pick_first(c):
                dve.wait_ge(pick_chain, c * 4 + 2)
                v.tensor_reduce(first[:, :], is_top[:], X, ALU.max).then_inc(pick_chain, 1)

            def pick_onehot(c):
                dve.wait_ge(pick_chain, c * 4 + 3)
                v.tensor_tensor(onehot[:], is_top[:], wide(first[:, :]), ALU.is_equal).then_inc(pick_chain, 1)

            def keep_onehot(c):
                dve.wait_ge(pick_chain, c * 4 + 4)
                v.tensor_copy(onehot_b[:], onehot[:]).then_inc(onehot_done, 1)


            def gate_sum(c):
                dve.wait_ge(expo_done, c + 1)
                if not isinstance(c, int) or c > 0:
                    dve.wait_ge(gate_chain, c * 2)
                v.tensor_reduce(expsum[:, :], expo[:], X, ALU.add).then_inc(gate_chain, 1)

            def gate_and_token(c, r):
                dve.wait_ge(gate_chain, c * 2 + 1)
                v.reciprocal(rows[:, r, :, GATE], expsum[:, :])
                v.tensor_copy(rows[:, r, :, TOKEN], token_no[:, :]).then_inc(row_done, 1)

            def next_tokens(c):
                dve.wait_ge(row_done, c + 1)
                v.tensor_scalar(token_no[:, :], token_no[:, :], float(CH), None, ALU.add).then_inc(gate_chain, 1)


            def place_base(c):
                dve.wait_ge(pos_done, c + 1)
                v.tensor_tensor(pos8[:], M2[:, 0:2 * EXPERTS].rearrange("p (a b) -> p a b", a=2),
                                region8[:, :].unsqueeze(1).to_broadcast([P, 2, EXPERTS]), ALU.add).then_inc(place_chain, 1)

            def place_pick(c):
                dve.wait_ge(place_chain, c * 3 + 1)
                v.tensor_tensor(pos8m[:], pos8[:], onehot[:], ALU.mult).then_inc(place_chain, 1)
                v.tensor_tensor(seen2[:, :], seen[:, :], onehot_b[:, 0, :], ALU.add).then_inc(place_chain, 1)

            def place_rows(c, r):
                dve.wait_ge(place_chain, c * 3 + 2)
                with nc.allow_low_precision(reason="whole numbers below 2 ** 24"):
                    v.tensor_reduce(dest[:, r, :], pos8m[:], X, ALU.add).then_inc(dest_done, 1)
                dve.wait_ge(place_chain, c * 3 + 3)
                v.tensor_tensor(seen[:, :], seen2[:, :], onehot_b[:, 1, :], ALU.add).then_inc(seen_done, 1)

            def quantise(e):
                dve.wait_ge(ffn_w_loaded[(e + 3) // 4], 2 * 16)
                w1, c1, c2 = w1_in[:, e], slice(2 * e, 2 * e + 2), slice(e, e + 1)
                v.tensor_reduce(s1[:, c1], w1, X, ALU.add, apply_absolute_value=True)
                then(v.tensor_reduce(s2[:, c2], w2_in[:, e, :], X, ALU.add, apply_absolute_value=True))
                v.tensor_scalar(s1[:, c1], s1[:, c1], 1.0 / D, 1e-5, ALU.mult, ALU.max)
                then(v.tensor_scalar(s2[:, c2], s2[:, c2], 1.0 / FE, 1e-5, ALU.mult, ALU.max))
                v.tensor_scalar(s1h[:, c1], s1[:, c1], 0.5, None, ALU.mult)
                v.tensor_scalar(s1n[:, c1], s1[:, c1], -0.5, None, ALU.mult)
                v.tensor_scalar(s2h[:, c2], s2[:, c2], 0.5, None, ALU.mult)
                then(v.tensor_scalar(s2n[:, c2], s2[:, c2], -0.5, None, ALU.mult))
                for c in range(2):
                    v.tensor_scalar(low1[:, c, :], w1[:, c, :], s1n[:, 2 * e + c:2 * e + c + 1], None, ALU.is_lt)
                then(v.tensor_scalar(low2[:, :], w2_in[:, e, :], s2n[:, c2], None, ALU.is_lt))
                for c in range(2):
                    v.scalar_tensor_tensor(sign1[:, e, c, :], w1[:, c, :], s1h[:, 2 * e + c:2 * e + c + 1], low1[:, c, :],
                                           ALU.is_gt, ALU.subtract)
                then(v.scalar_tensor_tensor(sign2[:, e, :], w2_in[:, e, :], s2h[:, c2], low2[:, :], ALU.is_gt, ALU.subtract))

            for c in range(2):
                x_stats(c, c, c)
            quantise(0)
            q_lo(0, 0)
            k_lo(0, 0)
            x_stats(2, 0, 2)
            quantise(1)
            q_lo(1, 1)
            k_lo(1, 1)
            x_stats(3, 1, 3)
            quantise(2)
            dve.wait_ge(bv_proj, 1)
            dve.wait_ge(w_loaded, W_LOADS * 16)
            v.tensor_tensor(b_row[:, :], M2[:, 0:D], bo_row[:, :], ALU.add).then_inc(bo_ready, 1)
            for half in range(2):
                v_low(0, 0, half)
            q_lo(2, 0)
            k_lo(2, 0)
            quantise(3)
            for half in range(2):
                maxima(0, 0, 0, half)

            quantised = {k: n + 4 for n, k in enumerate((12, 13, 14))}
            quantised_in_wait = {NCH: BLOCKS - 2, NCH + 1: BLOCKS - 1}

            def body(c, r, k):
                if has(k + 4):
                    x_moments(c + 4, r, k + 4)
                if has(k):
                    maxima(c * 2 + 1, 1, k, 0)
                    maxima(c * 2 + 1, 1, k, 1)
                if has(k + 4):
                    x_aggregate(c + 4, r, k + 4)
                if has(k + 1):
                    v_low(c + 1, 1 - r, 0)
                    v_low(c + 1, 1 - r, 1)
                if has(k + 4):
                    x_eps(c + 4, r)
                if has(k):
                    e_low(c * 2, 0, 2 * k)
                if has(k - 1):
                    denominators(c * 2 - 1)
                    if k - 1 >= 2:
                        dve.wait_ge(attn_turned, c - 2)
                    divide(c * 2 - 1, 1 - r, 1)
                if has(k + 3):
                    q_lo(c + 3, 1 - r)
                if has(k - 2):
                    if k in quantised_in_wait:
                        quantise(quantised_in_wait[k])
                    pick_top(c - 2)
                    pick_shift(c - 2, k - 2)
                    pick_rank(c - 2)
                if has(k + 3):
                    k_lo(c + 3, 1 - r)
                if has(k - 2):
                    pick_first(c - 2)
                if has(k + 1):
                    maxima(c * 2 + 2, 0, k + 1, 0)
                if has(k - 2):
                    pick_onehot(c - 2)
                if has(k + 1):
                    maxima(c * 2 + 2, 0, k + 1, 1)
                if has(k):
                    e_low(c * 2 + 1, 1, 2 * k + 1)
                if k in quantised:
                    quantise(quantised[k])
                if has(k - 2):
                    gate_sum(c - 2)
                    keep_onehot(c - 2)
                if has(k - 1):
                    residual(c - 1, 1 - r, k - 1)
                    moments2(c - 1, 1 - r)
                if has(k):
                    denominators(c * 2)
                if has(k - 1):
                    aggregate2(c - 1, k - 1)
                if has(k):
                    if k >= 2:
                        dve.wait_ge(attn_turned, c - 1)
                    divide(c * 2, r, 0)
                if has(k - 1):
                    variance2(c - 1)
                if has(k - 2):
                    gate_and_token(c - 2, r)
                    place_base(c - 2)
                    next_tokens(c - 2)
                    place_pick(c - 2)
                    place_rows(c - 2, r)

            chunks(dve, body)
            v.engine_nop().then_inc(signs, 1)

            row8 = lambda a: a.unsqueeze(1).to_broadcast([P, SLOTS, EXPERTS])
            col8 = lambda a: a.unsqueeze(2).to_broadcast([P, SLOTS, EXPERTS])
            dve.wait_ge(counts_done, 1)
            then(v.tensor_copy(cnt[:, :], M2[:, 0:EXPERTS]))
            then(v.tensor_tensor(over[:], cnt[:, :].unsqueeze(2).to_broadcast([P, EXPERTS, NT]), thr[:], ALU.is_gt))
            then(v.tensor_reduce(tiles8[:, :], over[:], X, ALU.add))
            then(v.tensor_tensor(prod8[:], tiles8[:, :].unsqueeze(1).to_broadcast([P, EXPERTS, EXPERTS]), tri8[:], ALU.mult))
            v.tensor_tensor(next8[:, 0:EXPERTS - 1], cnt[:, 1:EXPERTS], cnt[:, 0:EXPERTS - 1], ALU.subtract)
            v.tensor_scalar(next8[:, EXPERTS - 1:EXPERTS], cnt[:, EXPERTS - 1:EXPERTS], -1.0, None, ALU.mult)
            then(v.tensor_reduce(upto8[:, :], prod8[:], X, ALU.add))
            then(v.tensor_tensor(sl_ge[:], col8(slot_no[:, :]), row8(upto8[:, :]), ALU.is_ge))
            v.tensor_reduce(sl_e[:, :], sl_ge[:], X, ALU.add)
            v.tensor_tensor(sl_m[:], sl_ge[:], row8(tiles8[:, :]), ALU.mult)
            then(v.tensor_tensor(sl_m2[:], sl_ge[:], row8(next8[:, :]), ALU.mult))
            v.tensor_reduce(sl_start[:, :], sl_m[:], X, ALU.add)
            then(v.tensor_reduce(sl_n0[:, :], sl_m2[:], X, ALU.add))
            then(v.tensor_scalar(sl_n[:, :], sl_n0[:, :], cnt[:, 0:1], None, ALU.add))
            v.tensor_scalar(sl_last[:, :], sl_n[:, :], -float(TILE), 0.0, ALU.add, ALU.max)
            then(v.tensor_tensor(sl_j[:, :], slot_no[:, :], sl_start[:, :], ALU.subtract))
            then(v.tensor_scalar(sl_j[:, :], sl_j[:, :], float(TILE), None, ALU.mult))
            then(v.tensor_tensor(sl_off[:, :], sl_j[:, :], sl_last[:, :], ALU.min))
            v.tensor_scalar(sl_ec[:, :], sl_e[:, :], float(EXPERTS - 1), None, ALU.min)
            then(v.tensor_scalar(sl_row[:, :], sl_off[:, :], part_no[:, 0:1], None, ALU.add))
            v.tensor_tensor(sl_v1[:, :], sl_row[:, :], sl_j[:, :], ALU.is_ge)
            then(v.tensor_tensor(sl_v2[:, :], sl_row[:, :], sl_n[:, :], ALU.is_lt))
            then(v.tensor_tensor(valid[:, :], sl_v1[:, :], sl_v2[:, :], ALU.mult))
            then(v.scalar_tensor_tensor(sl_base[:, :], sl_ec[:, :], float(TOKENS), sl_off[:, :], ALU.mult, ALU.add))
            then(v.tensor_copy(tab[0:1, 0, :], sl_base[0:1, :]))
            v.tensor_copy(tab[0:1, 1, :], sl_ec[0:1, :]).then_inc(tab_done, 1)

            def split_h(u, r, k):
                dve.wait_ge(h32_done, u + 1)
                if k >= 2:
                    dve.wait_ge(f1_done, u * 2 - 2)
                v.tensor_copy(h_hi[:, r, :], h32[:, r, :]).then_inc(h_chain, 1)
                dve.wait_ge(h_chain, u + 1)
                v.tensor_tensor(h_lo[:, r, :], h32[:, r, :], h_hi[:, r, :], ALU.subtract).then_inc(h_done, 1)

            def split_g(u, r, k):
                if k >= 2:
                    dve.wait_ge(f2_done, u - 1)
                for w in range(2):
                    src, hi, lo = (t[:, r, w].rearrange("p b c -> p (b c)") for t in (g32, g_hi, g_lo))
                    dve.wait_ge(g32_done, u * 2 + 1 + w)
                    if w == 0:
                        v.tensor_copy(hi, src).then_inc(g_chain, 1)
                        dve.wait_ge(g_chain, u + 1)
                    v.tensor_tensor(lo, src, hi, ALU.subtract).then_inc(g_done, 1)

            def scale_sums(u, m, k, experts):
                r = m % 2
                dve.wait_ge(f2_done, u + 1)
                dve.wait_ge(rows_loaded[m % 2], twos(u, m % 2, 0) * 2)
                if k >= 1:
                    dve.wait_ge(parts_done, u)
                if k >= 2:
                    dve.wait_ge(sum_done, u - 1)
                    dve.wait_ge(out_stored[r], twos(u, r, -2) * 2)
                v.scalar_tensor_tensor(o_idx_f[:, :], in_rows[:, m, :, TOKEN], -NOWHERE, valid[:, bass.ds(u * 2, 2)],
                                       ALU.add, ALU.mult).then_inc(o_chain, 1)
                v.tensor_tensor(sh_out[:, r], YY[r][:, 0:2 * D].rearrange("p (a b) -> p a b", a=2),
                                s2_row[:, 0, :].unsqueeze(1).to_broadcast([P, 2, D]), ALU.mult)
                for i, e in enumerate(experts):
                    v.scalar_tensor_tensor(ex_out[:, r, i, :], YY[r][:, (2 + i) * D:(3 + i) * D], in_rows[:, m, i, GATE:GATE + 1],
                                           s2_row[:, bass.ds(e + 1, 1), :].rearrange("p a b -> p (a b)"), ALU.mult, ALU.mult)
                dve.wait_ge(o_chain, u + 1)
                v.tensor_scalar(o_idx[:, r, :], o_idx_f[:, :], NOWHERE, None, ALU.add).then_inc(parts_done, 1)

            def experts_of(u):
                return [dve.value_load(tab[0:1, 1, bass.ds(u * 2 + i, 1)], min_val=0, max_val=EXPERTS - 1) for i in range(2)]

            def body(u, m, k):
                r = m % 2
                if k + 1 < STEPS:
                    split_h(u + 1, 1 - r, k + 1)
                split_g(u, r, k)
                if k >= 1:
                    scale_sums(u - 1, (m + ROWBUFS - 1) % ROWBUFS, k - 1, experts_of(u - 1))

            dve.wait_ge(t_kept, 6)
            dve.wait_ge(tab_done, 1)
            split_h(0, 0, 0)
            steps(dve, body)
            scale_sums(STEPS - 1, (STEPS - 1) % ROWBUFS, STEPS - 1, experts_of(STEPS - 1))


_INS = ["x", "ctx_1024", "L0_xattn_Wq", "L0_xattn_bq", "L0_xattn_Wk", "L0_xattn_bk", "L0_xattn_Wv", "L0_xattn_bv",
        "L0_xattn_Wo", "L0_xattn_bo", "L0_ffn_shared_w1", "L0_ffn_shared_w2", "L0_ffn_expert_w1", "L0_ffn_expert_w2",
        "L0_ffn_router_w", "L0_ffn_ln_gamma", "L0_ffn_ln_beta"]


def kernel(**inputs):
    import numpy as np
    import concourse.bacc as bacc
    from concourse.bass_utils import run_bass_kernel_spmd

    nc = bacc.Bacc("TRN2", target_bir_lowering=False, num_devices=1)
    arrays, args = {}, []
    for name in _INS:
        a = np.ascontiguousarray(inputs[name])
        if name in ("x", "ctx_1024"):
            shape = a.shape
            a = a.reshape(-1, shape[-1])
        arrays["in_" + name] = a
        args.append(nc.dram_tensor("in_" + name, a.shape, mybir.dt.from_np(a.dtype), kind="ExternalInput").ap())
    args.append(nc.dram_tensor("out", arrays["in_x"].shape, F32, kind="ExternalOutput").ap())
    block_program(nc, *args)
    r = run_bass_kernel_spmd(nc, [arrays], core_ids=[0])
    return r.results[0]["out"].reshape(shape)
```
